# Optimizing a Trainium2 kernel written in Bass

```python
import numpy as np
import jax
import jax.numpy as jnp

def _softmax(x, axis=-1):
    return jax.nn.softmax(x, axis=axis)

def _gelu(x):
    return jax.nn.gelu(x, approximate=True)

def _silu(x):
    return jax.nn.silu(x)

def _sigmoid(x):
    return jax.nn.sigmoid(x)

def _layernorm(x, axis=-1, eps=1e-05):
    m = jnp.mean(x, axis=axis, keepdims=True)
    v = jnp.var(x, axis=axis, keepdims=True)
    return (x - m) / jnp.sqrt(v + eps)

def _scatter_add(tgt, idx, src, axis=0):
    return tgt.at[idx].add(src)

def _segment_sum(src, seg, n):
    return jax.ops.segment_sum(src, seg, n)
kernel_name = 'mk_prb_d2_jaxref_r8_864dfd'

def setup_inputs(seed: int=0):
    np.random.seed(seed)
    _w = jnp.asarray

    def _L0_attn_setup():
        import jax, jax.numpy as jnp
        import numpy as np
        B, T, D = (2, 256, 128)
        H, DK, DV = (16, 64, 64)

        def _hla(x, W_q, W_k, W_v, W_o):
            b, t, _ = x.shape
            q = (x @ W_q).reshape(b, t, H, DK).transpose(1, 0, 2, 3)
            k = (x @ W_k).reshape(b, t, H, DK).transpose(1, 0, 2, 3)
            v = (x @ W_v).reshape(b, t, H, DV).transpose(1, 0, 2, 3)
            S_K0 = jnp.zeros((b, H, DK, DK), x.dtype)
            C_QV0 = jnp.zeros((b, H, DK, DV), x.dtype)
            G0 = jnp.zeros((b, H, DK, DV), x.dtype)

            def step(carry, qkv):
                S_K, C_QV, G = carry
                q_t, k_t, v_t = qkv
                k_C = jnp.einsum('bhk,bhkv->bhv', k_t, C_QV)
                G = G + k_t[..., :, None] * k_C[..., None, :]
                S_K = S_K + k_t[..., :, None] * k_t[..., None, :]
                C_QV = C_QV + q_t[..., :, None] * v_t[..., None, :]
                S_C = jnp.einsum('bhkj,bhjv->bhkv', S_K, C_QV)
                o_t = jnp.einsum('bhk,bhkv->bhv', q_t, S_C - G)
                return ((S_K, C_QV, G), o_t)
            _, outs = jax.lax.scan(step, (S_K0, C_QV0, G0), (q, k, v))
            out = outs.transpose(1, 0, 2, 3).reshape(b, t, H * DV)
            return out @ W_o
        key = jax.random.key(seed)
        ks = jax.random.split(key, 5)
        scale = 0.1 * (6.0 / (D + D)) ** 0.5
        return {'x': jax.random.normal(ks[0], (B, T, D), dtype=jnp.float32), 'W_q': jax.random.normal(ks[1], (D, H * DK), dtype=jnp.float32) * scale, 'W_k': jax.random.normal(ks[2], (D, H * DK), dtype=jnp.float32) * scale, 'W_v': jax.random.normal(ks[3], (D, H * DV), dtype=jnp.float32) * scale, 'W_o': jax.random.normal(ks[4], (H * DV, D), dtype=jnp.float32) * scale}
    _L0_attn_in = _L0_attn_setup()

    def _L0_ffn_setup():
        import jax, jax.numpy as jnp
        import numpy as np
        D_MODEL = 128
        D_FF = 512
        N_EXPERTS = 8
        TOP_K = 2
        D_FF_PER = D_FF // N_EXPERTS
        B, T = (4, 256)
        key = jax.random.key(seed)
        ks = jax.random.split(key, 7)
        b1_bound = 1.0 / np.sqrt(D_MODEL)
        b2_bound = 1.0 / np.sqrt(D_FF_PER)
        return {'x': jax.random.normal(ks[0], (B, T, D_MODEL), dtype=jnp.float32), 'router_w': jax.random.uniform(ks[1], (D_MODEL, N_EXPERTS), minval=-b1_bound, maxval=b1_bound, dtype=jnp.float32), 'router_b': jax.random.uniform(ks[2], (N_EXPERTS,), minval=-b1_bound, maxval=b1_bound, dtype=jnp.float32), 'W1': jax.random.uniform(ks[3], (N_EXPERTS, D_MODEL, D_FF_PER), minval=-b1_bound, maxval=b1_bound, dtype=jnp.float32), 'b1': jax.random.uniform(ks[4], (N_EXPERTS, D_FF_PER), minval=-b1_bound, maxval=b1_bound, dtype=jnp.float32), 'W2': jax.random.uniform(ks[5], (N_EXPERTS, D_FF_PER, D_MODEL), minval=-b2_bound, maxval=b2_bound, dtype=jnp.float32), 'b2': jax.random.uniform(ks[6], (N_EXPERTS, D_MODEL), minval=-b2_bound, maxval=b2_bound, dtype=jnp.float32)}
    _L0_ffn_in = _L0_ffn_setup()

    def _L1_attn_setup():
        import jax, jax.numpy as jnp
        import numpy as np
        B, S, D, H, R = (2, 256, 128, 16, 64)
        HD = D // H
        VOCAB = 2 * R + 1
        key = jax.random.key(seed)
        ks = jax.random.split(key, 7)
        s = 0.02
        return {'x': jax.random.normal(ks[0], (B, S, D), jnp.float32), 'W_qkv': jax.random.normal(ks[1], (D, 3 * D), jnp.float32) * s, 'b_qkv': jnp.zeros((3 * D,), jnp.float32), 'W_out': jax.random.normal(ks[2], (D, D), jnp.float32) * s, 'b_out': jnp.zeros((D,), jnp.float32), 'rel_emb_k': jax.random.normal(ks[3], (VOCAB, HD), jnp.float32) * s, 'rel_emb_v': jax.random.normal(ks[4], (VOCAB, HD), jnp.float32) * s}
    _L1_attn_in = _L1_attn_setup()

    def _L1_ffn_setup():
        import jax, jax.numpy as jnp
        import numpy as np
        B, L, M = (4, 256, 128)
        G, E = (8, 8)
        CAP_FACTOR = 2.0

        def _ffn_size(m, widening=8.0):
            f = int(widening * m) * 2 // 3
            return f + (8 - f) % 8
        H = _ffn_size(M)

        def _gating_top2(logits, C):
            Gd, Sd, Ed = logits.shape
            raw = jax.nn.softmax(logits, axis=-1)
            idx1 = jnp.argmax(raw, axis=-1)
            m1 = jax.nn.one_hot(idx1, Ed, dtype=logits.dtype)
            gate1 = jnp.sum(raw * m1, axis=-1)
            rest = raw * (1.0 - m1)
            idx2 = jnp.argmax(rest, axis=-1)
            m2 = jax.nn.one_hot(idx2, Ed, dtype=logits.dtype)
            gate2 = jnp.sum(rest * m2, axis=-1)
            p1 = jnp.cumsum(m1, axis=-2) - m1
            m1 = m1 * (p1 < C).astype(m1.dtype)
            p1 = jnp.sum(p1 * m1, axis=-1)
            m1_flat = jnp.sum(m1, axis=-1)
            m1_count = jnp.sum(m1, axis=-2)
            p2 = jnp.cumsum(m2, axis=-2) - m2 + m1_count[:, None, :]
            m2 = m2 * (p2 < C).astype(m2.dtype)
            p2 = jnp.sum(p2 * m2, axis=-1)
            m2_flat = jnp.sum(m2, axis=-1)
            gate1 = gate1 * m1_flat
            gate2 = gate2 * m2_flat
            c1 = (gate1[..., None] * jax.nn.one_hot(idx1, Ed, dtype=jnp.float32))[..., None] * jax.nn.one_hot(p1.astype(jnp.int32), C, dtype=jnp.float32)[:, :, None, :]
            c2 = (gate2[..., None] * jax.nn.one_hot(idx2, Ed, dtype=jnp.float32))[..., None] * jax.nn.one_hot(p2.astype(jnp.int32), C, dtype=jnp.float32)[:, :, None, :]
            combine = (c1 + c2).astype(logits.dtype)
            dispatch = (combine != 0).astype(logits.dtype)
            return (dispatch, combine)
        key = jax.random.key(seed)
        k0, k1, k2, k3, k4 = jax.random.split(key, 5)
        return {'inputs': jax.random.normal(k0, (B, L, M), jnp.float32), 'router_w': jax.random.normal(k1, (M, E), jnp.float32) * 0.02, 'w0_kernel': jax.random.normal(k2, (E, M, H), jnp.float32) * 0.02, 'w1_kernel': jax.random.normal(k3, (E, M, H), jnp.float32) * 0.02, 'wo_kernel': jax.random.normal(k4, (E, H, M), jnp.float32) * 0.02}
    _L1_ffn_in = _L1_ffn_setup()
    _d = {'L0_attn_x': _L0_attn_in['x'], 'L0_attn_W_q': _L0_attn_in['W_q'], 'L0_attn_W_k': _L0_attn_in['W_k'], 'L0_attn_W_v': _L0_attn_in['W_v'], 'L0_attn_W_o': _L0_attn_in['W_o'], 'L0_ffn_router_w': _L0_ffn_in['router_w'], 'L0_ffn_router_b': _L0_ffn_in['router_b'], 'L0_ffn_W1': _L0_ffn_in['W1'], 'L0_ffn_b1': _L0_ffn_in['b1'], 'L0_ffn_W2': _L0_ffn_in['W2'], 'L0_ffn_b2': _L0_ffn_in['b2'], 'L1_attn_W_qkv': _L1_attn_in['W_qkv'], 'L1_attn_b_qkv': _L1_attn_in['b_qkv'], 'L1_attn_W_out': _L1_attn_in['W_out'], 'L1_attn_b_out': _L1_attn_in['b_out'], 'L1_attn_rel_emb_k': _L1_attn_in['rel_emb_k'], 'L1_attn_rel_emb_v': _L1_attn_in['rel_emb_v'], 'L1_ffn_router_w': _L1_ffn_in['router_w'], 'L1_ffn_w0_kernel': _L1_ffn_in['w0_kernel'], 'L1_ffn_w1_kernel': _L1_ffn_in['w1_kernel'], 'L1_ffn_wo_kernel': _L1_ffn_in['wo_kernel']}
    _x0 = _d['L0_attn_x']
    _d['L0_attn_x'] = jax.random.normal(jax.random.fold_in(jax.random.key(seed), 1), (16, 256, 128), dtype=_x0.dtype)
    del _x0
    return _d

def reference(L0_attn_x, L0_attn_W_q, L0_attn_W_k, L0_attn_W_v, L0_attn_W_o, L0_ffn_router_w, L0_ffn_router_b, L0_ffn_W1, L0_ffn_b1, L0_ffn_W2, L0_ffn_b2, L1_attn_W_qkv, L1_attn_b_qkv, L1_attn_W_out, L1_attn_b_out, L1_attn_rel_emb_k, L1_attn_rel_emb_v, L1_ffn_router_w, L1_ffn_w0_kernel, L1_ffn_w1_kernel, L1_ffn_wo_kernel):

    def _L0_attn_ref(x, W_q, W_k, W_v, W_o):
        import jax, jax.numpy as jnp
        import numpy as np
        B, T, D = (2, 256, 128)
        H, DK, DV = (16, 64, 64)

        def _hla(x, W_q, W_k, W_v, W_o):
            b, t, _ = x.shape
            q = (x @ W_q).reshape(b, t, H, DK).transpose(1, 0, 2, 3)
            k = (x @ W_k).reshape(b, t, H, DK).transpose(1, 0, 2, 3)
            v = (x @ W_v).reshape(b, t, H, DV).transpose(1, 0, 2, 3)
            S_K0 = jnp.zeros((b, H, DK, DK), x.dtype)
            C_QV0 = jnp.zeros((b, H, DK, DV), x.dtype)
            G0 = jnp.zeros((b, H, DK, DV), x.dtype)

            def step(carry, qkv):
                S_K, C_QV, G = carry
                q_t, k_t, v_t = qkv
                k_C = jnp.einsum('bhk,bhkv->bhv', k_t, C_QV)
                G = G + k_t[..., :, None] * k_C[..., None, :]
                S_K = S_K + k_t[..., :, None] * k_t[..., None, :]
                C_QV = C_QV + q_t[..., :, None] * v_t[..., None, :]
                S_C = jnp.einsum('bhkj,bhjv->bhkv', S_K, C_QV)
                o_t = jnp.einsum('bhk,bhkv->bhv', q_t, S_C - G)
                return ((S_K, C_QV, G), o_t)
            _, outs = jax.lax.scan(step, (S_K0, C_QV0, G0), (q, k, v))
            out = outs.transpose(1, 0, 2, 3).reshape(b, t, H * DV)
            return out @ W_o
        return _hla(x, W_q, W_k, W_v, W_o)

    def _L0_ffn_ref(x, router_w, router_b, W1, b1, W2, b2):
        import jax, jax.numpy as jnp
        import numpy as np
        D_MODEL = 128
        D_FF = 512
        N_EXPERTS = 8
        TOP_K = 2
        D_FF_PER = D_FF // N_EXPERTS
        B, T = (4, 256)
        router_logits = x @ router_w + router_b
        routing_weights = jax.nn.softmax(router_logits, axis=-1)
        top_k_weights, top_k_indices = jax.lax.top_k(routing_weights, TOP_K)
        top_k_weights = top_k_weights / jnp.sum(top_k_weights, axis=-1, keepdims=True)
        routing_mask = jnp.zeros_like(routing_weights)
        routing_mask = jnp.take_along_axis(routing_mask, top_k_indices, axis=-1)
        b_idx = jnp.arange(x.shape[0])[:, None, None]
        t_idx = jnp.arange(x.shape[1])[None, :, None]
        routing_mask = jnp.zeros_like(routing_weights).at[b_idx, t_idx, top_k_indices].set(top_k_weights)
        h1 = jnp.einsum('btd,nde->btne', x, W1) + b1
        h1 = jax.nn.gelu(h1, approximate=False)
        out_per_expert = jnp.einsum('btne,nef->btnf', h1, W2) + b2
        output = jnp.sum(out_per_expert * routing_mask[..., None], axis=-2)
        return output

    def _L1_attn_ref(x, W_qkv, b_qkv, W_out, b_out, rel_emb_k, rel_emb_v):
        import jax, jax.numpy as jnp
        import numpy as np
        B, S, D, H, R = (2, 256, 128, 16, 64)
        HD = D // H
        VOCAB = 2 * R + 1
        b, s, d = x.shape
        hd = d // H
        idx = jnp.arange(s)
        dist = jnp.clip(idx[None, :] - idx[:, None], -R, R) + R
        pe_k = rel_emb_k[dist]
        pe_v = rel_emb_v[dist]
        qkv = (x @ W_qkv + b_qkv).reshape(b, s, 3, H, hd)
        qkv = jnp.transpose(qkv, (2, 0, 3, 1, 4))
        q, k, v = (qkv[0], qkv[1], qkv[2])
        q = q / jnp.sqrt(jnp.asarray(hd, x.dtype))
        score = jnp.einsum('bhqd,bhkd->bhqk', q, k) + jnp.einsum('bhqd,qkd->bhqk', q, pe_k)
        attn = jax.nn.softmax(score, axis=-1)
        ctx = jnp.einsum('bhqk,bhkd->bhqd', attn, v) + jnp.einsum('bhqk,qkd->bhqd', attn, pe_v)
        ctx = jnp.transpose(ctx, (0, 2, 1, 3)).reshape(b, s, d)
        return ctx @ W_out + b_out

    def _L1_ffn_ref(inputs, router_w, w0_kernel, w1_kernel, wo_kernel):
        import jax, jax.numpy as jnp
        import numpy as np
        B, L, M = (4, 256, 128)
        G, E = (8, 8)
        CAP_FACTOR = 2.0

        def _ffn_size(m, widening=8.0):
            f = int(widening * m) * 2 // 3
            return f + (8 - f) % 8
        H = _ffn_size(M)

        def _gating_top2(logits, C):
            Gd, Sd, Ed = logits.shape
            raw = jax.nn.softmax(logits, axis=-1)
            idx1 = jnp.argmax(raw, axis=-1)
            m1 = jax.nn.one_hot(idx1, Ed, dtype=logits.dtype)
            gate1 = jnp.sum(raw * m1, axis=-1)
            rest = raw * (1.0 - m1)
            idx2 = jnp.argmax(rest, axis=-1)
            m2 = jax.nn.one_hot(idx2, Ed, dtype=logits.dtype)
            gate2 = jnp.sum(rest * m2, axis=-1)
            p1 = jnp.cumsum(m1, axis=-2) - m1
            m1 = m1 * (p1 < C).astype(m1.dtype)
            p1 = jnp.sum(p1 * m1, axis=-1)
            m1_flat = jnp.sum(m1, axis=-1)
            m1_count = jnp.sum(m1, axis=-2)
            p2 = jnp.cumsum(m2, axis=-2) - m2 + m1_count[:, None, :]
            m2 = m2 * (p2 < C).astype(m2.dtype)
            p2 = jnp.sum(p2 * m2, axis=-1)
            m2_flat = jnp.sum(m2, axis=-1)
            gate1 = gate1 * m1_flat
            gate2 = gate2 * m2_flat
            c1 = (gate1[..., None] * jax.nn.one_hot(idx1, Ed, dtype=jnp.float32))[..., None] * jax.nn.one_hot(p1.astype(jnp.int32), C, dtype=jnp.float32)[:, :, None, :]
            c2 = (gate2[..., None] * jax.nn.one_hot(idx2, Ed, dtype=jnp.float32))[..., None] * jax.nn.one_hot(p2.astype(jnp.int32), C, dtype=jnp.float32)[:, :, None, :]
            combine = (c1 + c2).astype(logits.dtype)
            dispatch = (combine != 0).astype(logits.dtype)
            return (dispatch, combine)
        Bb, Ll, Mm = inputs.shape
        S = Bb * Ll // G
        x = inputs.reshape(G, S, Mm)
        logits = jnp.einsum('GSM,ME->GSE', x, router_w)
        cap = int(CAP_FACTOR * S / E)
        C = (cap + 3) // 4 * 4
        dispatch, combine = _gating_top2(logits, C)
        expert_inputs = jnp.einsum('GSEC,GSM->EGCM', dispatch, x)
        layer_w0 = jnp.einsum('EGCM,EMH->EGCH', expert_inputs, w0_kernel)
        layer_w1 = jnp.einsum('EGCM,EMH->EGCH', expert_inputs, w1_kernel)
        hidden = jax.nn.gelu(layer_w0, approximate=True) * layer_w1
        expert_outputs = jnp.einsum('EGCH,EHM->EGCM', hidden, wo_kernel)
        out = jnp.einsum('EGCM,GSEC->GSM', expert_outputs, combine)
        return out.reshape(Bb, Ll, Mm)
    x = L0_attn_x
    xn = _layernorm(x, axis=-1)
    x = x + _L0_attn_ref(xn, L0_attn_W_q, L0_attn_W_k, L0_attn_W_v, L0_attn_W_o) + _L0_ffn_ref(xn, L0_ffn_router_w, L0_ffn_router_b, L0_ffn_W1, L0_ffn_b1, L0_ffn_W2, L0_ffn_b2)
    xn = _layernorm(x, axis=-1)
    x = x + _L1_attn_ref(xn, L1_attn_W_qkv, L1_attn_b_qkv, L1_attn_W_out, L1_attn_b_out, L1_attn_rel_emb_k, L1_attn_rel_emb_v) + _L1_ffn_ref(xn, L1_ffn_router_w, L1_ffn_w0_kernel, L1_ffn_w1_kernel, L1_ffn_wo_kernel)
    return x

_drawn_inputs = setup_inputs


def setup_inputs(seed=0):
    import zlib

    import numpy as np

    out = dict(_drawn_inputs(seed))
    spreads = {'L1_attn_b_qkv': (0.0, 0.761), 'L1_attn_b_out': (0.0, 0.539)}
    factors = {'L0_ffn_router_b': 3.709,
     'L0_ffn_b1': 8.0,
     'L1_attn_W_qkv': 8.0,
     'L1_attn_W_out': 5.426,
     'L1_attn_rel_emb_k': 8.0,
     'L1_attn_rel_emb_v': 8.0,
     'L1_ffn_router_w': 8.0,
     'L1_ffn_w0_kernel': 8.0,
     'L1_ffn_w1_kernel': 8.0,
     'L1_ffn_wo_kernel': 8.0}
    for name, (base, spread) in spreads.items():
        noise = np.random.default_rng([zlib.crc32(name.encode()), seed]).standard_normal(out[name].shape)
        drawn = base * np.exp(spread * noise) if base else spread * noise
        out[name] = jnp.asarray(drawn.astype(out[name].dtype))
    for name, factor in factors.items():
        out[name] = (out[name] * factor).astype(out[name].dtype)
    return out
```

```python
import concourse.bass as bass
from concourse import mybir
from contextlib import ExitStack

F32 = mybir.dt.float32
BF16 = mybir.dt.bfloat16
U32 = mybir.dt.uint32
I32 = mybir.dt.int32
ALU = mybir.AluOpType
ACT = mybir.ActivationFunctionType
AX = mybir.AxisListType

P = 128
B, T, D = 16, 256, 128
NT = B * T // P
TPG = 4
NG = NT // TPG
GT = TPG * P
EPS = 1e-5
H0, DK = 16, 64
PAIRS = H0 // 2
E = 8
FF0 = 512
FC0 = FF0 // P
EPC = P // (FF0 // E)


class Pool:

    def __init__(self, nc):
        self.nc, self.ctx = nc, ExitStack()

    def __enter__(self):
        self.ctx.__enter__()
        return self

    def __exit__(self, *a):
        return self.ctx.__exit__(*a)

    def sb(self, name, shape, dt=F32):
        return self.ctx.enter_context(self.nc.sbuf_tensor(name, shape, dt))

    def ps(self, name, shape=(P, 512), dt=F32):
        return self.ctx.enter_context(self.nc.psum_tensor(name, list(shape), dt))

    def sem(self, name):
        return self.ctx.enter_context(self.nc.semaphore(name))


class Steps:

    def __init__(self, sem, base=0):
        self.sem, self.base, self.n = sem, base, 0

    def value(self):
        self.n += 1
        return self.base + self.n


def up(n):
    return max(n, 0) if isinstance(n, int) else n


def rolled(eng, n, body):
    body(0)
    with eng.Fori(1, n) as i:
        body(i)


def constants(nc, ident, mask, expand, iota_e, ltri, ones_bf, group_base, one):
    with Pool(nc) as m:
        cs = m.sem("const_step")
        io = m.sb("iota_i", [P, E], I32)
        io_g = m.sb("iota_g", [P, NT], I32)
        with nc.Block() as block:
            @block.gpsimd
            def _(pool):
                nc.gpsimd.memset(ident[:, :], 0.0).then_inc(cs, 1)
                nc.gpsimd.memset(mask[:, :], 1.0).then_inc(cs, 1)
                nc.gpsimd.memset(expand[:, :, :], 1.0).then_inc(cs, 1)
                nc.gpsimd.memset(ltri[:, :], 1.0).then_inc(cs, 1)
                nc.gpsimd.memset(ones_bf[:, :], 1.0).then_inc(cs, 1)
                nc.gpsimd.memset(one[:, :], 1.0).then_inc(cs, 1)
                nc.gpsimd.iota(io[:, :], pattern=[[1, E]], base=0, channel_multiplier=0).then_inc(cs, 1)
                nc.gpsimd.iota(io_g[:, :], pattern=[[CAP, NG], [0, TPG]], base=0, channel_multiplier=0).then_inc(cs, 1)
                pool.wait_ge(cs, 8)
                nc.gpsimd.tensor_copy(group_base[:, :], io_g[:, :]).then_inc(cs, 1)
                nc.gpsimd.affine_select(out=ident[:, :], in_=ident[:, :], compare_op=ALU.not_equal, fill=1.0,
                                        base=0, pattern=[[-1, P]], channel_multiplier=1).then_inc(cs, 1)
                nc.gpsimd.affine_select(out=mask[:, 0:T], in_=mask[:, 0:T], compare_op=ALU.is_ge, fill=0.0,
                                        base=0, pattern=[[1, T]], channel_multiplier=-1).then_inc(cs, 1)
                nc.gpsimd.affine_select(out=mask[:, T:T + P], in_=mask[:, T:T + P], compare_op=ALU.is_ge, fill=0.0,
                                        base=0, pattern=[[1, P]], channel_multiplier=-1).then_inc(cs, 1)
                nc.gpsimd.affine_select(out=ltri[:, :], in_=ltri[:, :], compare_op=ALU.is_gt, fill=0.0,
                                        base=0, pattern=[[1, P]], channel_multiplier=-1).then_inc(cs, 1)
                w = FF0 // E
                nc.gpsimd.affine_select(out=expand[:, :, :], in_=expand[:, :, :], compare_op=ALU.is_ge, fill=0.0,
                                        base=0, pattern=[[P, FC0], [1, P]], channel_multiplier=-w).then_inc(cs, 1)
                nc.gpsimd.tensor_copy(iota_e[:, :], io[:, :]).then_inc(cs, 1)
                pool.wait_ge(cs, 15)
                nc.gpsimd.affine_select(out=expand[:, :, :], in_=expand[:, :, :], compare_op=ALU.is_ge, fill=0.0,
                                        base=w - 1, pattern=[[-P, FC0], [-1, P]], channel_multiplier=w).then_inc(cs, 1)
                pool.wait_ge(cs, 16)


def norm_stage(nc, x_all, xn_all, xnT_all, ident, router, logits, tag, load=None):
    with Pool(nc) as m:
        stats = m.sb(tag + "stats", [P, NT, 6])
        mean = m.sb(tag + "mean", [P, NT])
        mean2 = m.sb(tag + "mean2", [P, NT])
        rstd = m.sb(tag + "rstd", [P, NT])
        xn = [m.sb(f"{tag}xn{i}", [P, TPG, D]) for i in range(2)]
        xT = [m.sb(f"{tag}xT{i}", [P, GT]) for i in range(2)]
        ps_t = [m.ps(f"{tag}ps_t{i}") for i in range(2)]
        ps_l = [m.ps(f"{tag}ps_l{i}", (P, TPG, E)) for i in range(2)]
        loaded = m.sem(tag + "loaded")
        own = m.sem(tag + "vec_step")
        var_ready = m.sem(tag + "var_ready")
        std_ready = m.sem(tag + "std_ready")
        xn_ready = m.sem(tag + "xn_ready")
        xn_kept = m.sem(tag + "xn_kept")
        xT_done = m.sem(tag + "xT_done")
        xT_ready = m.sem(tag + "xT_ready")
        xT_kept = m.sem(tag + "xT_kept")
        lg_done = m.sem(tag + "lg_done")
        lg_kept = m.sem(tag + "lg_kept")
        with nc.Block() as block:
            @block.sync
            def _(sp):
                if load is not None:
                    for dst, src in load:
                        sp.dma_start(dst, src).then_inc(loaded, 16)

            @block.vector
            def _(v):
                st = Steps(own, NT)

                def done(ins):
                    ins.then_inc(own, 1)
                    v.wait_ge(own, st.value())

                if load is not None:
                    v.wait_ge(loaded, 16 * len(load))
                with v.Fori(0, NT) as t:
                    nc.vector.bn_stats(stats[:, bass.ds(t, 1), :], x_all[:, bass.ds(t, 1), :]).then_inc(own, 1)
                v.wait_ge(own, NT)
                done(nc.vector.tensor_tensor(mean[:, :], stats[:, :, 1], stats[:, :, 4], ALU.subtract))
                done(nc.vector.tensor_tensor(rstd[:, :], mean[:, :], mean[:, :], ALU.mult))
                done(nc.vector.tensor_scalar(rstd[:, :], rstd[:, :], 0.25, EPS, ALU.mult, ALU.add))
                done(nc.vector.tensor_tensor(mean[:, :], stats[:, :, 2], stats[:, :, 5], ALU.add))
                done(nc.vector.tensor_scalar(mean[:, :], mean[:, :], 1.0 / D, None, ALU.mult))
                nc.vector.tensor_tensor(rstd[:, :], rstd[:, :], mean[:, :], ALU.add).then_inc(var_ready, 1)
                done(nc.vector.tensor_tensor(mean2[:, :], stats[:, :, 1], stats[:, :, 4], ALU.add))
                done(nc.vector.tensor_scalar(mean2[:, :], mean2[:, :], 0.5, None, ALU.mult))
                v.wait_ge(std_ready, 1)
                done(nc.vector.reciprocal(rstd[:, :], rstd[:, :]))
                def group(half):
                    g = half * 2
                    for i in range(2):
                        v.wait_ge(xT_done, g)
                        if xn_all is not None:
                            v.wait_ge(xn_kept, g)
                        for j in range(TPG):
                            t = (g + i) * TPG + j
                            ins = nc.vector.tensor_scalar(xn[i][:, j, :], x_all[:, bass.ds(t, 1), :],
                                                          mean2[:, bass.ds(t, 1)], rstd[:, bass.ds(t, 1)],
                                                          ALU.subtract, ALU.mult)
                        ins.then_inc(xn_ready, 1)
                    for i in range(2):
                        v.wait_ge(lg_done, g + i + 1)
                        nc.vector.tensor_copy(logits[:, bass.ds((g + i) * TPG, TPG), :], ps_l[i][:, :, :]).then_inc(lg_kept, 1)

                rolled(v, NG // 2, group)
                v.wait_ge(lg_kept, NG)

            @block.scalar
            def _(a):
                a.wait_ge(var_ready, 1)
                nc.scalar.activation(rstd[:, :], rstd[:, :], ACT.Sqrt).then_inc(std_ready, 1)
                def group(half):
                    g = half * 2
                    for i in range(2):
                        a.wait_ge(xT_done, g + i + 1)
                        a.wait_ge(xT_kept, g)
                        nc.scalar.activation(xT[i][:, :], ps_t[i][:, :], ACT.Copy).then_inc(xT_ready, 1)

                rolled(a, NG // 2, group)
                a.wait_ge(xT_ready, NG)

            @block.tensor
            def _(pe):
                if load is not None:
                    pe.wait_ge(loaded, 16 * len(load))
                def group(half):
                    g = half * 2
                    for i in range(2):
                        pe.wait_ge(xn_ready, g + i + 1)
                        for j in range(TPG):
                            ins = nc.tensor.transpose(ps_t[i][:, j * P:(j + 1) * P], xn[i][:, j, :], ident[:, :])
                        ins.then_inc(xT_done, 1)
                    for i in range(2):
                        pe.wait_ge(xT_ready, g + i + 1)
                        pe.wait_ge(lg_kept, g)
                        for j in range(TPG):
                            ins = nc.tensor.matmul(ps_l[i][:, j, :], xT[i][:, j * P:(j + 1) * P], router[:, :],
                                                   start=True, stop=True)
                        ins.then_inc(lg_done, 1)

                rolled(pe, NG // 2, group)

            @block.gpsimd
            def _(pool):
                def group(half):
                    g = half * 2
                    for i in range(2):
                        if xn_all is not None:
                            pool.wait_ge(xn_ready, g + i + 1)
                            nc.gpsimd.tensor_copy(xn_all[:, bass.ds((g + i) * TPG, TPG), :], xn[i][:, :, :]).then_inc(xn_kept, 1)
                    for i in range(2):
                        pool.wait_ge(xT_ready, g + i + 1)
                        nc.gpsimd.tensor_copy(xnT_all[:, bass.ds((g + i) * GT, GT)], xT[i][:, :]).then_inc(xT_kept, 1)

                rolled(pool, NG // 2, group)
                pool.wait_ge(xT_kept, NG)
                if xn_all is not None:
                    pool.wait_ge(xn_kept, NG)


def bc(ap, axis, n):
    shape = list(ap.shape)
    shape.insert(axis, n)
    return ap.unsqueeze(axis).to_broadcast(shape)


def top2_steps(nc, v, done, soft, iota_e, m, tag, exp_start, exp_done):
    shape = [P, NT, E]
    mx = m.sb(tag + "mx", [P, NT])
    done(nc.vector.reduce_max(mx[:, :], soft[:, :, :], AX.X))
    nc.vector.tensor_tensor(soft[:, :, :], soft[:, :, :], bc(mx[:, :], 2, E), ALU.subtract).then_inc(exp_start, 1)
    v.wait_ge(exp_done, 1)
    done(nc.vector.reduce_sum(mx[:, :], soft[:, :, :], AX.X))
    done(nc.vector.reciprocal(mx[:, :], mx[:, :]))
    done(nc.vector.tensor_tensor(soft[:, :, :], soft[:, :, :], bc(mx[:, :], 2, E), ALU.mult))
    picks = []
    rest = soft
    for k in range(2):
        gate = m.sb(f"{tag}gate{k}", [P, NT])
        idx = m.sb(f"{tag}idx{k}", [P, NT])
        hot = m.sb(f"{tag}hot{k}", shape)
        cand = m.sb(f"{tag}cand{k}", shape)
        done(nc.vector.reduce_max(gate[:, :], rest[:, :, :], AX.X))
        done(nc.vector.tensor_tensor(hot[:, :, :], rest[:, :, :], bc(gate[:, :], 2, E), ALU.is_equal))
        done(nc.vector.tensor_scalar(cand[:, :, :], hot[:, :, :], -16.0, None, ALU.mult))
        done(nc.vector.tensor_tensor(cand[:, :, :], cand[:, :, :], bc(iota_e[:, :], 1, NT), ALU.add))
        done(nc.vector.tensor_reduce(idx[:, :], cand[:, :, :], AX.X, ALU.min))
        done(nc.vector.tensor_tensor(hot[:, :, :], cand[:, :, :], bc(idx[:, :], 2, E), ALU.is_equal))
        done(nc.vector.tensor_scalar(idx[:, :], idx[:, :], 16.0, None, ALU.add))
        picks.append((hot, idx, gate))
        if k == 0:
            rest = m.sb(tag + "rest", shape)
            done(nc.vector.tensor_tensor(cand[:, :, :], soft[:, :, :], hot[:, :, :], ALU.mult))
            done(nc.vector.tensor_tensor(rest[:, :, :], soft[:, :, :], cand[:, :, :], ALU.subtract))
    return picks


def ffn0_stage(nc, x_all, xnT_all, logits, router_b, W1, b1, W2, b2, ident, expand, iota_e):
    with Pool(nc) as m:
        w1 = m.sb("f0w1", [P, FC0, P])
        w2 = m.sb("f0w2", [P, FC0, D])
        b1c = m.sb("f0b1", [P, FC0])
        b2s = m.sb("f0b2", [E, D])
        rb = m.sb("f0rb", [P, E])
        wt = m.sb("f0wt", [P, NT, E])
        wtg = m.sb("f0wtg", [P, TPG, E])
        wT = m.sb("f0wT", [E, GT])
        h = m.sb("f0h", [P, FC0, GT])
        hw = m.sb("f0hw", [P, FC0, GT])
        den = m.sb("f0den", [P, NT])
        ps_h = [m.ps(f"f0ps_h{i}") for i in range(FC0)]
        ps_w = [m.ps(f"f0ps_w{i}") for i in range(2)]
        ps_t = m.ps("f0ps_t")
        ps_y = m.ps("f0ps_y", (P, TPG, D))
        loaded = m.sem("f0loaded")
        own = m.sem("f0vec_step")
        exp_start = m.sem("f0exp_start")
        exp_done = m.sem("f0exp_done")
        h_done = m.sem("f0h_done")
        h_ready = m.sem("f0h_ready")
        wtg_ready = m.sem("f0wtg_ready")
        wT_done = m.sem("f0wT_done")
        wT_ready = m.sem("f0wT_ready")
        w_done = m.sem("f0w_done")
        hw_ready = m.sem("f0hw_ready")
        y_done = m.sem("f0y_done")
        y_added = m.sem("f0y_added")
        NL = 6
        with nc.Block() as block:
            @block.sync
            def _(sp):
                sp.dma_start(rb[:, :], router_b.partition_broadcast(P)).then_inc(loaded, 16)
                for e in range(E):
                    c, o = divmod(e * (FF0 // E), P)
                    if e == 0:
                        sp.dma_start(w1[:, :, :].rearrange("p c (e f) -> p (c e) f", e=EPC),
                                     W1.rearrange("e d f -> d e f")).then_inc(loaded, 16)
                sp.dma_start(w2[:, :, :], W2.rearrange("e f d -> (e f) d").rearrange("(c p) d -> p c d", p=P)).then_inc(loaded, 16)
                sp.dma_start(b1c[:, :], b1.rearrange("(c e) f -> (e f) c", e=EPC), allow_slow_non_contiguous=True).then_inc(loaded, 16)
                sp.dma_start(b2s[:, :], b2).then_inc(loaded, 16)

            @block.vector
            def _(v):
                st = Steps(own)

                def done(ins):
                    ins.then_inc(own, 1)
                    v.wait_ge(own, st.value())

                v.wait_ge(loaded, 16 * 5)
                done(nc.vector.tensor_tensor(wt[:, :, :], logits[:, :, :], bc(rb[:, :], 1, NT), ALU.add))
                (hot1, _, g1), (hot2, _, g2) = top2_steps(nc, v, done, wt, iota_e, m, "f0", exp_start, exp_done)
                done(nc.vector.tensor_tensor(den[:, :], g1[:, :], g2[:, :], ALU.add))
                done(nc.vector.reciprocal(den[:, :], den[:, :]))
                done(nc.vector.tensor_tensor(g1[:, :], g1[:, :], den[:, :], ALU.mult))
                done(nc.vector.tensor_tensor(g2[:, :], g2[:, :], den[:, :], ALU.mult))
                done(nc.vector.tensor_tensor(hot1[:, :, :], hot1[:, :, :], bc(g1[:, :], 2, E), ALU.mult))
                done(nc.vector.tensor_tensor(hot2[:, :, :], hot2[:, :, :], bc(g2[:, :], 2, E), ALU.mult))
                done(nc.vector.tensor_tensor(wt[:, :, :], hot1[:, :, :], hot2[:, :, :], ALU.add))
                def group(g):
                    v.wait_ge(wT_done, g)
                    nc.vector.tensor_copy(wtg[:, :, :], wt[:, bass.ds(g * TPG, TPG), :]).then_inc(wtg_ready, 1)
                    for c in range(FC0):
                        v.wait_ge(h_ready, g * FC0 + c + 1)
                        v.wait_ge(w_done, g * FC0 + c + 1)
                        nc.vector.tensor_tensor(hw[:, c, :], h[:, c, :], ps_w[c % 2][:, :], ALU.mult).then_inc(hw_ready, 1)
                    v.wait_ge(y_done, g + 1)
                    xs = x_all[:, bass.ds(g * TPG, TPG), :]
                    nc.vector.tensor_tensor(xs, xs, ps_y[:, :, :], ALU.add).then_inc(y_added, 1)

                rolled(v, NG, group)
                v.wait_ge(y_added, NG)

            @block.scalar
            def _(a):
                a.wait_ge(exp_start, 1)
                nc.scalar.activation(wt[:, :, :], wt[:, :, :], ACT.Exp).then_inc(exp_done, 1)
                a.wait_ge(loaded, 16 * 5)
                def group(g):
                    a.wait_ge(wT_done, g + 1)
                    nc.scalar.activation(wT[:, :], ps_t[0:E, :], ACT.Copy).then_inc(wT_ready, 1)
                    for c in range(FC0):
                        a.wait_ge(h_done, g * FC0 + c + 1)
                        a.wait_ge(hw_ready, g * FC0)
                        nc.scalar.activation(h[:, c, :], ps_h[c][:, :], ACT.Gelu, bias=b1c[:, c:c + 1]).then_inc(h_ready, 1)

                rolled(a, NG, group)

            @block.tensor
            def _(pe):
                pe.wait_ge(loaded, 16 * 5)
                def group(g):
                    pe.wait_ge(wtg_ready, g + 1)
                    for j in range(TPG):
                        ins = nc.tensor.transpose(ps_t[0:E, j * P:(j + 1) * P], wtg[:, j, :], ident[:, :])
                    ins.then_inc(wT_done, 1)
                    for c in range(FC0):
                        pe.wait_ge(h_ready, g * FC0)
                        nc.tensor.matmul(ps_h[c][:, :], w1[:, c, :], xnT_all[:, bass.ds(g * GT, GT)],
                                         start=True, stop=True).then_inc(h_done, 1)
                    pe.wait_ge(wT_ready, g + 1)
                    for c in range(FC0):
                        if c >= 2:
                            pe.wait_ge(hw_ready, up(g * FC0 + c - 1))
                        nc.tensor.matmul(ps_w[c % 2][:, :], expand[:, c, :], wT[:, :], start=True, stop=True).then_inc(w_done, 1)
                    pe.wait_ge(hw_ready, (g + 1) * FC0)
                    pe.wait_ge(y_added, g)
                    for j in range(TPG):
                        for c in range(FC0):
                            nc.tensor.matmul(ps_y[:, j, :], hw[:, c, j * P:(j + 1) * P], w2[:, c, :],
                                             start=(c == 0), stop=False)
                        ins = nc.tensor.matmul(ps_y[:, j, :], wT[:, j * P:(j + 1) * P], b2s[:, :], start=False, stop=True)
                    ins.then_inc(y_done, 1)

                rolled(pe, NG, group)


def attn0_stage(nc, x_all, xnT_all, Wq, Wk, Wv, Wo, mask, one):
    HB = T + P
    with Pool(nc) as m:
        w_in = m.sb("a0w_in", [P, 3, H0 * DK])
        w_out = m.sb("a0w_out", [P, PAIRS, D])
        w_qk = m.sb("a0w_qk", [P, 2, P])
        w_v = m.sb("a0w_v", [P, P])
        xb = m.sb("a0xb", [P, T])
        qk = m.sb("a0qk", [P, 2, T])
        vv = m.sb("a0v", [P, 2, P])
        AT = [m.sb(f"a0AT{i}", [P, HB]) for i in range(2)]
        MT = [m.sb(f"a0MT{i}", [P, HB]) for i in range(2)]
        oT = m.sb("a0oT", [P, PAIRS, T])
        ps_qk = m.ps("a0ps_qk", (P, 2, T))
        ps_v = m.ps("a0ps_v", (P, 2, P))
        ps_A = [m.ps(f"a0ps_A{i}") for i in range(2)]
        ps_M = [m.ps(f"a0ps_M{i}") for i in range(2)]
        ps_o = m.ps("a0ps_o")
        ps_y = m.ps("a0ps_y", (P, 2, D))
        loaded = m.sem("a0loaded")
        xb_ready = m.sem("a0xb_ready")
        wqk_ready = m.sem("a0wqk_ready")
        wv_ready = m.sem("a0wv_ready")
        qk_done, qk_ready = m.sem("a0qk_done"), m.sem("a0qk_ready")
        v_done, v_ready = m.sem("a0v_done"), m.sem("a0v_ready")
        A_done, A_ready = m.sem("a0A_done"), m.sem("a0A_ready")
        M_done, M_ready = m.sem("a0M_done"), m.sem("a0M_ready")
        o_done, o_ready = m.sem("a0o_done"), m.sem("a0o_ready")
        y_done, y_added = m.sem("a0y_done"), m.sem("a0y_added")
        with nc.Block() as block:
            @block.sync
            def _(sp):
                for i, w in enumerate((Wq, Wk, Wv)):
                    sp.dma_start(w_in[:, i, :], w).then_inc(loaded, 16)
                sp.dma_start(w_out[:, :, :], Wo.rearrange("(c p) d -> p c d", p=P)).then_inc(loaded, 16)

            @block.gpsimd
            def _(pool):
                def copy(dst, src):
                    return nc.gpsimd.tensor_tensor(dst, src, one[:, :].to_broadcast([P, P]) if len(dst.shape) == 2
                                                   else bc(one[:, :].to_broadcast([P, P]), 1, 2), ALU.mult)

                pool.wait_ge(loaded, 16 * 4)
                def batch(b):
                    pool.wait_ge(v_done, b * PAIRS)
                    nc.gpsimd.tensor_copy(xb[:, :], xnT_all[:, bass.ds(b * T, T)]).then_inc(xb_ready, 1)

                    def pair(p):
                        pool.wait_ge(qk_done, b * PAIRS + p)
                        copy(w_qk[:, :, :], w_in[:, 0:2, bass.ds(p * P, P)]).then_inc(wqk_ready, 1)
                        pool.wait_ge(v_done, b * PAIRS + p)
                        copy(w_v[:, :], w_in[:, 2, bass.ds(p * P, P)]).then_inc(wv_ready, 1)

                    rolled(pool, PAIRS, pair)

                rolled(pool, B, batch)

            @block.tensor
            def _(pe):
                def project_qk(b, p):
                    pe.wait_ge(wqk_ready, b * PAIRS + p + 1)
                    for i in range(2):
                        ins = nc.tensor.matmul(ps_qk[:, i, :], w_qk[:, i, :], xnT_all[:, bass.ds(b * T, T)],
                                               start=True, stop=True)
                    ins.then_inc(qk_done, 1)

                def scores(b, p):
                    pe.wait_ge(qk_ready, b * PAIRS + p + 1)
                    for h in range(2):
                        r = slice(h * DK, (h + 1) * DK)
                        nc.tensor.matmul(ps_A[h][:, 0:T], qk[r, 1, 0:P], qk[r, 0, :], start=True, stop=True)
                        nc.tensor.matmul(ps_A[h][:, T:HB], qk[r, 1, P:T], qk[r, 0, P:T],
                                         start=True, stop=True).then_inc(A_done, 1)

                def values(b, p):
                    pe.wait_ge(wv_ready, b * PAIRS + p + 1)
                    pe.wait_ge(xb_ready, b + 1)
                    for j in range(2):
                        ins = nc.tensor.matmul(ps_v[:, j, :], xb[:, j * P:(j + 1) * P], w_v[:, :], start=True, stop=True)
                    ins.then_inc(v_done, 1)

                def squares(b, p):
                    for h in range(2):
                        pe.wait_ge(A_ready, (b * PAIRS + p) * 2 + h + 1)
                        nc.tensor.matmul(ps_M[h][:, 0:T], AT[h][:, 0:P], AT[h][:, 0:T], start=True, stop=True)
                        nc.tensor.matmul(ps_M[h][:, T:HB], AT[h][:, P:T], AT[h][:, P:T], start=True, stop=False)
                        nc.tensor.matmul(ps_M[h][:, T:HB], AT[h][:, T:HB], AT[h][:, T:HB],
                                         start=False, stop=True).then_inc(M_done, 1)

                def outputs(b, p):
                    pe.wait_ge(o_ready, b * PAIRS + p + 1)
                    pe.wait_ge(v_ready, b * PAIRS + p + 1)
                    for h in range(2):
                        r = slice(h * DK, (h + 1) * DK)
                        pe.wait_ge(M_ready, (b * PAIRS + p) * 2 + h + 1)
                        nc.tensor.matmul(ps_o[r, 0:T], vv[:, 0, r], MT[h][:, 0:T], start=True, stop=False)
                        ins = nc.tensor.matmul(ps_o[r, P:T], vv[:, 1, r], MT[h][:, T:HB], start=False, stop=True)
                    ins.then_inc(o_done, 1)

                pe.wait_ge(loaded, 16 * 4)
                def batch(b):
                    project_qk(b, 0)
                    scores(b, 0)
                    project_qk(b, 1)
                    values(b, 0)
                    squares(b, 0)
                    with pe.Fori(1, PAIRS - 1) as p:
                        scores(b, p)
                        project_qk(b, p + 1)
                        outputs(b, p - 1)
                        values(b, p)
                        squares(b, p)
                    last = PAIRS - 1
                    scores(b, last)
                    outputs(b, last - 1)
                    values(b, last)
                    squares(b, last)
                    outputs(b, last)
                    pe.wait_ge(y_added, b)
                    for j in range(2):
                        for p in range(PAIRS):
                            if j == 0 and p in (0, last):
                                pe.wait_ge(o_ready, b * PAIRS + (last if p == 0 else PAIRS) + 1)
                            ins = nc.tensor.matmul(ps_y[:, j, :], oT[:, p, j * P:(j + 1) * P], w_out[:, p, :],
                                                   start=(p == 0), stop=(p == last))
                    ins.then_inc(y_done, 1)

                rolled(pe, B, batch)

            @block.scalar
            def _(a):
                nc.scalar.sem_inc(o_ready, 1)

                def keep_qk(b, p):
                    a.wait_ge(qk_done, b * PAIRS + p + 1)
                    nc.scalar.activation(qk[:, :, :], ps_qk[:, :, :], ACT.Copy).then_inc(qk_ready, 1)

                def keep_v(b, p):
                    a.wait_ge(v_done, b * PAIRS + p + 1)
                    nc.scalar.activation(vv[:, :, :], ps_v[:, :, :], ACT.Copy).then_inc(v_ready, 1)

                def keep_o(b, p):
                    a.wait_ge(o_done, b * PAIRS + p + 1)
                    a.wait_ge(y_done, b)
                    nc.scalar.activation(oT[:, bass.ds(p, 1), :], ps_o[:, 0:T], ACT.Copy).then_inc(o_ready, 1)

                def batch(b):
                    keep_qk(b, 0)
                    keep_qk(b, 1)
                    keep_v(b, 0)
                    with a.Fori(1, PAIRS - 1) as p:
                        keep_qk(b, p + 1)
                        keep_o(b, p - 1)
                        keep_v(b, p)
                    keep_o(b, PAIRS - 2)
                    keep_v(b, PAIRS - 1)
                    keep_o(b, PAIRS - 1)

                rolled(a, B, batch)

            @block.vector
            def _(v):
                def batch(b):
                    with v.Fori(0, PAIRS) as p:
                        for h in range(2):
                            v.wait_ge(A_done, (b * PAIRS + p) * 2 + h + 1)
                            nc.vector.tensor_tensor(AT[h][:, :], ps_A[h][:, 0:HB], mask[:, :], ALU.mult).then_inc(A_ready, 1)
                        for h in range(2):
                            v.wait_ge(M_done, (b * PAIRS + p) * 2 + h + 1)
                            nc.vector.tensor_tensor(MT[h][:, :], ps_M[h][:, 0:HB], mask[:, :], ALU.mult).then_inc(M_ready, 1)
                    v.wait_ge(y_done, b + 1)
                    xs = x_all[:, bass.ds(b * 2, 2), :]
                    nc.vector.tensor_tensor(xs, xs, ps_y[:, :, :], ALU.add).then_inc(y_added, 1)

                rolled(v, B, batch)
                v.wait_ge(y_added, B)


CAP = (int(2.0 * GT / E) + 3) // 4 * 4
HID = int(8.0 * D) * 2 // 3
HID = HID + (8 - HID) % 8
HC = -(-HID // P)
SLOTS = E * NG * CAP
ET = NG * CAP
DROPPED = float(2 * SLOTS)


def hrows(c):
    return min(P, HID - c * P)


def gate1_stage(nc, logits, iota_e, ltri, ones_bf, xn_all, slots_dram, gates, slot_ids, group_base):
    with Pool(nc) as m:
        soft = m.sb("g1soft", [P, NT, E])
        hotb = [m.sb(f"g1hotb{k}", [P, NT, E], BF16) for k in range(2)]
        keptb = m.sb("g1keptb", [P, NT, E], BF16)
        kept = m.sb("g1kept", [P, NT, E])
        place = m.sb("g1place", [P, NT, E])
        pos = m.sb("g1pos", [P, NT])
        flat = m.sb("g1flat", [P, NT])
        slot = m.sb("g1slot", [P, NT])
        gone = m.sb("g1gone", [P, NT])
        send_ids = m.sb("g1send", [P, 2, NT], U32)
        zeros = m.sb("g1zeros", [P, SLOTS // P, 16])
        ps_p = [m.ps(f"g1ps_p{k}", (P, TPG, NG, E)) for k in range(2)]
        own = m.sem("g1vec_step")
        exp_start, exp_done = m.sem("g1exp_start"), m.sem("g1exp_done")
        hot_ready, kept_ready = m.sem("g1hot_ready"), m.sem("g1kept_ready")
        place_done = m.sem("g1place_done")
        zero_ready, zeroed = m.sem("g1zero_ready"), m.sem("g1zeroed")
        ids_ready, sent = m.sem("g1ids_ready"), m.sem("g1sent")
        NZ = D // 16
        with nc.Block() as block:
            @block.sync
            def _(sp):
                sp.wait_ge(zero_ready, 1)
                for z in range(NZ):
                    sp.dma_start(slots_dram.rearrange("(p s) d -> p s d", p=P)[:, :, z * 16:(z + 1) * 16],
                                 zeros[:, :, :]).then_inc(zeroed, 16)

            @block.vector
            def _(v):
                st = Steps(own)

                def done(ins):
                    ins.then_inc(own, 1)
                    v.wait_ge(own, st.value())

                nc.vector.memset(zeros[:, :, :], 0.0).then_inc(zero_ready, 1)
                done(nc.vector.tensor_copy(soft[:, :, :], logits[:, :, :]))
                picks = top2_steps(nc, v, done, soft, iota_e, m, "g1", exp_start, exp_done)
                for k in range(2):
                    nc.vector.tensor_copy(hotb[k][:, :, :], picks[k][0][:, :, :]).then_inc(hot_ready, 1)
                for k in range(2):
                    hot, idx, gate = picks[k]
                    v.wait_ge(place_done, k + 1)
                    done(nc.vector.tensor_copy(place[:, :, :].rearrange("p (g q) e -> p q g e", q=TPG), ps_p[k][:, :, :, :]))
                    done(nc.vector.tensor_scalar(kept[:, :, :], place[:, :, :], float(CAP), None, ALU.is_lt))
                    done(nc.vector.tensor_tensor(kept[:, :, :], kept[:, :, :], hot[:, :, :], ALU.mult))
                    if k == 0:
                        nc.vector.tensor_copy(keptb[:, :, :], kept[:, :, :]).then_inc(kept_ready, 1)
                    done(nc.vector.tensor_tensor(place[:, :, :], place[:, :, :], kept[:, :, :], ALU.mult))
                    done(nc.vector.reduce_sum(pos[:, :], place[:, :, :], AX.X))
                    done(nc.vector.reduce_sum(flat[:, :], kept[:, :, :], AX.X))
                    done(nc.vector.tensor_scalar(slot[:, :], idx[:, :], float(ET), None, ALU.mult))
                    done(nc.vector.tensor_tensor(slot[:, :], slot[:, :], pos[:, :], ALU.add))
                    done(nc.vector.tensor_tensor(slot[:, :], slot[:, :], group_base[:, :], ALU.add))
                    done(nc.vector.tensor_tensor(gates[:, k, :], gate[:, :], flat[:, :], ALU.mult))
                    done(nc.vector.tensor_tensor(pos[:, :], slot[:, :], flat[:, :], ALU.mult))
                    done(nc.vector.tensor_copy(slot_ids[:, k, :], pos[:, :]))
                    done(nc.vector.tensor_scalar(gone[:, :], flat[:, :], -DROPPED, DROPPED, ALU.mult, ALU.add))
                    done(nc.vector.tensor_tensor(slot[:, :], slot[:, :], gone[:, :], ALU.add))
                    nc.vector.tensor_copy(send_ids[:, k, :], slot[:, :]).then_inc(ids_ready, 1)
                v.wait_ge(ids_ready, 2)

            @block.scalar
            def _(a):
                a.wait_ge(exp_start, 1)
                nc.scalar.activation(soft[:, :, :], soft[:, :, :], ACT.Exp).then_inc(exp_done, 1)

            @block.tensor
            def _(pe):
                def tiles(t, q):
                    return t[:, :, :].rearrange("p (g q) e -> p q g e", q=TPG)[:, q, :, :]

                for k in range(2):
                    pe.wait_ge(hot_ready, k + 1)
                    if k == 1:
                        pe.wait_ge(kept_ready, 1)
                    for q in range(TPG):
                        terms = [(ltri, hotb[k], q)] + [(ones_bf, hotb[k], r) for r in range(q)]
                        if k == 1:
                            terms += [(ones_bf, keptb, r) for r in range(TPG)]
                        for n, (w, src, r) in enumerate(terms):
                            ins = nc.tensor.matmul(ps_p[k][:, q, :, :], w[:, :], tiles(src, r),
                                                   start=(n == 0), stop=(n == len(terms) - 1))
                    ins.then_inc(place_done, 1)

            @block.gpsimd
            def _(pool):
                pool.wait_ge(zeroed, 16 * NZ)
                for k in range(2):
                    pool.wait_ge(ids_ready, k + 1)
                    for t in range(NT):
                        nc.gpsimd.indirect_dma_start(
                            out=slots_dram, out_offset=bass.IndirectOffsetOnAxis(ap=send_ids[:, k, t:t + 1], axis=0),
                            in_=xn_all[:, t, :], in_offset=None, bounds_check=SLOTS - 1, oob_is_err=False).then_inc(sent, 16)
                pool.wait_ge(sent, 16 * 2 * NT)


def ffn1_stage(nc, w0_d, w1_d, wo_d, slots_dram, eo_dram, ident):
    NH = ET // 512
    with Pool(nc) as m:
        w0 = [m.sb(f"f1w0{i}", [P, HID]) for i in range(2)]
        w1 = [m.sb(f"f1w1{i}", [P, HID]) for i in range(2)]
        wo = [m.sb(f"f1wo{i}", [P, HC, D]) for i in range(2)]
        xe = [m.sb(f"f1xe{i}", [P, NG, D]) for i in range(2)]
        xT = m.sb("f1xT", [P, ET])
        ge = m.sb("f1ge", [P, 2, 512])
        hid = m.sb("f1hid", [P, HC, ET])
        eo = [m.sb(f"f1eo{i}", [P, NG, D]) for i in range(2)]
        ps_t = [m.ps(f"f1ps_t{i}") for i in range(2)]
        ps_a = [m.ps(f"f1ps_a{i}") for i in range(2)]
        ps_b = [m.ps(f"f1ps_b{i}") for i in range(2)]
        ps_o = [m.ps(f"f1ps_o{i}", (P, 4, D)) for i in range(2)]
        loaded = [m.sem(f"f1loaded{i}") for i in range(2)]
        xT_done, xT_ready = m.sem("f1xT_done"), m.sem("f1xT_ready")
        a_done, a_ready = m.sem("f1a_done"), m.sem("f1a_ready")
        b_done, hid_ready = m.sem("f1b_done"), m.sem("f1hid_ready")
        o_done, o_ready = m.sem("f1o_done"), m.sem("f1o_ready")
        stored = m.sem("f1stored")
        NL = 5
        UN = HC * NH
        xs_v = slots_dram.rearrange("(e g p) d -> e p g d", e=E, p=P)
        eo_v = eo_dram.rearrange("(e g p) d -> e p g d", e=E, p=P)
        full = (HC - 1) * P
        with nc.Block() as block:
            @block.sync
            def _(sp):
                def experts(r):
                    for i in range(2):
                        e = r * 2 + i
                        sp.wait_ge(o_done, up((e - 2) * 2 + 2))
                        sp.dma_start(xe[i][:, :, :], xs_v[bass.ds(e, 1)]).then_inc(loaded[i], 16)
                        sp.dma_start(w0[i][:, :], w0_d[bass.ds(e, 1)]).then_inc(loaded[i], 16)
                        sp.dma_start(w1[i][:, :], w1_d[bass.ds(e, 1)]).then_inc(loaded[i], 16)
                        sp.dma_start(wo[i][:, 0:HC - 1, :], wo_d[bass.ds(e, 1), 0:full].rearrange("a (c p) d -> p (a c) d", p=P)).then_inc(loaded[i], 16)
                        sp.dma_start(wo[i][0:HID - full, HC - 1, :], wo_d[bass.ds(e, 1), full:HID]).then_inc(loaded[i], 16)

                rolled(sp, E // 2, experts)

            @block.gpsimd
            def _(pool):
                def experts(r):
                    for i in range(2):
                        pool.wait_ge(o_ready, (r * 2 + i) * 2 + 2)
                        pool.dma_start(eo_v[bass.ds(r * 2 + i, 1)], eo[i][:, :, :]).then_inc(stored, 16)

                rolled(pool, E // 2, experts)
                pool.wait_ge(stored, 16 * E)

            @block.tensor
            def _(pe):
                def experts(r):
                    for i in range(2):
                        e = r * 2 + i
                        pe.wait_ge(loaded[i], (r + 1) * (16 * NL))
                        for g in range(NG):
                            ins = nc.tensor.transpose(ps_t[g // 4][:, (g % 4) * P:(g % 4 + 1) * P], xe[i][:, g, :], ident[:, :])
                            if g % 4 == 3:
                                ins.then_inc(xT_done, 1)
                        pe.wait_ge(xT_ready, (e + 1) * 2)
                        for u in range(UN):
                            c, half = divmod(u, NH)
                            n = hrows(c)
                            rhs = xT[:, half * 512:(half + 1) * 512]
                            if u >= 2:
                                pe.wait_ge(a_ready, up(e * UN + u - 1))
                                pe.wait_ge(hid_ready, up(e * UN + u - 1))
                            nc.tensor.matmul(ps_a[u % 2][0:n, :], w0[i][:, c * P:c * P + n], rhs, start=True, stop=True).then_inc(a_done, 1)
                            nc.tensor.matmul(ps_b[u % 2][0:n, :], w1[i][:, c * P:c * P + n], rhs, start=True, stop=True).then_inc(b_done, 1)
                        pe.wait_ge(hid_ready, (e + 1) * UN)
                        for s in range(NG):
                            for c in range(HC):
                                n = hrows(c)
                                ins = nc.tensor.matmul(ps_o[s // 4][:, s % 4, :], hid[0:n, c, s * P:(s + 1) * P], wo[i][0:n, c, :],
                                                       start=(c == 0), stop=(c == HC - 1))
                            if s % 4 == 3:
                                ins.then_inc(o_done, 1)

                rolled(pe, E // 2, experts)

            @block.scalar
            def _(a):
                def experts(r):
                    for i in range(2):
                        e = r * 2 + i
                        for k in range(2):
                            a.wait_ge(xT_done, e * 2 + k + 1)
                            nc.scalar.activation(xT[:, k * 512:(k + 1) * 512], ps_t[k][:, :], ACT.Copy).then_inc(xT_ready, 1)
                        for u in range(UN):
                            n = hrows(u // NH)
                            a.wait_ge(a_done, e * UN + u + 1)
                            if u >= 2:
                                a.wait_ge(hid_ready, up(e * UN + u - 1))
                            nc.scalar.activation(ge[0:n, u % 2, :], ps_a[u % 2][0:n, :], ACT.Gelu_apprx_tanh).then_inc(a_ready, 1)
                        for k in range(2):
                            a.wait_ge(o_done, e * 2 + k + 1)
                            if k == 0:
                                a.wait_ge(stored, r * 32)
                            nc.scalar.activation(eo[i][:, k * 4:(k + 1) * 4, :], ps_o[k][:, :, :], ACT.Copy).then_inc(o_ready, 1)

                rolled(a, E // 2, experts)

            @block.vector
            def _(v):
                def experts(r):
                    for i in range(2):
                        e = r * 2 + i
                        for u in range(UN):
                            c, half = divmod(u, NH)
                            n = hrows(c)
                            v.wait_ge(a_ready, e * UN + u + 1)
                            v.wait_ge(b_done, e * UN + u + 1)
                            nc.vector.tensor_tensor(hid[0:n, c, half * 512:(half + 1) * 512], ge[0:n, u % 2, :],
                                                    ps_b[u % 2][0:n, :], ALU.mult).then_inc(hid_ready, 1)

                rolled(v, E // 2, experts)


def combine1_stage(nc, x_all, eo_dram, gates, slot_ids):
    with Pool(nc) as m:
        rows = m.sb("c1rows", [P, 2, NT, D])
        got = m.sem("c1got")
        added = m.sem("c1added")
        with nc.Block() as block:
            @block.gpsimd
            def _(pool):
                for k in range(2):
                    for t in range(NT):
                        nc.gpsimd.indirect_dma_start(
                            out=rows[:, k, t, :], out_offset=None, in_=eo_dram,
                            in_offset=bass.IndirectOffsetOnAxis(ap=slot_ids[:, k, t:t + 1], axis=0)).then_inc(got, 16)

            @block.vector
            def _(v):
                v.wait_ge(got, 16 * 2 * NT)
                for k in range(2):
                    if k:
                        v.wait_ge(added, NT * k)
                    for t in range(NT):
                        nc.vector.scalar_tensor_tensor(out=x_all[:, t, :], in0=rows[:, k, t, :], scalar=gates[:, k, t:t + 1],
                                                       in1=x_all[:, t, :], op0=ALU.mult, op1=ALU.add).then_inc(added, 1)
                v.wait_ge(added, 2 * NT)


H1 = 16
HD = D // H1
REL = 64
NREL = 2 * REL + 1
BAND = P + REL
PITCH = BAND + P - 1
GI = 16
PARTS = 3
KS = PARTS * PARTS * HD
TAB = 2 * T - 1


def tables1_stage(nc, a, rel_k, rel_v, b_qkv, ident, bias_q, bias_k, bias_v, rel_st, tabs, pick, fold, ones_row):
    with Pool(nc) as m:
        rk = m.sb("t1rk", [HD, NREL])
        rpad = m.sb("t1rpad", [HD, 2, BAND])
        rlow = m.sb("t1rlow", [HD, 2, BAND])
        parts = [m.sb(f"t1parts{i}", [HD, 2, BAND], BF16) for i in range(PARTS)]
        rv = m.sb("t1rv", [1, TAB, HD])
        rvd = m.sb("t1rvd", [1, 2, TAB, HD])
        edge_v = m.sb("t1edge_v", [P, 2, HD])
        edge_k = m.sb("t1edge_k", [P, 2])
        bq = m.sb("t1bq", [P, 2])
        bv = m.sb("t1bv", [P, D])
        loaded = m.sem("t1loaded")
        own = m.sem("t1step")
        own_p = m.sem("t1pool_step")
        made = m.sem("t1made")
        moved = m.sem("t1moved")
        listed = m.sem("t1listed")
        zz = m.sb("t1zz", [P, H1, P - 1])
        skew = a["skew"]
        rv_dram = a["rv_table"]
        NLD = [0]
        with nc.Block() as block:
            @block.sync
            def _(sp):
                def load(dst, src):
                    sp.dma_start(dst, src, allow_slow_non_contiguous=True).then_inc(loaded, 16)
                    NLD[0] += 1

                load(rk[:, :], rel_k.rearrange("m d -> d m"))
                lo = T - 1 - REL
                load(rv[:, 0:lo, :], rel_v[0:1, :].unsqueeze(1).to_broadcast([1, lo, HD]))
                load(rv[:, lo:lo + NREL, :], rel_v.unsqueeze(0))
                load(rv[:, lo + NREL:TAB, :], rel_v[NREL - 1:NREL, :].unsqueeze(1).to_broadcast([1, TAB - lo - NREL, HD]))
                for n, row in enumerate((NREL - 1, 0)):
                    load(edge_v[:, n, :], rel_v[row, :].partition_broadcast(P))
                    for h in range(H1):
                        load(edge_k[h * HD:(h + 1) * HD, n:n + 1], rel_k[row, :].unsqueeze(1))
                load(bq[:, :], b_qkv[0:2 * D].rearrange("(w p) -> p w", p=P))
                load(bv[:, :], b_qkv[2 * D:3 * D].partition_broadcast(P))
                sp.wait_ge(made, 1)
                for n in range(2):
                    for cq in range(PARTS):
                        for ck in range(PARTS):
                            r = (cq * PARTS + ck) * HD
                            sp.dma_start(rel_st[r:r + HD, n, :], parts[ck][:, n, :]).then_inc(moved, 16)
                sp.wait_ge(made, 2)
                sp.dma_start(rv_dram.unsqueeze(0), rvd[:, :, :, :]).then_inc(listed, 16)
                sp.dma_start(skew[0][:, :, BAND:PITCH], zz[:, :, :]).then_inc(moved, 16)
                sp.dma_start(skew[1][:, :, 0:P - 1], zz[:, :, :]).then_inc(moved, 16)
                sp.wait_ge(listed, 16)
                for n, (it, jt, ig) in enumerate(TABLES):
                    first = jt * P - (it * P + ig * GI + GI - 1) + T - 1
                    flat = rv_dram[it].rearrange("t d -> (t d)")
                    src = bass.AP(flat.tensor, flat.offset + first * HD, [[HD, P], [1, P]])
                    sp.dma_start(tabs[:, n, :], src).then_inc(moved, 16)
                sp.wait_ge(moved, 16 * (2 * PARTS * PARTS + 2 + len(TABLES)))

            NLOADS = 1 + 3 + 2 * (1 + H1) + 2

            @block.vector
            def _(v):
                st = Steps(own)

                def done(ins):
                    ins.then_inc(own, 1)
                    v.wait_ge(own, st.value())

                v.wait_ge(loaded, 16 * NLOADS)
                nc.vector.memset(zz[:, :, :], 0.0)
                e = NREL - 1
                done(nc.vector.tensor_scalar(rpad[:, 0, REL - 1:BAND], rk[:, :], rk[:, e:e + 1], None, ALU.subtract))
                done(nc.vector.tensor_scalar(rpad[:, 1, 0:NREL], rk[:, :], rk[:, 0:1], None, ALU.subtract))
                done(nc.vector.tensor_copy(rpad[:, 0, 0:REL - 1], rpad[:, 0, REL - 1:REL].to_broadcast([HD, REL - 1])))
                done(nc.vector.tensor_copy(rpad[:, 1, NREL:BAND], rpad[:, 1, NREL - 1:NREL].to_broadcast([HD, REL - 1])))
                done(nc.vector.tensor_copy(parts[0][:, :, :], rpad[:, :, :]))
                done(nc.vector.tensor_tensor(rlow[:, :, :], rpad[:, :, :], parts[0][:, :, :], ALU.subtract))
                done(nc.vector.tensor_copy(parts[1][:, :, :], rlow[:, :, :]))
                done(nc.vector.tensor_tensor(rlow[:, :, :], rlow[:, :, :], parts[1][:, :, :], ALU.subtract))
                nc.vector.tensor_copy(parts[2][:, :, :], rlow[:, :, :]).then_inc(made, 1)
                for n in range(2):
                    row = TAB - 1 if n == 0 else 0
                    ins = nc.vector.tensor_tensor(rvd[:, n, :, :], rv[:, :, :], rv[:, row:row + 1, :].to_broadcast([1, TAB, HD]), ALU.subtract)
                    done(ins)
                    done(nc.vector.tensor_tensor(bias_v[:, n, :, :], bv[:, :].rearrange("p (h d) -> p h d", h=H1),
                                                 bc(edge_v[:, n, :], 1, H1), ALU.add))
                    done(nc.vector.tensor_tensor(bias_k[:, n:n + 1], bq[:, 1:2], edge_k[:, n:n + 1], ALU.add))
                done(nc.vector.tensor_scalar(bias_q[:, :], bq[:, 0:1], float(HD) ** -0.5, None, ALU.mult))
                done(nc.vector.memset(fold[:, :], 0.0))
                done(nc.vector.memset(ones_row[:, :], 1.0))
                nc.vector.tensor_reduce(fold[:, 0:HD], ident[:, :].rearrange("p (r d) -> p d r", d=HD), AX.X, ALU.add).then_inc(made, 1)
                v.wait_ge(made, 2)

            @block.gpsimd
            def _(pool):
                nc.gpsimd.memset(pick[:, :], 1.0).then_inc(own_p, 1)
                pool.wait_ge(own_p, 1)
                nc.gpsimd.affine_select(out=pick[:, :], in_=pick[:, :], compare_op=ALU.is_ge, fill=0.0,
                                        base=-(GI - 1) * HD, pattern=[[HD, GI]], channel_multiplier=1).then_inc(own_p, 1)
                pool.wait_ge(own_p, 2)
                nc.gpsimd.affine_select(out=pick[:, :], in_=pick[:, :], compare_op=ALU.is_ge, fill=0.0,
                                        base=GI * HD - 1, pattern=[[-HD, GI]], channel_multiplier=-1).then_inc(own_p, 1)
                pool.wait_ge(own_p, 3)


TABLES = [(it, jt, ig) for it in range(2) for ig in range(P // GI)
          for jt in range(2) if jt == it or (ig >= REL // GI if it == 0 else ig < REL // GI)]


def attn1_stage(nc, x_all, xnT_all, a, ident, one, bias_q, bias_k, bias_v, rel_st, tabs, pick, fold, ones_row):
    skew, parts = a["skew"], a["parts"]
    HP = H1 // 2
    S2 = 2 * B
    with Pool(nc) as m:
        w_in = m.sb("a1w_in", [P, 3, D])
        w_out = m.sb("a1w_out", [P, D])
        b_out = m.sb("a1b_out", [1, D])
        xb = m.sb("a1xb", [P, T])
        qkf = m.sb("a1qkf", [P, 3, T])
        low = m.sb("a1low", [P, 3, T])
        prt = m.sb("a1prt", [P, PARTS, 3, T], BF16)
        stk = [m.sb(f"a1stk{i}", [KS, 3, H1, T], BF16) for i in range(2)]
        vx = [m.sb(f"a1vx{i}", [P, 2, 2, H1, HD + 1]) for i in range(2)]
        Rt = m.sb("a1Rt", [P, H1, BAND])
        Sb = [m.sb(f"a1Sb{i}", [P, H1, T]) for i in range(2)]
        Pm = m.sb("a1Pm", [P, H1, T])
        nmx = [m.sb(f"a1nmx{i}", [P, H1]) for i in range(2)]
        PT = m.sb("a1PT", [P, 2, H1, P])
        X = m.sb("a1X", [P, H1, P])
        taker = m.sb("a1taker", [1, HP])
        rden = m.sb("a1rden", [P, H1])
        cx = m.sb("a1cx", [P, H1, HD])
        cT = m.sb("a1cT", [P, P])
        ps_p = m.ps("a1ps_p", (P, 2, T))
        ps_R = m.ps("a1ps_R", (P, 2, BAND))
        ps_S = [m.ps(f"a1ps_S{i}", (P, 2, T)) for i in range(2)]
        ps_T = [m.ps(f"a1ps_T{i}", (P, 2, 2, P)) for i in range(2)]
        ps_X = m.ps("a1ps_X", (P, 2, H1, GI))
        ps_c = m.ps("a1ps_c", (P, 512))
        ctx_ps = ps_c[:, 0:H1 * (HD + 1)].rearrange("p (h e) -> p h e", e=HD + 1)
        names = ("loaded xb_ready qk_done qk_ready split parts_out stacked0 stacked1 v_done v_ready R_done R_ready skew_out0 skew_out1 "
                 "skew_in0 skew_in1 S_done S_ready P_ready T_done Ta_ready Tv_ready X_done X_ready c_done cx_ready cT_done "
                 "cT_ready y_done y_added pool_step vec_step cleared")
        sm = {n: m.sem("a1" + n) for n in names.split()}
        stacked = [sm["stacked0"], sm["stacked1"]]
        skew_out = [sm["skew_out0"], sm["skew_out1"]]
        skew_in = [sm["skew_in0"], sm["skew_in1"]]
        STACK = 16 * PARTS * PARTS * 3
        HH = H1 // 2

        def steps(eng, step):
            for i in range(4):
                step(0, i)
            with eng.Fori(1, B // 2) as r:
                for i in range(4):
                    step(r, i)

        def tile_of(i):
            i %= 4
            return i % 2, i // 2

        with nc.Block() as block:
            @block.tensor
            def _(pe):
                def project_qk(n):
                    pe.wait_ge(sm["v_ready"], n if not isinstance(n, int) or n > 1 else 0)
                    pe.wait_ge(sm["qk_ready"], n)
                    for w in range(2):
                        ins = nc.tensor.matmul(ps_p[:, w, :], w_in[:, w, :], xnT_all[:, bass.ds(n * T, T)], start=True, stop=True)
                    ins.then_inc(sm["qk_done"], 1)

                def project_v(n):
                    pe.wait_ge(sm["xb_ready"], n + 1)
                    pe.wait_ge(sm["qk_ready"], n + 1 if not isinstance(n, int) or n else 2)
                    pe.wait_ge(sm["v_ready"], n)
                    for j in range(2):
                        ins = nc.tensor.matmul(ps_p[:, 0, j * D:(j + 1) * D], xb[:, j * P:(j + 1) * P], w_in[:, 2, :],
                                               start=True, stop=True)
                    ins.then_inc(sm["v_done"], 1)

                def rel_scores(s, it, par, hp):
                    pe.wait_ge(sm["R_ready"], s * HP + hp)
                    for n in range(2):
                        ins = nc.tensor.matmul(ps_R[:, n, :], stk[par][:, 0, 2 * hp + n, it * P:(it + 1) * P], rel_st[:, it, :],
                                               start=True, stop=True)
                    ins.then_inc(sm["R_done"], 1)

                def key_scores(s, it, par, hp):
                    pe.wait_ge(sm["S_ready"], up(s * H1 + 2 * hp - 2))
                    for n in range(2):
                        h = 2 * hp + n
                        ins = nc.tensor.matmul(ps_S[hp % 2][:, n, :], stk[par][:, 0, h, it * P:(it + 1) * P],
                                               stk[par][:, 1 + it, h, :], start=True, stop=True)
                    ins.then_inc(sm["S_done"], 1)

                def rel_values(s, it, k):
                    pe.wait_ge(sm["X_ready"], s * 4 + k)
                    if k == 0:
                        pe.wait_ge(sm["Ta_ready"], (s + 1) * 4)
                        pe.wait_ge(sm["Tv_ready"], (s + 1) * 4)
                    for n in range(2):
                        ig = 2 * k + n
                        use = [(t, jt) for t, (i2, jt, g2) in enumerate(TABLES) if (i2, g2) == (it, ig)]
                        for q, (t, jt) in enumerate(use):
                            ins = nc.tensor.matmul(ps_X[:, n, :, :], tabs[:, t, :], PT[:, jt, :, ig * GI:(ig + 1) * GI],
                                                   start=(q == 0), stop=(q == len(use) - 1))
                    ins.then_inc(sm["X_done"], 1)

                def context(s, b, it, par):
                    pe.wait_ge(sm["y_added"], s)
                    pe.wait_ge(sm["v_ready"], b + 1)
                    pe.wait_ge(sm["X_ready"], (s + 1) * 4)
                    for h in range(H1):
                        for jt in range(2):
                            nc.tensor.matmul(ctx_ps[:, h, :], PT[:, jt, h, :], vx[par][:, it, jt, h, :],
                                             start=(jt == 0), stop=False)
                        ins = nc.tensor.matmul(ctx_ps[:, h, :], X[:, h, :], fold[:, :], start=False, stop=True)
                    ins.then_inc(sm["c_done"], 1)

                def project_out(s):
                    pe.wait_ge(sm["cx_ready"], s + 1)
                    nc.tensor.transpose(ps_c[:, 256:384], cx[:, :, :].rearrange("p h d -> p (h d)"), ident[:, :]).then_inc(sm["cT_done"], 1)
                    pe.wait_ge(sm["cT_ready"], s + 1)
                    nc.tensor.matmul(ps_c[:, 384:512], cT[:, :], w_out[:, :], start=True, stop=False)
                    nc.tensor.matmul(ps_c[:, 384:512], ones_row[:, :], b_out[:, :], start=False, stop=True).then_inc(sm["y_done"], 1)

                def transposes(s, k):
                    pe.wait_ge(sm["P_ready"], s * H1 + 2 * k + 2)
                    pe.wait_ge(sm["Ta_ready" if k % 2 == 0 else "Tv_ready"], s * 4 + k // 2)
                    for n in range(2):
                        for jt in range(2):
                            ins = nc.tensor.transpose(ps_T[k % 2][:, n, jt, :], Pm[:, 2 * k + n, jt * P:(jt + 1) * P], ident[:, :])
                    ins.then_inc(sm["T_done"], 1)

                def step(r, i):
                    s = r * 4 + i
                    it, par = tile_of(i)
                    nit, npar = tile_of(i + 1)
                    pit, ppar = tile_of(i + 3)
                    after_first = not isinstance(r, int) or i > 0
                    prev_b = r * 2 + par - (1 if it == 0 else 0)
                    if it == 1:
                        project_qk(r * 2 + par + 2)
                        pe.wait_ge(stacked[npar], (r + 1 + (1 if i == 3 else 0)) * STACK)
                    for hp in range(HP):
                        key_scores(s, it, par, hp)
                        rel_scores(s + 1, nit, npar, hp)
                        if after_first and hp % 2 == 1:
                            rel_values(s - 1, pit, hp // 2)
                    if after_first:
                        context(s - 1, prev_b, pit, ppar)
                        project_out(s - 1)
                    if it == 0:
                        project_v(r * 2 + par + 1)
                    for k in range(HP):
                        transposes(s, k)

                pe.wait_ge(sm["loaded"], 16 * 4)
                project_qk(0)
                project_qk(1)
                project_v(0)
                pe.wait_ge(stacked[0], STACK)
                for hp in range(HP):
                    rel_scores(0, 0, 0, hp)
                steps(pe, step)
                last = 2 * B - 1
                for k in range(4):
                    rel_values(last, 1, k)
                context(last, B - 1, 1, 1)
                project_out(last)

            @block.scalar
            def _(act):
                def keep_qk(n):
                    act.wait_ge(sm["qk_done"], n + 1)
                    act.wait_ge(sm["split"], n)
                    nc.scalar.activation(qkf[:, 0, :], ps_p[:, 0, :], ACT.Identity, bias=bias_q[:, 0:1], scale=float(HD) ** -0.5)
                    nc.scalar.activation(qkf[:, 1, :], ps_p[:, 1, :], ACT.Identity, bias=bias_k[:, 0:1])
                    nc.scalar.activation(qkf[:, 2, :], ps_p[:, 1, :], ACT.Identity, bias=bias_k[:, 1:2]).then_inc(sm["qk_ready"], 1)

                def keep_R(s, hp):
                    act.wait_ge(sm["R_done"], s * HP + hp + 1)
                    if hp % (HP // 2) == 0:
                        act.wait_ge(skew_out[hp // (HP // 2)], s * 16)
                    nc.scalar.activation(Rt[:, 2 * hp:2 * hp + 2, :], ps_R[:, :, :], ACT.Copy).then_inc(sm["R_ready"], 1)

                def exponentials(s, it, hp):
                    for h in (2 * hp, 2 * hp + 1):
                        act.wait_ge(sm["S_ready"], s * H1 + h + 1)
                        nc.scalar.activation(Pm[:, h, :], Pm[:, h, :], ACT.Exp, bias=nmx[it][:, h:h + 1], scale=-1.0).then_inc(sm["P_ready"], 1)

                def keep_cT(s):
                    act.wait_ge(sm["cT_done"], s + 1)
                    nc.scalar.activation(cT[:, :], ps_c[:, 256:384], ACT.Copy).then_inc(sm["cT_ready"], 1)

                def keep_T(s, k):
                    act.wait_ge(sm["T_done"], s * HP + k + 1)
                    act.wait_ge(sm["c_done"], s)
                    nc.scalar.activation(PT[:, :, 2 * k:2 * k + 2, :].rearrange("p j h i -> p h j i"), ps_T[0][:, :, :, :],
                                         ACT.Copy).then_inc(sm["Ta_ready"], 1)

                def step(r, i):
                    s = r * 4 + i
                    it, par = tile_of(i)
                    if it == 1:
                        keep_qk(r * 2 + par + 2)
                    for hp in range(HP):
                        exponentials(s, it, hp)
                        keep_R(s + 1, hp)
                    if not isinstance(r, int) or i > 0:
                        keep_cT(s - 1)
                    for k in range(0, HP, 2):
                        keep_T(s, k)

                keep_qk(0)
                keep_qk(1)
                for hp in range(HP):
                    keep_R(0, hp)
                steps(act, step)
                keep_cT(2 * B - 1)

            @block.vector
            def _(v):
                def keep_v(n, par):
                    v.wait_ge(sm["v_done"], n + 1)
                    for q in range(2):
                        ins = nc.vector.tensor_tensor(vx[par][:, q, :, :, 0:HD],
                                                      ps_p[:, 0, :].rearrange("p (j h d) -> p j h d", j=2, h=H1),
                                                      bc(bias_v[:, q, :, :], 1, 2), ALU.add)
                    ins.then_inc(sm["v_ready"], 1)

                def add_scores(r, i, hp):
                    s = r * 4 + i
                    it, par = tile_of(i)
                    if hp == 0:
                        v.wait_ge(skew_in[it], (r * 2 + par + 1) * 32)
                    v.wait_ge(sm["S_done"], s * HP + hp + 1)
                    v.wait_ge(sm["T_done"], up((s - 1) * HP + hp + 1))
                    nc.vector.memset(taker[:, hp:hp + 1], 0.0)
                    for h in (2 * hp, 2 * hp + 1):
                        nc.vector.tensor_tensor_reduce(out=Pm[:, h, :], in0=ps_S[hp % 2][:, h % 2, :], in1=Sb[it][:, h, :],
                                                       scale=-1.0, scalar=3.0e38, op0=ALU.add, op1=ALU.min,
                                                       accum_out=nmx[it][:, h:h + 1]).then_inc(sm["S_ready"], 1)

                def pick_diagonal(s, k):
                    v.wait_ge(sm["X_done"], s * 4 + k + 1)
                    v.wait_ge(sm["c_done"], s)
                    out = X[:, :, k * 2 * GI:(k + 1) * 2 * GI].rearrange("p h (n i) -> p n h i", n=2)
                    nc.vector.tensor_tensor(out, ps_X[:, :, :, :], bc(bc(pick[:, :], 1, H1), 1, 2), ALU.mult).then_inc(sm["X_ready"], 1)

                def finish(s):
                    v.wait_ge(sm["c_done"], s + 1)
                    nc.vector.reciprocal(rden[:, :], ctx_ps[:, :, HD]).then_inc(sm["vec_step"], 1)
                    v.wait_ge(sm["vec_step"], s + 1)
                    nc.vector.tensor_tensor(cx[:, :, :], ctx_ps[:, :, 0:HD], bc(rden[:, :], 2, HD), ALU.mult).then_inc(sm["cx_ready"], 1)
                    v.wait_ge(sm["y_done"], s + 1)
                    xs = x_all[:, bass.ds(s, 1), :]
                    nc.vector.tensor_tensor(xs, xs, ps_c[:, 384:512].unsqueeze(1), ALU.add).then_inc(sm["y_added"], 1)

                def keep_T(s, k):
                    v.wait_ge(sm["T_done"], s * HP + k + 1)
                    nc.vector.tensor_copy(PT[:, :, 2 * k:2 * k + 2, :].rearrange("p j h i -> p h j i"),
                                          ps_T[1][:, :, :, :]).then_inc(sm["Tv_ready"], 1)

                def step(r, i):
                    s = r * 4 + i
                    it, par = tile_of(i)
                    after_first = not isinstance(r, int) or i > 0
                    for hp in range(HP):
                        add_scores(r, i, hp)
                        if after_first and hp % 2 == 1:
                            pick_diagonal(s - 1, hp // 2)
                    if after_first:
                        finish(s - 1)
                    if it == 0:
                        keep_v(r * 2 + par + 1, 1 - par)
                    for k in range(1, HP, 2):
                        keep_T(s, k)

                for t in vx:
                    nc.vector.memset(t[:, :, :, :, HD:HD + 1], 1.0)
                nc.vector.memset(Sb[0][:, :, BAND:T], 0.0)
                nc.vector.memset(Sb[1][:, :, 0:T - BAND], 0.0).then_inc(sm["cleared"], 1)
                v.wait_ge(sm["cleared"], 1)
                keep_v(0, 0)
                steps(v, step)
                last = 2 * B - 1
                for k in range(4):
                    pick_diagonal(last, k)
                finish(last)
                v.wait_ge(sm["y_added"], 2 * B)

            @block.gpsimd
            def _(pool):
                def copy_x(n):
                    pool.wait_ge(sm["v_done"], n)
                    nc.gpsimd.tensor_copy(xb[:, :], xnT_all[:, bass.ds(n * T, T)]).then_inc(sm["xb_ready"], 1)

                def split(n, before, done_before):
                    pool.wait_ge(sm["qk_ready"], n + 1)
                    pool.wait_ge(stacked[before], done_before)
                    src = qkf
                    for k in range(PARTS):
                        ins = nc.gpsimd.tensor_tensor(prt[:, k, :, :], src[:, :, :], bc(one[:, :].to_broadcast([P, T]), 1, 3), ALU.mult)
                        if k == PARTS - 1:
                            ins.then_inc(sm["split"], 1)
                        else:
                            ins.then_inc(sm["pool_step"], 1)
                            pool.wait_ge(sm["pool_step"], n * 4 + 2 * k + 1)
                            nc.gpsimd.tensor_tensor(low[:, :, :], src[:, :, :], prt[:, k, :, :], ALU.subtract).then_inc(sm["pool_step"], 1)
                            pool.wait_ge(sm["pool_step"], n * 4 + 2 * k + 2)
                            src = low

                def step(r, i):
                    it, par = tile_of(i)
                    if it == 0:
                        copy_x(r * 2 + par + 1)
                    else:
                        split(r * 2 + par + 2, 1 - par, (r + 1 + par) * STACK)

                pool.wait_ge(sm["loaded"], 16 * 4)
                pool.wait_ge(sm["cleared"], 1)
                copy_x(0)
                split(0, 1, 0)
                split(1, 0, STACK)
                steps(pool, step)

            @block.sync
            def _(sp):
                def stack(n, par):
                    sp.wait_ge(sm["split"], n + 1)
                    sp.dma_start(parts, prt[:, :, :, :]).then_inc(sm["parts_out"], 16)
                    sp.wait_ge(sm["parts_out"], (n + 1) * 16)
                    by_head = parts.rearrange("(h d) k w t -> d k w h t", d=HD)
                    for cq in range(PARTS):
                        for ck in range(PARTS):
                            row = (cq * PARTS + ck) * HD
                            for w in range(3):
                                sp.dma_start(stk[par][row:row + HD, w, :, :], by_head[:, cq if w == 0 else ck, w, :, :])\
                                  .then_inc(stacked[par], 16)

                def skew_tile(s, it):
                    for half in range(2):
                        hs = slice(half * HH, (half + 1) * HH)
                        sp.wait_ge(sm["R_ready"], s * HP + (half + 1) * (HP // 2))
                        c0 = 0 if it == 0 else P - 1
                        sp.dma_start(skew[it][:, hs, c0:c0 + BAND], Rt[:, hs, :]).then_inc(skew_out[half], 16)
                    for half in range(2):
                        hs = slice(half * HH, (half + 1) * HH)
                        sp.wait_ge(skew_out[half], (s + 1) * 16)
                        c0 = 0 if it == 0 else T - BAND
                        flat = skew[it].rearrange("i h c -> (i h c)")
                        sp.dma_start(Sb[it][:, hs, c0:c0 + BAND],
                                     bass.AP(flat.tensor, flat.offset + half * HH * PITCH + P - 1,
                                             [[H1 * PITCH - 1, P], [PITCH, HH], [1, BAND]])).then_inc(skew_in[it], 16)

                def step(r, i):
                    s = r * 4 + i
                    it, par = tile_of(i)
                    nit, npar = tile_of(i + 1)
                    skew_tile(s + 1, nit)
                    if it == 1:
                        stack(r * 2 + par + 2, par)

                sp.dma_start(w_in[:, :, :], a["L1_attn_W_qkv"].rearrange("d (w n) -> d w n", w=3)).then_inc(sm["loaded"], 16)
                sp.dma_start(w_out[:, :], a["L1_attn_W_out"]).then_inc(sm["loaded"], 16)
                sp.dma_start(b_out[:, :], a["L1_attn_b_out"].unsqueeze(0)).then_inc(sm["loaded"], 16)
                sp.dma_start(xnT_all[:, B * T:(B + 2) * T], xnT_all[:, 0:2 * T]).then_inc(sm["loaded"], 16)
                stack(0, 0)
                stack(1, 1)
                sp.wait_ge(sm["cleared"], 1)
                skew_tile(0, 0)
                steps(sp, step)
                sp.wait_ge(stacked[0], (B // 2 + 1) * STACK)
                sp.wait_ge(stacked[1], (B // 2 + 1) * STACK)
                sp.wait_ge(skew_in[0], (B + 1) * 32)


def store_stage(nc, x_all, out):
    with Pool(nc) as m:
        stored = m.sem("stored")
        with nc.Block() as block:
            @block.sync
            def _(sp):
                sp.dma_start(out.rearrange("b (t p) d -> p (b t) d", p=P), x_all[:, :, :]).then_inc(stored, 16)
                sp.wait_ge(stored, 16)


def program(nc, a):
    with Pool(nc) as m:
        ident = m.sb("ident", [P, P])
        mask = m.sb("mask", [P, T + P])
        expand = m.sb("expand", [E, FC0, P])
        iota_e = m.sb("iota_e", [P, E])
        ltri = m.sb("ltri", [P, P], BF16)
        ones_bf = m.sb("ones_bf", [P, P], BF16)
        group_base = m.sb("group_base", [P, NT])
        one = m.sb("one", [P, 1])
        router = m.sb("router", [P, 2, E])
        x_all = m.sb("x_all", [P, NT, D])
        xnT_all = m.sb("xnT_all", [P, (B + 2) * T])
        logits = m.sb("logits", [P, NT, E])
        constants(nc, ident, mask, expand, iota_e, ltri, ones_bf, group_base, one)
        x_dram = a["L0_attn_x"].rearrange("b (t p) d -> p (b t) d", p=P)
        load = [(x_all[:, :, :], x_dram), (router[:, 0, :], a["L0_ffn_router_w"]), (router[:, 1, :], a["L1_ffn_router_w"])]
        norm_stage(nc, x_all, None, xnT_all, ident, router[:, 0, :], logits, "n0", load)
        ffn0_stage(nc, x_all, xnT_all, logits, a["L0_ffn_router_b"], a["L0_ffn_W1"], a["L0_ffn_b1"], a["L0_ffn_W2"],
                   a["L0_ffn_b2"], ident, expand, iota_e)
        attn0_stage(nc, x_all, xnT_all, a["L0_attn_W_q"], a["L0_attn_W_k"], a["L0_attn_W_v"], a["L0_attn_W_o"], mask, one)
        gates = m.sb("gates", [P, 2, NT])
        slot_ids = m.sb("slot_ids", [P, 2, NT], U32)
        with Pool(nc) as g:
            xn_all = g.sb("xn_all", [P, NT, D])
            norm_stage(nc, x_all, xn_all, xnT_all, ident, router[:, 1, :], logits, "n1")
            gate1_stage(nc, logits, iota_e, ltri, ones_bf, xn_all, a["slots"], gates, slot_ids, group_base)
        with Pool(nc) as g:
            bias_q = g.sb("bias_q", [P, 1])
            bias_k = g.sb("bias_k", [P, 2])
            bias_v = g.sb("bias_v", [P, 2, H1, HD])
            rel_st = g.sb("rel_st", [KS, 2, BAND], BF16)
            tabs = g.sb("tabs", [P, len(TABLES), P])
            pick = g.sb("pick", [P, GI])
            fold = g.sb("fold", [P, HD + 1])
            ones_row = g.sb("ones_row", [1, P])
            tables1_stage(nc, a, a["L1_attn_rel_emb_k"], a["L1_attn_rel_emb_v"], a["L1_attn_b_qkv"], ident,
                          bias_q, bias_k, bias_v, rel_st, tabs, pick, fold, ones_row)
            attn1_stage(nc, x_all, xnT_all, a, ident, one, bias_q, bias_k, bias_v, rel_st, tabs, pick, fold, ones_row)
        ffn1_stage(nc, a["L1_ffn_w0_kernel"], a["L1_ffn_w1_kernel"], a["L1_ffn_wo_kernel"], a["slots"], a["eo"], ident)
        combine1_stage(nc, x_all, a["eo"], gates, slot_ids)
        store_stage(nc, x_all, a["out"])


NAMES = ["L0_attn_x", "L0_attn_W_q", "L0_attn_W_k", "L0_attn_W_v", "L0_attn_W_o", "L0_ffn_router_w", "L0_ffn_router_b",
         "L0_ffn_W1", "L0_ffn_b1", "L0_ffn_W2", "L0_ffn_b2", "L1_attn_W_qkv", "L1_attn_b_qkv", "L1_attn_W_out",
         "L1_attn_b_out", "L1_attn_rel_emb_k", "L1_attn_rel_emb_v", "L1_ffn_router_w", "L1_ffn_w0_kernel",
         "L1_ffn_w1_kernel", "L1_ffn_wo_kernel"]


def kernel(**inputs):
    import numpy as np
    import concourse.bacc as bacc
    from concourse.bass_utils import run_bass_kernel_spmd

    nc = bacc.Bacc("TRN2", target_bir_lowering=False, num_devices=1)
    arrays, aps = {}, {}
    for name in NAMES:
        a = np.ascontiguousarray(inputs[name])
        arrays["in_" + name] = a
        aps[name] = nc.dram_tensor("in_" + name, a.shape, mybir.dt.from_np(a.dtype), kind="ExternalInput").ap()
    aps["slots"] = nc.dram_tensor("slots", (SLOTS, D), F32, kind="Internal").ap()
    aps["eo"] = nc.dram_tensor("eo", (SLOTS, D), F32, kind="Internal").ap()
    aps["skew"] = [nc.dram_tensor(f"skew{i}", (P, H1, PITCH), F32, kind="Internal").ap() for i in range(2)]
    aps["parts"] = nc.dram_tensor("parts", (P, PARTS, 3, T), BF16, kind="Internal").ap()
    aps["rv_table"] = nc.dram_tensor("rv_table", (2, TAB, HD), F32, kind="Internal").ap()
    aps["out"] = nc.dram_tensor("out", (B, T, D), F32, kind="ExternalOutput").ap()
    program(nc, aps)
    r = run_bass_kernel_spmd(nc, [arrays], core_ids=[0])
    return r.results[0]["out"]
```

```python
import concourse.bass as bass
from concourse import mybir
from contextlib import ExitStack

F32 = mybir.dt.float32
BF16 = mybir.dt.bfloat16
U32 = mybir.dt.uint32
I32 = mybir.dt.int32
ALU = mybir.AluOpType
ACT = mybir.ActivationFunctionType
AX = mybir.AxisListType

P = 128
B, T, D = 16, 256, 128
NT = B * T // P
TPG = 4
NG = NT // TPG
GT = TPG * P
EPS = 1e-5
H0, DK = 16, 64
PAIRS = H0 // 2
E = 8
FF0 = 512
FC0 = FF0 // P
EPC = P // (FF0 // E)


class Pool:

    def __init__(self, nc):
        self.nc, self.ctx = nc, ExitStack()

    def __enter__(self):
        self.ctx.__enter__()
        return self

    def __exit__(self, *a):
        return self.ctx.__exit__(*a)

    def sb(self, name, shape, dt=F32):
        return self.ctx.enter_context(self.nc.sbuf_tensor(name, shape, dt))

    def ps(self, name, shape=(P, 512), dt=F32):
        return self.ctx.enter_context(self.nc.psum_tensor(name, list(shape), dt))

    def sem(self, name):
        return self.ctx.enter_context(self.nc.semaphore(name))


class Steps:

    def __init__(self, sem, base=0):
        self.sem, self.base, self.n = sem, base, 0

    def value(self):
        self.n += 1
        return self.base + self.n


def up(n):
    return max(n, 0) if isinstance(n, int) else n


def rolled(eng, n, body):
    body(0)
    with eng.Fori(1, n) as i:
        body(i)


def constants(nc, ident, mask, expand, iota_e, ltri, ones_bf, group_base, one):
    with Pool(nc) as m:
        cs = m.sem("const_step")
        io = m.sb("iota_i", [P, E], I32)
        io_g = m.sb("iota_g", [P, NT], I32)
        with nc.Block() as block:
            @block.gpsimd
            def _(pool):
                nc.gpsimd.memset(ident[:, :], 0.0).then_inc(cs, 1)
                nc.gpsimd.memset(mask[:, :], 1.0).then_inc(cs, 1)
                nc.gpsimd.memset(expand[:, :, :], 1.0).then_inc(cs, 1)
                nc.gpsimd.memset(ltri[:, :], 1.0).then_inc(cs, 1)
                nc.gpsimd.memset(ones_bf[:, :], 1.0).then_inc(cs, 1)
                nc.gpsimd.memset(one[:, :], 1.0).then_inc(cs, 1)
                nc.gpsimd.iota(io[:, :], pattern=[[1, E]], base=0, channel_multiplier=0).then_inc(cs, 1)
                nc.gpsimd.iota(io_g[:, :], pattern=[[CAP, NG], [0, TPG]], base=0, channel_multiplier=0).then_inc(cs, 1)
                pool.wait_ge(cs, 8)
                nc.gpsimd.tensor_copy(group_base[:, :], io_g[:, :]).then_inc(cs, 1)
                nc.gpsimd.affine_select(out=ident[:, :], in_=ident[:, :], compare_op=ALU.not_equal, fill=1.0,
                                        base=0, pattern=[[-1, P]], channel_multiplier=1).then_inc(cs, 1)
                nc.gpsimd.affine_select(out=mask[:, 0:T], in_=mask[:, 0:T], compare_op=ALU.is_ge, fill=0.0,
                                        base=0, pattern=[[1, T]], channel_multiplier=-1).then_inc(cs, 1)
                nc.gpsimd.affine_select(out=mask[:, T:T + P], in_=mask[:, T:T + P], compare_op=ALU.is_ge, fill=0.0,
                                        base=0, pattern=[[1, P]], channel_multiplier=-1).then_inc(cs, 1)
                nc.gpsimd.affine_select(out=ltri[:, :], in_=ltri[:, :], compare_op=ALU.is_gt, fill=0.0,
                                        base=0, pattern=[[1, P]], channel_multiplier=-1).then_inc(cs, 1)
                w = FF0 // E
                nc.gpsimd.affine_select(out=expand[:, :, :], in_=expand[:, :, :], compare_op=ALU.is_ge, fill=0.0,
                                        base=0, pattern=[[P, FC0], [1, P]], channel_multiplier=-w).then_inc(cs, 1)
                nc.gpsimd.tensor_copy(iota_e[:, :], io[:, :]).then_inc(cs, 1)
                pool.wait_ge(cs, 15)
                nc.gpsimd.affine_select(out=expand[:, :, :], in_=expand[:, :, :], compare_op=ALU.is_ge, fill=0.0,
                                        base=w - 1, pattern=[[-P, FC0], [-1, P]], channel_multiplier=w).then_inc(cs, 1)
                pool.wait_ge(cs, 16)


def norm_stage(nc, x_all, xn_all, xnT_all, ident, router, logits, tag, load=None):
    with Pool(nc) as m:
        stats = m.sb(tag + "stats", [P, NT, 6])
        mean = m.sb(tag + "mean", [P, NT])
        mean2 = m.sb(tag + "mean2", [P, NT])
        rstd = m.sb(tag + "rstd", [P, NT])
        xn = [m.sb(f"{tag}xn{i}", [P, TPG, D]) for i in range(2)]
        xT = [m.sb(f"{tag}xT{i}", [P, GT]) for i in range(2)]
        ps_t = [m.ps(f"{tag}ps_t{i}") for i in range(2)]
        ps_l = [m.ps(f"{tag}ps_l{i}", (P, TPG, E)) for i in range(2)]
        loaded = m.sem(tag + "loaded")
        own = m.sem(tag + "vec_step")
        var_ready = m.sem(tag + "var_ready")
        std_ready = m.sem(tag + "std_ready")
        xn_ready = m.sem(tag + "xn_ready")
        xn_kept = m.sem(tag + "xn_kept")
        xT_done = m.sem(tag + "xT_done")
        xT_ready = m.sem(tag + "xT_ready")
        xT_kept = m.sem(tag + "xT_kept")
        lg_done = m.sem(tag + "lg_done")
        lg_kept = m.sem(tag + "lg_kept")
        with nc.Block() as block:
            @block.sync
            def _(sp):
                if load is not None:
                    for dst, src in load:
                        sp.dma_start(dst, src).then_inc(loaded, 16)

            @block.vector
            def _(v):
                st = Steps(own, NT)

                def done(ins):
                    ins.then_inc(own, 1)
                    v.wait_ge(own, st.value())

                if load is not None:
                    v.wait_ge(loaded, 16 * len(load))
                with v.Fori(0, NT // 8) as r:
                    for i in range(8):
                        t = r * 8 + i
                        nc.vector.bn_stats(stats[:, bass.ds(t, 1), :], x_all[:, bass.ds(t, 1), :]).then_inc(own, 1)
                v.wait_ge(own, NT)
                done(nc.vector.tensor_tensor(mean[:, :], stats[:, :, 1], stats[:, :, 4], ALU.subtract))
                done(nc.vector.tensor_tensor(rstd[:, :], mean[:, :], mean[:, :], ALU.mult))
                done(nc.vector.tensor_scalar(rstd[:, :], rstd[:, :], 0.25, EPS, ALU.mult, ALU.add))
                done(nc.vector.tensor_tensor(mean[:, :], stats[:, :, 2], stats[:, :, 5], ALU.add))
                done(nc.vector.tensor_scalar(mean[:, :], mean[:, :], 1.0 / D, None, ALU.mult))
                nc.vector.tensor_tensor(rstd[:, :], rstd[:, :], mean[:, :], ALU.add).then_inc(var_ready, 1)
                done(nc.vector.tensor_tensor(mean2[:, :], stats[:, :, 1], stats[:, :, 4], ALU.add))
                done(nc.vector.tensor_scalar(mean2[:, :], mean2[:, :], 0.5, None, ALU.mult))
                v.wait_ge(std_ready, 1)
                done(nc.vector.reciprocal(rstd[:, :], rstd[:, :]))
                def group(half):
                    g = half * 2
                    for i in range(2):
                        v.wait_ge(xT_done, g)
                        if xn_all is not None:
                            v.wait_ge(xn_kept, g)
                        for j in range(TPG):
                            t = (g + i) * TPG + j
                            ins = nc.vector.tensor_scalar(xn[i][:, j, :], x_all[:, bass.ds(t, 1), :],
                                                          mean2[:, bass.ds(t, 1)], rstd[:, bass.ds(t, 1)],
                                                          ALU.subtract, ALU.mult)
                        ins.then_inc(xn_ready, 1)
                    for i in range(2):
                        v.wait_ge(lg_done, g + i + 1)
                        nc.vector.tensor_copy(logits[:, bass.ds((g + i) * TPG, TPG), :], ps_l[i][:, :, :]).then_inc(lg_kept, 1)

                rolled(v, NG // 2, group)
                v.wait_ge(lg_kept, NG)

            @block.scalar
            def _(a):
                a.wait_ge(var_ready, 1)
                nc.scalar.activation(rstd[:, :], rstd[:, :], ACT.Sqrt).then_inc(std_ready, 1)
                def group(half):
                    g = half * 2
                    for i in range(2):
                        a.wait_ge(xT_done, g + i + 1)
                        a.wait_ge(xT_kept, g)
                        nc.scalar.activation(xT[i][:, :], ps_t[i][:, :], ACT.Copy).then_inc(xT_ready, 1)

                rolled(a, NG // 2, group)
                a.wait_ge(xT_ready, NG)

            @block.tensor
            def _(pe):
                if load is not None:
                    pe.wait_ge(loaded, 16 * len(load))
                def group(half):
                    g = half * 2
                    for i in range(2):
                        pe.wait_ge(xn_ready, g + i + 1)
                        for j in range(TPG):
                            ins = nc.tensor.transpose(ps_t[i][:, j * P:(j + 1) * P], xn[i][:, j, :], ident[:, :])
                        ins.then_inc(xT_done, 1)
                    for i in range(2):
                        pe.wait_ge(xT_ready, g + i + 1)
                        pe.wait_ge(lg_kept, g)
                        for j in range(TPG):
                            ins = nc.tensor.matmul(ps_l[i][:, j, :], xT[i][:, j * P:(j + 1) * P], router[:, :],
                                                   start=True, stop=True)
                        ins.then_inc(lg_done, 1)

                rolled(pe, NG // 2, group)

            @block.gpsimd
            def _(pool):
                def group(half):
                    g = half * 2
                    for i in range(2):
                        if xn_all is not None:
                            pool.wait_ge(xn_ready, g + i + 1)
                            nc.gpsimd.tensor_copy(xn_all[:, bass.ds((g + i) * TPG, TPG), :], xn[i][:, :, :]).then_inc(xn_kept, 1)
                    for i in range(2):
                        pool.wait_ge(xT_ready, g + i + 1)
                        nc.gpsimd.tensor_copy(xnT_all[:, bass.ds((g + i) * GT, GT)], xT[i][:, :]).then_inc(xT_kept, 1)

                rolled(pool, NG // 2, group)
                pool.wait_ge(xT_kept, NG)
                if xn_all is not None:
                    pool.wait_ge(xn_kept, NG)


def bc(ap, axis, n):
    shape = list(ap.shape)
    shape.insert(axis, n)
    return ap.unsqueeze(axis).to_broadcast(shape)


def top2_steps(nc, v, done, soft, iota_e, m, tag, exp_start, exp_done):
    shape = [P, NT, E]
    mx = m.sb(tag + "mx", [P, NT])
    done(nc.vector.reduce_max(mx[:, :], soft[:, :, :], AX.X))
    nc.vector.tensor_tensor(soft[:, :, :], soft[:, :, :], bc(mx[:, :], 2, E), ALU.subtract).then_inc(exp_start, 1)
    v.wait_ge(exp_done, 1)
    done(nc.vector.reduce_sum(mx[:, :], soft[:, :, :], AX.X))
    done(nc.vector.reciprocal(mx[:, :], mx[:, :]))
    done(nc.vector.tensor_tensor(soft[:, :, :], soft[:, :, :], bc(mx[:, :], 2, E), ALU.mult))
    picks = []
    rest = soft
    for k in range(2):
        gate = m.sb(f"{tag}gate{k}", [P, NT])
        idx = m.sb(f"{tag}idx{k}", [P, NT])
        hot = m.sb(f"{tag}hot{k}", shape)
        cand = m.sb(f"{tag}cand{k}", shape)
        done(nc.vector.reduce_max(gate[:, :], rest[:, :, :], AX.X))
        done(nc.vector.tensor_tensor(hot[:, :, :], rest[:, :, :], bc(gate[:, :], 2, E), ALU.is_equal))
        done(nc.vector.tensor_scalar(cand[:, :, :], hot[:, :, :], -16.0, None, ALU.mult))
        done(nc.vector.tensor_tensor(cand[:, :, :], cand[:, :, :], bc(iota_e[:, :], 1, NT), ALU.add))
        done(nc.vector.tensor_reduce(idx[:, :], cand[:, :, :], AX.X, ALU.min))
        done(nc.vector.tensor_tensor(hot[:, :, :], cand[:, :, :], bc(idx[:, :], 2, E), ALU.is_equal))
        done(nc.vector.tensor_scalar(idx[:, :], idx[:, :], 16.0, None, ALU.add))
        picks.append((hot, idx, gate))
        if k == 0:
            rest = m.sb(tag + "rest", shape)
            done(nc.vector.tensor_tensor(cand[:, :, :], soft[:, :, :], hot[:, :, :], ALU.mult))
            done(nc.vector.tensor_tensor(rest[:, :, :], soft[:, :, :], cand[:, :, :], ALU.subtract))
    return picks


def ffn0_stage(nc, x_all, xnT_all, logits, router_b, W1, b1, W2, b2, ident, expand, iota_e):
    with Pool(nc) as m:
        w1 = m.sb("f0w1", [P, FC0, P])
        w2 = m.sb("f0w2", [P, FC0, D])
        b1c = m.sb("f0b1", [P, FC0])
        b2s = m.sb("f0b2", [E, D])
        rb = m.sb("f0rb", [P, E])
        wt = m.sb("f0wt", [P, NT, E])
        wtg = m.sb("f0wtg", [P, TPG, E])
        wT = m.sb("f0wT", [E, GT])
        h = m.sb("f0h", [P, FC0, GT])
        hw = m.sb("f0hw", [P, FC0, GT])
        den = m.sb("f0den", [P, NT])
        ps_h = [m.ps(f"f0ps_h{i}") for i in range(FC0)]
        ps_w = [m.ps(f"f0ps_w{i}") for i in range(2)]
        ps_t = m.ps("f0ps_t")
        ps_y = m.ps("f0ps_y", (P, TPG, D))
        loaded = m.sem("f0loaded")
        own = m.sem("f0vec_step")
        exp_start = m.sem("f0exp_start")
        exp_done = m.sem("f0exp_done")
        h_done = m.sem("f0h_done")
        h_ready = m.sem("f0h_ready")
        wtg_ready = m.sem("f0wtg_ready")
        wT_done = m.sem("f0wT_done")
        wT_ready = m.sem("f0wT_ready")
        w_done = m.sem("f0w_done")
        hw_ready = m.sem("f0hw_ready")
        y_done = m.sem("f0y_done")
        y_added = m.sem("f0y_added")
        NL = 6
        with nc.Block() as block:
            @block.sync
            def _(sp):
                sp.dma_start(rb[:, :], router_b.partition_broadcast(P)).then_inc(loaded, 16)
                for e in range(E):
                    c, o = divmod(e * (FF0 // E), P)
                    if e == 0:
                        sp.dma_start(w1[:, :, :].rearrange("p c (e f) -> p (c e) f", e=EPC),
                                     W1.rearrange("e d f -> d e f")).then_inc(loaded, 16)
                sp.dma_start(w2[:, :, :], W2.rearrange("e f d -> (e f) d").rearrange("(c p) d -> p c d", p=P)).then_inc(loaded, 16)
                sp.dma_start(b1c[:, :], b1.rearrange("(c e) f -> (e f) c", e=EPC), allow_slow_non_contiguous=True).then_inc(loaded, 16)
                sp.dma_start(b2s[:, :], b2).then_inc(loaded, 16)

            @block.vector
            def _(v):
                st = Steps(own)

                def done(ins):
                    ins.then_inc(own, 1)
                    v.wait_ge(own, st.value())

                v.wait_ge(loaded, 16 * 5)
                done(nc.vector.tensor_tensor(wt[:, :, :], logits[:, :, :], bc(rb[:, :], 1, NT), ALU.add))
                (hot1, _, g1), (hot2, _, g2) = top2_steps(nc, v, done, wt, iota_e, m, "f0", exp_start, exp_done)
                done(nc.vector.tensor_tensor(den[:, :], g1[:, :], g2[:, :], ALU.add))
                done(nc.vector.reciprocal(den[:, :], den[:, :]))
                done(nc.vector.tensor_tensor(g1[:, :], g1[:, :], den[:, :], ALU.mult))
                done(nc.vector.tensor_tensor(g2[:, :], g2[:, :], den[:, :], ALU.mult))
                done(nc.vector.tensor_tensor(hot1[:, :, :], hot1[:, :, :], bc(g1[:, :], 2, E), ALU.mult))
                done(nc.vector.tensor_tensor(hot2[:, :, :], hot2[:, :, :], bc(g2[:, :], 2, E), ALU.mult))
                done(nc.vector.tensor_tensor(wt[:, :, :], hot1[:, :, :], hot2[:, :, :], ALU.add))
                def group(g):
                    v.wait_ge(wT_done, g)
                    nc.vector.tensor_copy(wtg[:, :, :], wt[:, bass.ds(g * TPG, TPG), :]).then_inc(wtg_ready, 1)
                    for c in range(FC0):
                        v.wait_ge(h_ready, g * FC0 + c + 1)
                        v.wait_ge(w_done, g * FC0 + c + 1)
                        nc.vector.tensor_tensor(hw[:, c, :], h[:, c, :], ps_w[c % 2][:, :], ALU.mult).then_inc(hw_ready, 1)
                    v.wait_ge(y_done, g + 1)
                    xs = x_all[:, bass.ds(g * TPG, TPG), :]
                    nc.vector.tensor_tensor(xs, xs, ps_y[:, :, :], ALU.add).then_inc(y_added, 1)

                rolled(v, NG, group)
                v.wait_ge(y_added, NG)

            @block.scalar
            def _(a):
                a.wait_ge(exp_start, 1)
                nc.scalar.activation(wt[:, :, :], wt[:, :, :], ACT.Exp).then_inc(exp_done, 1)
                a.wait_ge(loaded, 16 * 5)
                def group(g):
                    a.wait_ge(wT_done, g + 1)
                    nc.scalar.activation(wT[:, :], ps_t[0:E, :], ACT.Copy).then_inc(wT_ready, 1)
                    for c in range(FC0):
                        a.wait_ge(h_done, g * FC0 + c + 1)
                        a.wait_ge(hw_ready, g * FC0)
                        nc.scalar.activation(h[:, c, :], ps_h[c][:, :], ACT.Gelu, bias=b1c[:, c:c + 1]).then_inc(h_ready, 1)

                rolled(a, NG, group)

            @block.tensor
            def _(pe):
                pe.wait_ge(loaded, 16 * 5)
                def group(g):
                    pe.wait_ge(wtg_ready, g + 1)
                    for j in range(TPG):
                        ins = nc.tensor.transpose(ps_t[0:E, j * P:(j + 1) * P], wtg[:, j, :], ident[:, :])
                    ins.then_inc(wT_done, 1)
                    for c in range(FC0):
                        pe.wait_ge(h_ready, g * FC0)
                        nc.tensor.matmul(ps_h[c][:, :], w1[:, c, :], xnT_all[:, bass.ds(g * GT, GT)],
                                         start=True, stop=True).then_inc(h_done, 1)
                    pe.wait_ge(wT_ready, g + 1)
                    for c in range(FC0):
                        if c >= 2:
                            pe.wait_ge(hw_ready, up(g * FC0 + c - 1))
                        nc.tensor.matmul(ps_w[c % 2][:, :], expand[:, c, :], wT[:, :], start=True, stop=True).then_inc(w_done, 1)
                    pe.wait_ge(hw_ready, (g + 1) * FC0)
                    pe.wait_ge(y_added, g)
                    for j in range(TPG):
                        for c in range(FC0):
                            nc.tensor.matmul(ps_y[:, j, :], hw[:, c, j * P:(j + 1) * P], w2[:, c, :],
                                             start=(c == 0), stop=False)
                        ins = nc.tensor.matmul(ps_y[:, j, :], wT[:, j * P:(j + 1) * P], b2s[:, :], start=False, stop=True)
                    ins.then_inc(y_done, 1)

                rolled(pe, NG, group)


def attn0_stage(nc, x_all, xnT_all, Wq, Wk, Wv, Wo, mask, one):
    HB = T + P
    with Pool(nc) as m:
        w_in = m.sb("a0w_in", [P, 3, H0 * DK])
        w_out = m.sb("a0w_out", [P, PAIRS, D])
        w_qk = m.sb("a0w_qk", [P, 2, P])
        w_v = m.sb("a0w_v", [P, P])
        xb = m.sb("a0xb", [P, T])
        qk = m.sb("a0qk", [P, 2, T])
        vv = m.sb("a0v", [P, 2, P])
        AT = [m.sb(f"a0AT{i}", [P, HB]) for i in range(2)]
        MT = [m.sb(f"a0MT{i}", [P, HB]) for i in range(2)]
        oT = m.sb("a0oT", [P, PAIRS, T])
        ps_qk = m.ps("a0ps_qk", (P, 2, T))
        ps_v = m.ps("a0ps_v", (P, 2, P))
        ps_A = [m.ps(f"a0ps_A{i}") for i in range(2)]
        ps_M = [m.ps(f"a0ps_M{i}") for i in range(2)]
        ps_o = m.ps("a0ps_o")
        ps_y = m.ps("a0ps_y", (P, 2, D))
        loaded = m.sem("a0loaded")
        xb_ready = m.sem("a0xb_ready")
        wqk_ready = m.sem("a0wqk_ready")
        wv_ready = m.sem("a0wv_ready")
        qk_done, qk_ready = m.sem("a0qk_done"), m.sem("a0qk_ready")
        v_done, v_ready = m.sem("a0v_done"), m.sem("a0v_ready")
        A_done, A_ready = m.sem("a0A_done"), m.sem("a0A_ready")
        M_done, M_ready = m.sem("a0M_done"), m.sem("a0M_ready")
        o_done, o_ready = m.sem("a0o_done"), m.sem("a0o_ready")
        y_done, y_added = m.sem("a0y_done"), m.sem("a0y_added")
        with nc.Block() as block:
            @block.sync
            def _(sp):
                for i, w in enumerate((Wq, Wk, Wv)):
                    sp.dma_start(w_in[:, i, :], w).then_inc(loaded, 16)
                sp.dma_start(w_out[:, :, :], Wo.rearrange("(c p) d -> p c d", p=P)).then_inc(loaded, 16)

            @block.gpsimd
            def _(pool):
                def copy(dst, src):
                    return nc.gpsimd.tensor_tensor(dst, src, one[:, :].to_broadcast([P, P]) if len(dst.shape) == 2
                                                   else bc(one[:, :].to_broadcast([P, P]), 1, 2), ALU.mult)

                pool.wait_ge(loaded, 16 * 4)
                def batch(b):
                    pool.wait_ge(v_done, b * PAIRS)
                    nc.gpsimd.tensor_copy(xb[:, :], xnT_all[:, bass.ds(b * T, T)]).then_inc(xb_ready, 1)

                    def pair(p):
                        pool.wait_ge(qk_done, b * PAIRS + p)
                        copy(w_qk[:, :, :], w_in[:, 0:2, bass.ds(p * P, P)]).then_inc(wqk_ready, 1)
                        pool.wait_ge(v_done, b * PAIRS + p)
                        copy(w_v[:, :], w_in[:, 2, bass.ds(p * P, P)]).then_inc(wv_ready, 1)

                    rolled(pool, PAIRS, pair)

                rolled(pool, B, batch)

            @block.tensor
            def _(pe):
                def project_qk(b, p):
                    pe.wait_ge(wqk_ready, b * PAIRS + p + 1)
                    for i in range(2):
                        ins = nc.tensor.matmul(ps_qk[:, i, :], w_qk[:, i, :], xnT_all[:, bass.ds(b * T, T)],
                                               start=True, stop=True)
                    ins.then_inc(qk_done, 1)

                def scores(b, p):
                    pe.wait_ge(qk_ready, b * PAIRS + p + 1)
                    for h in range(2):
                        r = slice(h * DK, (h + 1) * DK)
                        nc.tensor.matmul(ps_A[h][:, 0:T], qk[r, 1, 0:P], qk[r, 0, :], start=True, stop=True)
                        nc.tensor.matmul(ps_A[h][:, T:HB], qk[r, 1, P:T], qk[r, 0, P:T],
                                         start=True, stop=True).then_inc(A_done, 1)

                def values(b, p):
                    pe.wait_ge(wv_ready, b * PAIRS + p + 1)
                    pe.wait_ge(xb_ready, b + 1)
                    for j in range(2):
                        ins = nc.tensor.matmul(ps_v[:, j, :], xb[:, j * P:(j + 1) * P], w_v[:, :], start=True, stop=True)
                    ins.then_inc(v_done, 1)

                def squares(b, p):
                    for h in range(2):
                        pe.wait_ge(A_ready, (b * PAIRS + p) * 2 + h + 1)
                        nc.tensor.matmul(ps_M[h][:, 0:T], AT[h][:, 0:P], AT[h][:, 0:T], start=True, stop=True)
                        nc.tensor.matmul(ps_M[h][:, T:HB], AT[h][:, P:T], AT[h][:, P:T], start=True, stop=False)
                        nc.tensor.matmul(ps_M[h][:, T:HB], AT[h][:, T:HB], AT[h][:, T:HB],
                                         start=False, stop=True).then_inc(M_done, 1)

                def outputs(b, p):
                    pe.wait_ge(o_ready, b * PAIRS + p + 1)
                    pe.wait_ge(v_ready, b * PAIRS + p + 1)
                    rows = [slice(h * DK, (h + 1) * DK) for h in range(2)]
                    for h, r in enumerate(rows):
                        pe.wait_ge(M_ready, (b * PAIRS + p) * 2 + h + 1)
                        nc.tensor.matmul(ps_o[r, 0:T], vv[:, 0, r], MT[h][:, 0:T], start=True, stop=False)
                    for h, r in enumerate(rows):
                        ins = nc.tensor.matmul(ps_o[r, P:T], vv[:, 1, r], MT[h][:, T:HB], start=False, stop=True)
                    ins.then_inc(o_done, 1)

                pe.wait_ge(loaded, 16 * 4)
                def batch(b):
                    project_qk(b, 0)
                    scores(b, 0)
                    project_qk(b, 1)
                    values(b, 0)
                    squares(b, 0)
                    with pe.Fori(1, PAIRS - 1) as p:
                        scores(b, p)
                        project_qk(b, p + 1)
                        outputs(b, p - 1)
                        values(b, p)
                        squares(b, p)
                    last = PAIRS - 1
                    scores(b, last)
                    outputs(b, last - 1)
                    values(b, last)
                    squares(b, last)
                    outputs(b, last)
                    pe.wait_ge(y_added, b)
                    for j in range(2):
                        for p in range(PAIRS):
                            if j == 0 and p in (0, last):
                                pe.wait_ge(o_ready, b * PAIRS + (last if p == 0 else PAIRS) + 1)
                            ins = nc.tensor.matmul(ps_y[:, j, :], oT[:, p, j * P:(j + 1) * P], w_out[:, p, :],
                                                   start=(p == 0), stop=(p == last))
                    ins.then_inc(y_done, 1)

                rolled(pe, B, batch)

            @block.scalar
            def _(a):
                nc.scalar.sem_inc(o_ready, 1)

                def keep_qk(b, p):
                    a.wait_ge(qk_done, b * PAIRS + p + 1)
                    nc.scalar.activation(qk[:, :, :], ps_qk[:, :, :], ACT.Copy).then_inc(qk_ready, 1)

                def keep_v(b, p):
                    a.wait_ge(v_done, b * PAIRS + p + 1)
                    nc.scalar.activation(vv[:, :, :], ps_v[:, :, :], ACT.Copy).then_inc(v_ready, 1)

                def keep_o(b, p):
                    a.wait_ge(o_done, b * PAIRS + p + 1)
                    a.wait_ge(y_done, b)
                    nc.scalar.activation(oT[:, bass.ds(p, 1), :], ps_o[:, 0:T], ACT.Copy).then_inc(o_ready, 1)

                def batch(b):
                    keep_qk(b, 0)
                    keep_qk(b, 1)
                    keep_v(b, 0)
                    with a.Fori(1, PAIRS - 1) as p:
                        keep_qk(b, p + 1)
                        keep_o(b, p - 1)
                        keep_v(b, p)
                    keep_o(b, PAIRS - 2)
                    keep_v(b, PAIRS - 1)
                    keep_o(b, PAIRS - 1)

                rolled(a, B, batch)

            @block.vector
            def _(v):
                def batch(b):
                    with v.Fori(0, PAIRS) as p:
                        for h in range(2):
                            v.wait_ge(A_done, (b * PAIRS + p) * 2 + h + 1)
                            nc.vector.tensor_tensor(AT[h][:, :], ps_A[h][:, 0:HB], mask[:, :], ALU.mult).then_inc(A_ready, 1)
                        for h in range(2):
                            v.wait_ge(M_done, (b * PAIRS + p) * 2 + h + 1)
                            nc.vector.tensor_tensor(MT[h][:, :], ps_M[h][:, 0:HB], mask[:, :], ALU.mult).then_inc(M_ready, 1)
                    v.wait_ge(y_done, b + 1)
                    xs = x_all[:, bass.ds(b * 2, 2), :]
                    nc.vector.tensor_tensor(xs, xs, ps_y[:, :, :], ALU.add).then_inc(y_added, 1)

                rolled(v, B, batch)
                v.wait_ge(y_added, B)


CAP = (int(2.0 * GT / E) + 3) // 4 * 4
HID = int(8.0 * D) * 2 // 3
HID = HID + (8 - HID) % 8
HC = -(-HID // P)
SLOTS = E * NG * CAP
ET = NG * CAP
DROPPED = float(2 * SLOTS)


def hrows(c):
    return min(P, HID - c * P)


def gate1_stage(nc, logits, iota_e, ltri, ones_bf, slots_dram, gates, slot_ids, send_ids, group_base):
    with Pool(nc) as m:
        soft = m.sb("g1soft", [P, NT, E])
        hotb = [m.sb(f"g1hotb{k}", [P, NT, E], BF16) for k in range(2)]
        keptb = m.sb("g1keptb", [P, NT, E], BF16)
        kept = m.sb("g1kept", [P, NT, E])
        place = m.sb("g1place", [P, NT, E])
        pos = m.sb("g1pos", [P, NT])
        flat = m.sb("g1flat", [P, NT])
        slot = m.sb("g1slot", [P, NT])
        gone = m.sb("g1gone", [P, NT])
        zeros = m.sb("g1zeros", [P, SLOTS // P, 16])
        ps_p = [m.ps(f"g1ps_p{k}", (P, TPG, NG, E)) for k in range(2)]
        own = m.sem("g1vec_step")
        exp_start, exp_done = m.sem("g1exp_start"), m.sem("g1exp_done")
        hot_ready, kept_ready = m.sem("g1hot_ready"), m.sem("g1kept_ready")
        place_done = m.sem("g1place_done")
        zero_ready, zeroed = m.sem("g1zero_ready"), m.sem("g1zeroed")
        ids_ready = m.sem("g1ids_ready")
        NZ = D // 16
        with nc.Block() as block:
            @block.sync
            def _(sp):
                sp.wait_ge(zero_ready, 1)
                for z in range(NZ):
                    sp.dma_start(slots_dram.rearrange("(p s) d -> p s d", p=P)[:, :, z * 16:(z + 1) * 16],
                                 zeros[:, :, :]).then_inc(zeroed, 16)
                sp.wait_ge(zeroed, 16 * NZ)

            @block.vector
            def _(v):
                st = Steps(own)

                def done(ins):
                    ins.then_inc(own, 1)
                    v.wait_ge(own, st.value())

                nc.vector.memset(zeros[:, :, :], 0.0).then_inc(zero_ready, 1)
                done(nc.vector.tensor_copy(soft[:, :, :], logits[:, :, :]))
                picks = top2_steps(nc, v, done, soft, iota_e, m, "g1", exp_start, exp_done)
                for k in range(2):
                    nc.vector.tensor_copy(hotb[k][:, :, :], picks[k][0][:, :, :]).then_inc(hot_ready, 1)
                for k in range(2):
                    hot, idx, gate = picks[k]
                    v.wait_ge(place_done, k + 1)
                    done(nc.vector.tensor_copy(place[:, :, :].rearrange("p (g q) e -> p q g e", q=TPG), ps_p[k][:, :, :, :]))
                    done(nc.vector.tensor_scalar(kept[:, :, :], place[:, :, :], float(CAP), None, ALU.is_lt))
                    done(nc.vector.tensor_tensor(kept[:, :, :], kept[:, :, :], hot[:, :, :], ALU.mult))
                    if k == 0:
                        nc.vector.tensor_copy(keptb[:, :, :], kept[:, :, :]).then_inc(kept_ready, 1)
                    done(nc.vector.tensor_tensor(place[:, :, :], place[:, :, :], kept[:, :, :], ALU.mult))
                    done(nc.vector.reduce_sum(pos[:, :], place[:, :, :], AX.X))
                    done(nc.vector.reduce_sum(flat[:, :], kept[:, :, :], AX.X))
                    done(nc.vector.tensor_scalar(slot[:, :], idx[:, :], float(ET), None, ALU.mult))
                    done(nc.vector.tensor_tensor(slot[:, :], slot[:, :], pos[:, :], ALU.add))
                    done(nc.vector.tensor_tensor(slot[:, :], slot[:, :], group_base[:, :], ALU.add))
                    done(nc.vector.tensor_tensor(gates[:, k, :], gate[:, :], flat[:, :], ALU.mult))
                    done(nc.vector.tensor_tensor(pos[:, :], slot[:, :], flat[:, :], ALU.mult))
                    done(nc.vector.tensor_copy(slot_ids[:, k, :], pos[:, :]))
                    done(nc.vector.tensor_scalar(gone[:, :], flat[:, :], -DROPPED, DROPPED, ALU.mult, ALU.add))
                    done(nc.vector.tensor_tensor(slot[:, :], slot[:, :], gone[:, :], ALU.add))
                    nc.vector.tensor_copy(send_ids[:, k, :], slot[:, :]).then_inc(ids_ready, 1)
                v.wait_ge(ids_ready, 2)

            @block.scalar
            def _(a):
                a.wait_ge(exp_start, 1)
                nc.scalar.activation(soft[:, :, :], soft[:, :, :], ACT.Exp).then_inc(exp_done, 1)

            @block.tensor
            def _(pe):
                def tiles(t, q):
                    return t[:, :, :].rearrange("p (g q) e -> p q g e", q=TPG)[:, q, :, :]

                for k in range(2):
                    pe.wait_ge(hot_ready, k + 1)
                    if k == 1:
                        pe.wait_ge(kept_ready, 1)
                    for q in range(TPG):
                        terms = [(ltri, hotb[k], q)] + [(ones_bf, hotb[k], r) for r in range(q)]
                        if k == 1:
                            terms += [(ones_bf, keptb, r) for r in range(TPG)]
                        for n, (w, src, r) in enumerate(terms):
                            ins = nc.tensor.matmul(ps_p[k][:, q, :, :], w[:, :], tiles(src, r),
                                                   start=(n == 0), stop=(n == len(terms) - 1))
                    ins.then_inc(place_done, 1)


def ffn1_stage(nc, w0_d, w1_d, wo_d, slots_dram, eo_dram, ident):
    NH = ET // 512
    with Pool(nc) as m:
        w0 = [m.sb(f"f1w0{i}", [P, HID]) for i in range(2)]
        w1 = [m.sb(f"f1w1{i}", [P, HID]) for i in range(2)]
        wo = [m.sb(f"f1wo{i}", [P, HC, D]) for i in range(2)]
        xe = [m.sb(f"f1xe{i}", [P, NG, D]) for i in range(2)]
        xT = m.sb("f1xT", [P, ET])
        ge = m.sb("f1ge", [P, 2, 512])
        hid = m.sb("f1hid", [P, HC, ET])
        eo = [m.sb(f"f1eo{i}", [P, NG, D]) for i in range(2)]
        ps_t = [m.ps(f"f1ps_t{i}") for i in range(2)]
        ps_a = [m.ps(f"f1ps_a{i}") for i in range(2)]
        ps_b = [m.ps(f"f1ps_b{i}") for i in range(2)]
        ps_o = [m.ps(f"f1ps_o{i}", (P, 4, D)) for i in range(2)]
        loaded = [m.sem(f"f1loaded{i}") for i in range(2)]
        xT_done, xT_ready = m.sem("f1xT_done"), m.sem("f1xT_ready")
        a_done, a_ready = m.sem("f1a_done"), m.sem("f1a_ready")
        b_done, hid_ready = m.sem("f1b_done"), m.sem("f1hid_ready")
        o_done, o_ready = m.sem("f1o_done"), m.sem("f1o_ready")
        stored = m.sem("f1stored")
        NL = 5
        UN = HC * NH
        xs_v = slots_dram.rearrange("(e g p) d -> e p g d", e=E, p=P)
        eo_v = eo_dram.rearrange("(e g p) d -> e p g d", e=E, p=P)
        full = (HC - 1) * P
        with nc.Block() as block:
            @block.sync
            def _(sp):
                def experts(r):
                    for i in range(2):
                        e = r * 2 + i
                        sp.wait_ge(o_done, up((e - 2) * 2 + 2))
                        sp.dma_start(xe[i][:, :, :], xs_v[bass.ds(e, 1)]).then_inc(loaded[i], 16)
                        sp.dma_start(w0[i][:, :], w0_d[bass.ds(e, 1)]).then_inc(loaded[i], 16)
                        sp.dma_start(w1[i][:, :], w1_d[bass.ds(e, 1)]).then_inc(loaded[i], 16)
                        sp.dma_start(wo[i][:, 0:HC - 1, :], wo_d[bass.ds(e, 1), 0:full].rearrange("a (c p) d -> p (a c) d", p=P)).then_inc(loaded[i], 16)
                        sp.dma_start(wo[i][0:HID - full, HC - 1, :], wo_d[bass.ds(e, 1), full:HID]).then_inc(loaded[i], 16)

                rolled(sp, E // 2, experts)

            @block.gpsimd
            def _(pool):
                def experts(r):
                    for i in range(2):
                        pool.wait_ge(o_ready, (r * 2 + i) * 2 + 2)
                        pool.dma_start(eo_v[bass.ds(r * 2 + i, 1)], eo[i][:, :, :]).then_inc(stored, 16)

                rolled(pool, E // 2, experts)
                pool.wait_ge(stored, 16 * E)

            @block.tensor
            def _(pe):
                def experts(r):
                    for i in range(2):
                        e = r * 2 + i
                        pe.wait_ge(loaded[i], (r + 1) * (16 * NL))
                        for g in range(NG):
                            ins = nc.tensor.transpose(ps_t[g // 4][:, (g % 4) * P:(g % 4 + 1) * P], xe[i][:, g, :], ident[:, :])
                            if g % 4 == 3:
                                ins.then_inc(xT_done, 1)
                        pe.wait_ge(xT_ready, (e + 1) * 2)
                        for u in range(UN):
                            c, half = divmod(u, NH)
                            n = hrows(c)
                            rhs = xT[:, half * 512:(half + 1) * 512]
                            if u >= 2:
                                pe.wait_ge(a_ready, up(e * UN + u - 1))
                                pe.wait_ge(hid_ready, up(e * UN + u - 1))
                            nc.tensor.matmul(ps_a[u % 2][0:n, :], w0[i][:, c * P:c * P + n], rhs, start=True, stop=True).then_inc(a_done, 1)
                            nc.tensor.matmul(ps_b[u % 2][0:n, :], w1[i][:, c * P:c * P + n], rhs, start=True, stop=True).then_inc(b_done, 1)
                        pe.wait_ge(hid_ready, (e + 1) * UN)
                        for s in range(NG):
                            for c in range(HC):
                                n = hrows(c)
                                ins = nc.tensor.matmul(ps_o[s // 4][:, s % 4, :], hid[0:n, c, s * P:(s + 1) * P], wo[i][0:n, c, :],
                                                       start=(c == 0), stop=(c == HC - 1))
                            if s % 4 == 3:
                                ins.then_inc(o_done, 1)

                rolled(pe, E // 2, experts)

            @block.scalar
            def _(a):
                def experts(r):
                    for i in range(2):
                        e = r * 2 + i
                        for k in range(2):
                            a.wait_ge(xT_done, e * 2 + k + 1)
                            nc.scalar.activation(xT[:, k * 512:(k + 1) * 512], ps_t[k][:, :], ACT.Copy).then_inc(xT_ready, 1)
                        for u in range(UN):
                            n = hrows(u // NH)
                            a.wait_ge(a_done, e * UN + u + 1)
                            if u >= 2:
                                a.wait_ge(hid_ready, up(e * UN + u - 1))
                            nc.scalar.activation(ge[0:n, u % 2, :], ps_a[u % 2][0:n, :], ACT.Gelu_apprx_tanh).then_inc(a_ready, 1)
                        for k in range(2):
                            a.wait_ge(o_done, e * 2 + k + 1)
                            if k == 0:
                                a.wait_ge(stored, r * 32)
                            nc.scalar.activation(eo[i][:, k * 4:(k + 1) * 4, :], ps_o[k][:, :, :], ACT.Copy).then_inc(o_ready, 1)

                rolled(a, E // 2, experts)

            @block.vector
            def _(v):
                def experts(r):
                    for i in range(2):
                        e = r * 2 + i
                        for u in range(UN):
                            c, half = divmod(u, NH)
                            n = hrows(c)
                            v.wait_ge(a_ready, e * UN + u + 1)
                            v.wait_ge(b_done, e * UN + u + 1)
                            nc.vector.tensor_tensor(hid[0:n, c, half * 512:(half + 1) * 512], ge[0:n, u % 2, :],
                                                    ps_b[u % 2][0:n, :], ALU.mult).then_inc(hid_ready, 1)

                rolled(v, E // 2, experts)




H1 = 16
HD = D // H1
REL = 64
NREL = 2 * REL + 1
BAND = P + REL
PITCH = BAND + P - 1
GI = 16
PARTS = 3
KS = PARTS * PARTS * HD
QUAD = 4
QW = QUAD * HD
TAB = 2 * T - 1


def tables1_stage(nc, a, xn_all, send_ids, rel_k, rel_v, b_qkv, ident, bias_q, bias_k, bias_v, rel_st, tabs, pick, fold, ones_row):
    with Pool(nc) as m:
        rk = m.sb("t1rk", [HD, NREL])
        rpad = m.sb("t1rpad", [HD, 2, BAND])
        rlow = m.sb("t1rlow", [HD, 2, BAND])
        parts = [m.sb(f"t1parts{i}", [HD, 2, BAND], BF16) for i in range(PARTS)]
        rv = m.sb("t1rv", [1, TAB, HD])
        rvd = m.sb("t1rvd", [1, 2, TAB, HD])
        edge_v = m.sb("t1edge_v", [P, 2, HD])
        edge_k = m.sb("t1edge_k", [P, 2])
        bq = m.sb("t1bq", [P, 2])
        bv = m.sb("t1bv", [P, D])
        loaded = m.sem("t1loaded")
        own = m.sem("t1step")
        own_p = m.sem("t1pool_step")
        made = m.sem("t1made")
        moved = m.sem("t1moved")
        listed = m.sem("t1listed")
        sent = m.sem("t1sent")
        zz = m.sb("t1zz", [P, H1, P - 1])
        skew = a["skew"]
        rv_dram = a["rv_table"]
        NLD = [0]
        with nc.Block() as block:
            @block.sync
            def _(sp):
                def load(dst, src):
                    sp.dma_start(dst, src, allow_slow_non_contiguous=True).then_inc(loaded, 16)
                    NLD[0] += 1

                load(rk[:, :], rel_k.rearrange("m d -> d m"))
                lo = T - 1 - REL
                load(rv[:, 0:lo, :], rel_v[0:1, :].unsqueeze(1).to_broadcast([1, lo, HD]))
                load(rv[:, lo:lo + NREL, :], rel_v.unsqueeze(0))
                load(rv[:, lo + NREL:TAB, :], rel_v[NREL - 1:NREL, :].unsqueeze(1).to_broadcast([1, TAB - lo - NREL, HD]))
                for n, row in enumerate((NREL - 1, 0)):
                    load(edge_v[:, n, :], rel_v[row, :].partition_broadcast(P))
                    for h in range(H1):
                        load(edge_k[h * HD:(h + 1) * HD, n:n + 1], rel_k[row, :].unsqueeze(1))
                load(bq[:, :], b_qkv[0:2 * D].rearrange("(w p) -> p w", p=P))
                load(bv[:, :], b_qkv[2 * D:3 * D].partition_broadcast(P))
                sp.wait_ge(made, 1)
                for c in range(PARTS):
                    for k in range(PARTS):
                        sp.dma_start(rel_st[c * PARTS * HD + k:(c + 1) * PARTS * HD:PARTS, :, :], parts[k][:, :, :]).then_inc(moved, 16)
                sp.wait_ge(made, 2)
                sp.dma_start(rv_dram.unsqueeze(0), rvd[:, :, :, :]).then_inc(listed, 16)
                sp.dma_start(skew[0][:, :, BAND:PITCH], zz[:, :, :]).then_inc(moved, 16)
                sp.dma_start(skew[1][:, :, 0:P - 1], zz[:, :, :]).then_inc(moved, 16)
                sp.wait_ge(listed, 16)
                for n, (it, jt, ig) in enumerate(TABLES):
                    first = jt * P - (it * P + ig * GI + GI - 1) + T - 1
                    flat = rv_dram[it].rearrange("t d -> (t d)")
                    src = bass.AP(flat.tensor, flat.offset + first * HD, [[HD, P], [1, P]])
                    sp.dma_start(tabs[:, n, :], src).then_inc(moved, 16)
                sp.wait_ge(moved, 16 * (PARTS * PARTS + 2 + len(TABLES)))

            NLOADS = 1 + 3 + 2 * (1 + H1) + 2

            @block.vector
            def _(v):
                st = Steps(own)

                def done(ins):
                    ins.then_inc(own, 1)
                    v.wait_ge(own, st.value())

                v.wait_ge(loaded, 16 * NLOADS)
                nc.vector.memset(zz[:, :, :], 0.0)
                e = NREL - 1
                done(nc.vector.tensor_scalar(rpad[:, 0, REL - 1:BAND], rk[:, :], rk[:, e:e + 1], None, ALU.subtract))
                done(nc.vector.tensor_scalar(rpad[:, 1, 0:NREL], rk[:, :], rk[:, 0:1], None, ALU.subtract))
                done(nc.vector.tensor_copy(rpad[:, 0, 0:REL - 1], rpad[:, 0, REL - 1:REL].to_broadcast([HD, REL - 1])))
                done(nc.vector.tensor_copy(rpad[:, 1, NREL:BAND], rpad[:, 1, NREL - 1:NREL].to_broadcast([HD, REL - 1])))
                done(nc.vector.tensor_copy(parts[0][:, :, :], rpad[:, :, :]))
                done(nc.vector.tensor_tensor(rlow[:, :, :], rpad[:, :, :], parts[0][:, :, :], ALU.subtract))
                done(nc.vector.tensor_copy(parts[1][:, :, :], rlow[:, :, :]))
                done(nc.vector.tensor_tensor(rlow[:, :, :], rlow[:, :, :], parts[1][:, :, :], ALU.subtract))
                nc.vector.tensor_copy(parts[2][:, :, :], rlow[:, :, :]).then_inc(made, 1)
                for n in range(2):
                    row = TAB - 1 if n == 0 else 0
                    ins = nc.vector.tensor_tensor(rvd[:, n, :, :], rv[:, :, :], rv[:, row:row + 1, :].to_broadcast([1, TAB, HD]), ALU.subtract)
                    done(ins)
                    done(nc.vector.tensor_tensor(bias_v[:, n, :, :], bv[:, :].rearrange("p (h d) -> p h d", h=H1),
                                                 bc(edge_v[:, n, :], 1, H1), ALU.add))
                    done(nc.vector.tensor_tensor(bias_k[:, n:n + 1], bq[:, 1:2], edge_k[:, n:n + 1], ALU.add))
                done(nc.vector.tensor_scalar(bias_q[:, :], bq[:, 0:1], float(HD) ** -0.5, None, ALU.mult))
                done(nc.vector.memset(fold[:, :, :], 0.0))
                done(nc.vector.memset(ones_row[:, :], 1.0))
                for q in range(QUAD):
                    ins = nc.vector.tensor_reduce(fold[:, q, q * HD:(q + 1) * HD],
                                                  ident[:, :].rearrange("p (r d) -> p d r", d=HD), AX.X, ALU.add)
                ins.then_inc(made, 1)
                v.wait_ge(made, 2)

            @block.gpsimd
            def _(pool):
                nc.gpsimd.memset(pick[:, :], 1.0).then_inc(own_p, 1)
                pool.wait_ge(own_p, 1)
                nc.gpsimd.affine_select(out=pick[:, :], in_=pick[:, :], compare_op=ALU.is_ge, fill=0.0,
                                        base=-(GI - 1) * HD, pattern=[[HD, GI]], channel_multiplier=1).then_inc(own_p, 1)
                pool.wait_ge(own_p, 2)
                nc.gpsimd.affine_select(out=pick[:, :], in_=pick[:, :], compare_op=ALU.is_ge, fill=0.0,
                                        base=GI * HD - 1, pattern=[[-HD, GI]], channel_multiplier=-1).then_inc(own_p, 1)
                pool.wait_ge(own_p, 3)
                for k in range(2):
                    for t in range(NT):
                        nc.gpsimd.indirect_dma_start(
                            out=a["slots"], out_offset=bass.IndirectOffsetOnAxis(ap=send_ids[:, k, t:t + 1], axis=0),
                            in_=xn_all[:, t, :], in_offset=None, bounds_check=SLOTS - 1, oob_is_err=False).then_inc(sent, 16)
                pool.wait_ge(sent, 16 * 2 * NT)


TABLES = [(it, jt, ig) for it in range(2) for ig in range(P // GI)
          for jt in range(2) if jt == it or (ig >= REL // GI if it == 0 else ig < REL // GI)]


def attn1_stage(nc, x_all, xnT_all, a, gates, slot_ids, ident, one, bias_q, bias_k, bias_v, rel_st, tabs, pick, fold, ones_row):
    skew, parts = a["skew"], a["parts"]
    HP = H1 // 2
    S2 = 2 * B
    with Pool(nc) as m:
        w_in = m.sb("a1w_in", [P, 3, D])
        w_out = m.sb("a1w_out", [P, D])
        b_out = m.sb("a1b_out", [1, D])
        xb = m.sb("a1xb", [P, T])
        qkf = m.sb("a1qkf", [P, 3, T])
        low = m.sb("a1low", [P, 3, T])
        prt = m.sb("a1prt", [P, PARTS, 3, T], BF16)
        stk = [m.sb(f"a1stk{i}", [KS, 3, H1, T], BF16) for i in range(2)]
        vx = m.sb("a1vx", [P, 2, 2, H1, QW])
        Rt = m.sb("a1Rt", [P, H1, BAND])
        Sb = [m.sb(f"a1Sb{i}", [P, H1, T]) for i in range(2)]
        Pm = m.sb("a1Pm", [P, H1, T])
        nmx = [m.sb(f"a1nmx{i}", [P, H1]) for i in range(2)]
        PT = m.sb("a1PT", [P, 2, H1, P])
        X = m.sb("a1X", [P, H1, P])
        ids = m.sb("a1ids", [P, 2, 1], U32)
        rows = m.sb("a1rows", [P, 2, D])
        pool_taker = m.sb("a1pool_taker", [P, 1])
        taker = m.sb("a1taker", [1, HP])
        den = [m.sb(f"a1den{i}", [P, H1]) for i in range(2)]
        rden = m.sb("a1rden", [P, H1])
        rrep = m.sb("a1rrep", [P, H1, HD])
        rdT = m.sb("a1rdT", [P, P])
        cT = m.sb("a1cT", [P, P])
        ps_p = m.ps("a1ps_p", (P, 2, T))
        ps_R0 = m.ps("a1ps_R", (P, 2, BAND))
        ps_S0 = [m.ps(f"a1ps_S{i}", (P, 2, T)) for i in range(2)]
        ps_T = [m.ps(f"a1ps_T{i}", (P, 2, 2, P)) for i in range(2)]
        ps_R = [ps_R0[:, :, :], ps_T[0][:, :, :, :].rearrange("p a b i -> p (a b i)")[:, 0:2 * BAND].rearrange("p (n c) -> p n c", n=2)]
        ps_TT = [ps_T[0][:, :, :, :], ps_T[1][:, :, :, :]] + [b[:, :, :].rearrange("p a (b i) -> p a b i", b=2) for b in ps_S0]
        ps_S = [ps_S0[0][:, :, :], ps_S0[1][:, :, :], ps_T[1][:, :, :, :].rearrange("p a b i -> p a (b i)")]
        ps_X = [m.ps("a1ps_X", (P, 2, H1, GI))[:, :, :, :], ps_p[:, :, :].rearrange("p n (h i) -> p n h i", h=H1)]
        ps_c = m.ps("a1ps_c", (P, 512))
        ctx_ps, rdT_ps, y_ps = ps_c[:, 0:P], ps_c[:, P:2 * P], ps_c[:, 2 * P:3 * P]
        names = ("loaded xb_ready qk_done qk_ready split parts_out stacked0 stacked1 v_done v_ready R_done R_ready skew_out0 skew_out1 "
                 "skew_in00 skew_in01 skew_in10 skew_in11 S_done S_ready P_ready T_done Ta_ready Tv_ready X_done X_ready c_done cT_ready rrep_ready "
                 "rdT_done rdT_ready y_done y_added pool_step vec_step cleared ids_ready rows_in first_added combined")
        sm = {n: m.sem("a1" + n) for n in names.split()}
        stacked = [sm["stacked0"], sm["stacked1"]]
        skew_out = [sm["skew_out0"], sm["skew_out1"]]
        skew_in = [[sm[f"skew_in{it}{half}"] for half in range(2)] for it in range(2)]
        STACK = 16 * PARTS * (2 + PARTS)
        HH = H1 // 2

        def steps(eng, step):
            for i in range(4):
                step(0, i)
            with eng.Fori(1, B // 2) as r:
                for i in range(4):
                    step(r, i)

        def tile_of(i):
            i %= 4
            return i % 2, i // 2

        with nc.Block() as block:
            @block.tensor
            def _(pe):
                def project_qk(n):
                    pe.wait_ge(sm["v_ready"], up(n - 1))
                    pe.wait_ge(sm["X_ready"], up((n - 2) * 8 + 4))
                    pe.wait_ge(sm["qk_ready"], n)
                    for w in range(2):
                        ins = nc.tensor.matmul(ps_p[:, w, :], w_in[:, w, :], xnT_all[:, bass.ds(n * T, T)], start=True, stop=True)
                    ins.then_inc(sm["qk_done"], 1)

                def project_v(n):
                    pe.wait_ge(sm["xb_ready"], n + 1)
                    pe.wait_ge(sm["qk_ready"], n + 2)
                    pe.wait_ge(sm["X_ready"], n * 8)
                    for j in range(2):
                        ins = nc.tensor.matmul(ps_p[:, 0, j * D:(j + 1) * D], xb[:, j * P:(j + 1) * P], w_in[:, 2, :],
                                               start=True, stop=True)
                    ins.then_inc(sm["v_done"], 1)

                def rel_scores(s, it, par, hp):
                    pe.wait_ge(sm["R_ready"], up(s * HP + hp - 1))
                    if hp == 1:
                        pe.wait_ge(sm["Ta_ready"], up((s - 1) * 4))
                    for n in range(2):
                        ins = nc.tensor.matmul(ps_R[hp % 2][:, n, :], stk[par][:, 0, 2 * hp + n, it * P:(it + 1) * P], rel_st[:, it, :],
                                               start=True, stop=True)
                    ins.then_inc(sm["R_done"], 1)

                def key_scores(s, it, par, hp):
                    pe.wait_ge(sm["S_ready"], up(s * H1 + 2 * (hp - 2) if hp > 2 else s * H1))
                    if hp == 0:
                        pe.wait_ge(sm["Ta_ready"], s * 4)
                    if hp == 1:
                        pe.wait_ge(sm["Tv_ready"], s * 4)
                    for n in range(2):
                        h = 2 * hp + n
                        ins = nc.tensor.matmul(ps_S[hp % 3][:, n, :], stk[par][:, 0, h, it * P:(it + 1) * P],
                                               stk[par][:, 1 + it, h, :], start=True, stop=True)
                    ins.then_inc(sm["S_done"], 1)

                def rel_values(s, b, it, k):
                    pe.wait_ge(sm["X_ready"], up(s * 4 + k - 1))
                    if k == 1:
                        if it == 0:
                            pe.wait_ge(sm["v_ready"], b + 1)
                        else:
                            pe.wait_ge(sm["qk_ready"], b + 3)
                    if k == 0:
                        pe.wait_ge(sm["Ta_ready"], (s + 1) * 4)
                        pe.wait_ge(sm["Tv_ready"], (s + 1) * 4)
                    for n in range(2):
                        ig = 2 * k + n
                        use = [(t, jt) for t, (i2, jt, g2) in enumerate(TABLES) if (i2, g2) == (it, ig)]
                        for q, (t, jt) in enumerate(use):
                            ins = nc.tensor.matmul(ps_X[k % 2][:, n, :, :], tabs[:, t, :], PT[:, jt, :, ig * GI:(ig + 1) * GI],
                                                   start=(q == 0), stop=(q == len(use) - 1))
                    ins.then_inc(sm["X_done"], 1)

                def context(s, b, it, quads):
                    if 0 in quads:
                        pe.wait_ge(sm["rdT_ready"], s + 1)
                        pe.wait_ge(sm["v_ready"], b + 1)
                        pe.wait_ge(sm["X_ready"], (s + 1) * 4)
                    for q in quads:
                        for part in range(3):
                            for g in range(H1 // QUAD):
                                h = g * QUAD + q
                                w, rhs = (fold[:, q, :], X[:, h, :]) if part == 2 else (vx[:, it, part, h, :], PT[:, part, h, :])
                                ins = nc.tensor.matmul(ctx_ps[g * QW:(g + 1) * QW, :], w, rhs,
                                                       start=(q == 0 and part == 0), stop=(q == QUAD - 1 and part == 2))
                    if QUAD - 1 in quads:
                        ins.then_inc(sm["c_done"], 1)

                def reciprocals(s):
                    pe.wait_ge(sm["rrep_ready"], s + 1)
                    pe.wait_ge(sm["y_added"], s)
                    nc.tensor.transpose(rdT_ps, rrep[:, :, :].rearrange("p h d -> p (h d)"), ident[:, :]).then_inc(sm["rdT_done"], 1)

                def project_out(s):
                    pe.wait_ge(sm["cT_ready"], s + 1)
                    nc.tensor.matmul(y_ps, cT[:, :], w_out[:, :], start=True, stop=False)
                    nc.tensor.matmul(y_ps, ones_row[:, :], b_out[:, :], start=False, stop=True).then_inc(sm["y_done"], 1)

                def transposes(s, k):
                    if k == 0:
                        pe.wait_ge(sm["R_ready"], (s + 2) * HP)
                    if 0 < k < 4:
                        pe.wait_ge(sm["S_ready"], s * H1 + 2 * (5 if k == 1 else k + 4) + 2)
                    pe.wait_ge(sm["P_ready"], s * H1 + 2 * k + 2)
                    if k >= 4:
                        pe.wait_ge(sm["Ta_ready" if k % 2 == 0 else "Tv_ready"], s * 4 + k // 2 - 1)
                    for n in range(2):
                        for jt in range(2):
                            ins = nc.tensor.transpose(ps_TT[k % 4][:, n, jt, :], Pm[:, 2 * k + n, jt * P:(jt + 1) * P], ident[:, :])
                    ins.then_inc(sm["T_done"], 1)

                def step(r, i):
                    s = r * 4 + i
                    it, par = tile_of(i)
                    nit, npar = tile_of(i + 1)
                    pit, ppar = tile_of(i + 3)
                    after_first = not isinstance(r, int) or i > 0
                    prev_b = r * 2 + par - (1 if it == 0 else 0)
                    if it == 1:
                        pe.wait_ge(stacked[npar], (r + 1 + (1 if i == 3 else 0)) * STACK)
                    for hp in range(HP):
                        key_scores(s, it, par, hp)
                        rel_scores(s + 1, nit, npar, hp)
                        if after_first and hp == 1:
                            reciprocals(s - 1)
                        if after_first and hp < 4:
                            rel_values(s - 1, prev_b, pit, hp)
                        if it == 1 and hp == 4:
                            project_qk(r * 2 + par + 2)
                        if after_first and hp >= 4:
                            context(s - 1, prev_b, pit, (hp - 4,))
                    for k in range(HP):
                        transposes(s, k)
                        if after_first and k == HP // 2 - 1:
                            project_out(s - 1)
                    if it == 0:
                        project_v(r * 2 + par)

                pe.wait_ge(sm["loaded"], 16 * 4)
                project_qk(0)
                project_qk(1)
                pe.wait_ge(stacked[0], STACK)
                for hp in range(HP):
                    rel_scores(0, 0, 0, hp)
                steps(pe, step)
                last = 2 * B - 1
                for k in range(4):
                    rel_values(last, B - 1, 1, k)
                reciprocals(last)
                context(last, B - 1, 1, range(QUAD))
                project_out(last)

            @block.scalar
            def _(act):
                def keep_qk(n):
                    act.wait_ge(sm["qk_done"], n + 1)
                    act.wait_ge(sm["split"], n)
                    nc.scalar.activation(qkf[:, 0, :], ps_p[:, 0, :], ACT.Identity, bias=bias_q[:, 0:1], scale=float(HD) ** -0.5)
                    nc.scalar.activation(qkf[:, 1, :], ps_p[:, 1, :], ACT.Identity, bias=bias_k[:, 0:1])
                    nc.scalar.activation(qkf[:, 2, :], ps_p[:, 1, :], ACT.Identity, bias=bias_k[:, 1:2]).then_inc(sm["qk_ready"], 1)

                def keep_R(s, hp):
                    act.wait_ge(sm["R_done"], s * HP + hp + 1)
                    if hp % (HP // 2) == 0:
                        act.wait_ge(skew_out[hp // (HP // 2)], s * 16)
                    nc.scalar.activation(Rt[:, 2 * hp:2 * hp + 2, :], ps_R[hp % 2], ACT.Copy).then_inc(sm["R_ready"], 1)

                def exponentials(s, it, hp):
                    for h in (2 * hp, 2 * hp + 1):
                        act.wait_ge(sm["S_ready"], s * H1 + h + 1)
                        nc.scalar.activation(Pm[:, h, :], Pm[:, h, :], ACT.Exp, bias=nmx[it][:, h:h + 1], scale=-1.0,
                                             accum_out=den[it][:, h:h + 1]).then_inc(sm["P_ready"], 1)

                def keep_rdT(s):
                    act.wait_ge(sm["rdT_done"], s + 1)
                    act.wait_ge(sm["cT_ready"], s)
                    nc.scalar.activation(rdT[:, :], rdT_ps, ACT.Copy).then_inc(sm["rdT_ready"], 1)

                def keep_T(s, k):
                    act.wait_ge(sm["T_done"], s * HP + k + 1)
                    act.wait_ge(sm["c_done"], s)
                    nc.scalar.activation(PT[:, :, 2 * k:2 * k + 2, :].rearrange("p j h i -> p h j i"), ps_TT[k % 4],
                                         ACT.Copy).then_inc(sm["Ta_ready"], 1)

                def step(r, i):
                    s = r * 4 + i
                    it, par = tile_of(i)
                    for hp in range(HP):
                        keep_R(s + 1, hp)
                        exponentials(s, it, hp)
                        if hp == 1 and (not isinstance(r, int) or i > 0):
                            keep_rdT(s - 1)
                        if it == 1 and hp == 4:
                            keep_qk(r * 2 + par + 2)
                    for k in range(0, HP, 2):
                        keep_T(s, k)

                keep_qk(0)
                keep_qk(1)
                for hp in range(HP):
                    keep_R(0, hp)
                steps(act, step)
                keep_rdT(2 * B - 1)

            @block.vector
            def _(v):
                def keep_v(n):
                    v.wait_ge(sm["v_done"], n + 1)
                    for tile in range(2):
                        to = vx[:, tile, :, :, :].rearrange("p j (g q) c -> p j g q c", q=QUAD)
                        src = ps_p[:, 0, :].rearrange("p (j g q d) -> p j g q d", j=2, q=QUAD, d=HD)
                        bias = bias_v[:, tile, :, :].rearrange("p (g q) d -> p g q d", q=QUAD)
                        for q in range(QUAD):
                            ins = nc.vector.tensor_tensor(to[:, :, :, q, q * HD:(q + 1) * HD], src[:, :, :, q, :],
                                                          bc(bias[:, :, q, :], 1, 2), ALU.add)
                    ins.then_inc(sm["v_ready"], 1)

                def add_scores(r, i, hp):
                    s = r * 4 + i
                    it, par = tile_of(i)
                    if hp % (HP // 2) == 0:
                        v.wait_ge(skew_in[it][hp // (HP // 2)], (r * 2 + par + 1) * 16)
                    v.wait_ge(sm["S_done"], s * HP + hp + 1)
                    v.wait_ge(sm["T_done"], up((s - 1) * HP + hp + 1))
                    nc.vector.memset(taker[:, hp:hp + 1], 0.0)
                    for h in (2 * hp, 2 * hp + 1):
                        nc.vector.tensor_tensor_reduce(out=Pm[:, h, :], in0=ps_S[hp % 3][:, h % 2, :], in1=Sb[it][:, h, :],
                                                       scale=-1.0, scalar=3.0e38, op0=ALU.add, op1=ALU.min,
                                                       accum_out=nmx[it][:, h:h + 1]).then_inc(sm["S_ready"], 1)

                def pick_diagonal(s, k):
                    v.wait_ge(sm["X_done"], s * 4 + k + 1)
                    v.wait_ge(sm["c_done"], s)
                    out = X[:, :, k * 2 * GI:(k + 1) * 2 * GI].rearrange("p h (n i) -> p n h i", n=2)
                    nc.vector.tensor_tensor(out, ps_X[k % 2], bc(bc(pick[:, :], 1, H1), 1, 2), ALU.mult).then_inc(sm["X_ready"], 1)

                def divide(s):
                    v.wait_ge(sm["c_done"], s + 1)
                    v.wait_ge(sm["rdT_ready"], s + 1)
                    v.wait_ge(sm["y_done"], s)
                    nc.vector.tensor_tensor(cT[:, :], ctx_ps, rdT[:, :], ALU.mult).then_inc(sm["cT_ready"], 1)

                def add_y(s):
                    v.wait_ge(sm["y_done"], s + 1)
                    xs = x_all[:, bass.ds(s, 1), :]
                    nc.vector.tensor_tensor(xs, xs, y_ps.unsqueeze(1), ALU.add).then_inc(sm["y_added"], 1)

                def combine(s):
                    v.wait_ge(sm["rows_in"], (s + 1) * 32)
                    v.wait_ge(sm["y_added"], s + 1)
                    xs = x_all[:, bass.ds(s, 1), :]
                    for k in range(2):
                        if k == 1:
                            v.wait_ge(sm["first_added"], s + 1)
                        nc.vector.scalar_tensor_tensor(out=xs, in0=rows[:, k:k + 1, :], scalar=gates[:, k, bass.ds(s, 1)], in1=xs,
                                                       op0=ALU.mult, op1=ALU.add).then_inc(sm["first_added" if k == 0 else "combined"], 1)

                def invert(s, it):
                    v.wait_ge(sm["P_ready"], (s + 1) * H1)
                    nc.vector.reciprocal(rden[:, :], den[it][:, :]).then_inc(sm["vec_step"], 1)
                    v.wait_ge(sm["vec_step"], s + 1)
                    v.wait_ge(sm["rdT_done"], s)
                    nc.vector.tensor_copy(rrep[:, :, :], bc(rden[:, :], 2, HD)).then_inc(sm["rrep_ready"], 1)

                def keep_T(s, k):
                    v.wait_ge(sm["T_done"], s * HP + k + 1)
                    nc.vector.tensor_copy(PT[:, :, 2 * k:2 * k + 2, :].rearrange("p j h i -> p h j i"),
                                          ps_TT[k % 4]).then_inc(sm["Tv_ready"], 1)

                def step(r, i):
                    s = r * 4 + i
                    it, par = tile_of(i)
                    after_first = not isinstance(r, int) or i > 0
                    for hp in range(HP):
                        add_scores(r, i, hp)
                        if after_first and hp < 4:
                            pick_diagonal(s - 1, hp)
                    if after_first:
                        divide(s - 1)
                    for k in range(1, HP, 2):
                        keep_T(s, k)
                        if after_first and k == HP // 2 + 1:
                            add_y(s - 1)
                            combine(s - 1)
                    if it == 0:
                        keep_v(r * 2 + par)
                    invert(s, it)

                nc.vector.memset(vx[:, :, :, :, :], 0.0)
                nc.vector.memset(Sb[0][:, :, BAND:T], 0.0)
                nc.vector.memset(Sb[1][:, :, 0:T - BAND], 0.0).then_inc(sm["cleared"], 1)
                v.wait_ge(sm["cleared"], 1)
                steps(v, step)
                last = 2 * B - 1
                for k in range(4):
                    pick_diagonal(last, k)
                divide(last)
                add_y(last)
                combine(last)
                v.wait_ge(sm["combined"], 2 * B)

            @block.gpsimd
            def _(pool):
                def copy_x(n):
                    pool.wait_ge(sm["v_done"], n)
                    nc.gpsimd.tensor_copy(xb[:, :], xnT_all[:, bass.ds(n * T, T)]).then_inc(sm["xb_ready"], 1)

                def split(n, before, done_before):
                    pool.wait_ge(sm["qk_ready"], n + 1)
                    pool.wait_ge(stacked[before], done_before)
                    src = qkf
                    for k in range(PARTS):
                        ins = nc.gpsimd.tensor_tensor(prt[:, k, :, :], src[:, :, :], bc(one[:, :].to_broadcast([P, T]), 1, 3), ALU.mult)
                        if k == PARTS - 1:
                            ins.then_inc(sm["split"], 1)
                        else:
                            ins.then_inc(sm["pool_step"], 1)
                            pool.wait_ge(sm["pool_step"], n * 4 + 2 * k + 1)
                            nc.gpsimd.tensor_tensor(low[:, :, :], src[:, :, :], prt[:, k, :, :], ALU.subtract).then_inc(sm["pool_step"], 1)
                            pool.wait_ge(sm["pool_step"], n * 4 + 2 * k + 2)
                            src = low

                def gather(s):
                    pool.wait_ge(sm["combined"], s)
                    nc.gpsimd.tensor_copy(ids[:, :, :], slot_ids[:, :, bass.ds(s, 1)]).then_inc(sm["ids_ready"], 1)
                    pool.wait_ge(sm["ids_ready"], s + 1)
                    nc.gpsimd.tensor_tensor(pool_taker[:, :], one[:, :], one[:, :], ALU.mult)
                    for k in range(2):
                        nc.gpsimd.indirect_dma_start(
                            out=rows[:, k, :], out_offset=None, in_=a["eo"],
                            in_offset=bass.IndirectOffsetOnAxis(ap=ids[:, k, :], axis=0)).then_inc(sm["rows_in"], 16)

                def step(r, i):
                    it, par = tile_of(i)
                    if it == 0:
                        copy_x(r * 2 + par + 1)
                    else:
                        split(r * 2 + par + 2, 1 - par, (r + 1 + par) * STACK)
                    gather(r * 4 + i)

                pool.wait_ge(sm["loaded"], 16 * 4)
                pool.wait_ge(sm["cleared"], 1)
                copy_x(0)
                split(0, 1, 0)
                split(1, 0, STACK)
                steps(pool, step)

            @block.sync
            def _(sp):
                def send_parts(n):
                    sp.wait_ge(sm["split"], n + 1)
                    sp.dma_start(parts, prt[:, :, :, :]).then_inc(sm["parts_out"], 16)

                def stack(n, par):
                    sp.wait_ge(sm["parts_out"], (n + 1) * 16)
                    k_rows = parts.rearrange("(h d) k w t -> (d k) w h t", d=HD)
                    q_rows = parts.rearrange("(h d) k w t -> d k w h t", d=HD)
                    for c in range(PARTS):
                        rows = slice(c * PARTS * HD, (c + 1) * PARTS * HD)
                        for w in (1, 2):
                            sp.dma_start(stk[par][rows, w, :, :], k_rows[:, w, :, :]).then_inc(stacked[par], 16)
                        for k in range(PARTS):
                            sp.dma_start(stk[par][c * PARTS * HD + k:(c + 1) * PARTS * HD:PARTS, 0, :, :],
                                         q_rows[:, (k + c) % PARTS, 0, :, :]).then_inc(stacked[par], 16)

                def skew_tile(s, it, between):
                    for half in range(2):
                        hs = slice(half * HH, (half + 1) * HH)
                        sp.wait_ge(sm["R_ready"], s * HP + (half + 1) * (HP // 2))
                        c0 = 0 if it == 0 else P - 1
                        sp.dma_start(skew[it][:, hs, c0:c0 + BAND], Rt[:, hs, :]).then_inc(skew_out[half], 16)
                        between(half)
                        sp.wait_ge(skew_out[half], (s + 1) * 16)
                        c0 = 0 if it == 0 else T - BAND
                        flat = skew[it].rearrange("i h c -> (i h c)")
                        sp.dma_start(Sb[it][:, hs, c0:c0 + BAND],
                                     bass.AP(flat.tensor, flat.offset + half * HH * PITCH + P - 1,
                                             [[H1 * PITCH - 1, P], [PITCH, HH], [1, BAND]])).then_inc(skew_in[it][half], 16)

                def step(r, i):
                    s = r * 4 + i
                    it, par = tile_of(i)
                    nit, npar = tile_of(i + 1)
                    if it == 0:
                        skew_tile(s + 1, nit, lambda half: stack(r * 2 + par + 1, 1 - par) if half == 0 else None)
                    else:
                        skew_tile(s + 1, nit, lambda half: None)
                        send_parts(r * 2 + par + 2)

                sp.dma_start(w_in[:, :, :], a["L1_attn_W_qkv"].rearrange("d (w n) -> d w n", w=3)).then_inc(sm["loaded"], 16)
                sp.dma_start(w_out[:, :], a["L1_attn_W_out"]).then_inc(sm["loaded"], 16)
                sp.dma_start(b_out[:, :], a["L1_attn_b_out"].unsqueeze(0)).then_inc(sm["loaded"], 16)
                sp.dma_start(xnT_all[:, B * T:(B + 2) * T], xnT_all[:, 0:2 * T]).then_inc(sm["loaded"], 16)
                send_parts(0)
                stack(0, 0)
                sp.wait_ge(sm["cleared"], 1)
                skew_tile(0, 0, lambda half: None)
                send_parts(1)
                steps(sp, step)
                sp.wait_ge(stacked[0], (B // 2 + 1) * STACK)
                sp.wait_ge(sm["parts_out"], (B + 2) * 16)
                for half in range(2):
                    sp.wait_ge(skew_in[0][half], (B + 1) * 16)


def store_stage(nc, x_all, out):
    with Pool(nc) as m:
        stored = m.sem("stored")
        with nc.Block() as block:
            @block.sync
            def _(sp):
                sp.dma_start(out.rearrange("b (t p) d -> p (b t) d", p=P), x_all[:, :, :]).then_inc(stored, 16)
                sp.wait_ge(stored, 16)


def program(nc, a):
    with Pool(nc) as m:
        ident = m.sb("ident", [P, P])
        iota_e = m.sb("iota_e", [P, E])
        ltri = m.sb("ltri", [P, P], BF16)
        ones_bf = m.sb("ones_bf", [P, P], BF16)
        group_base = m.sb("group_base", [P, NT])
        one = m.sb("one", [P, 1])
        router = m.sb("router", [P, 2, E])
        x_all = m.sb("x_all", [P, NT, D])
        xnT_all = m.sb("xnT_all", [P, (B + 2) * T])
        with Pool(nc) as g:
            mask = g.sb("mask", [P, T + P])
            expand = g.sb("expand", [E, FC0, P])
            logits = g.sb("logits0", [P, NT, E])
            constants(nc, ident, mask, expand, iota_e, ltri, ones_bf, group_base, one)
            x_dram = a["L0_attn_x"].rearrange("b (t p) d -> p (b t) d", p=P)
            load = [(x_all[:, :, :], x_dram), (router[:, 0, :], a["L0_ffn_router_w"]), (router[:, 1, :], a["L1_ffn_router_w"])]
            norm_stage(nc, x_all, None, xnT_all, ident, router[:, 0, :], logits, "n0", load)
            ffn0_stage(nc, x_all, xnT_all, logits, a["L0_ffn_router_b"], a["L0_ffn_W1"], a["L0_ffn_b1"], a["L0_ffn_W2"],
                       a["L0_ffn_b2"], ident, expand, iota_e)
            attn0_stage(nc, x_all, xnT_all, a["L0_attn_W_q"], a["L0_attn_W_k"], a["L0_attn_W_v"], a["L0_attn_W_o"], mask, one)
        gates = m.sb("gates", [P, 2, NT])
        slot_ids = m.sb("slot_ids", [P, 2, NT], U32)
        bias_q = m.sb("bias_q", [P, 1])
        bias_k = m.sb("bias_k", [P, 2])
        bias_v = m.sb("bias_v", [P, 2, H1, HD])
        rel_st = m.sb("rel_st", [KS, 2, BAND], BF16)
        tabs = m.sb("tabs", [P, len(TABLES), P])
        pick = m.sb("pick", [P, GI])
        fold = m.sb("fold", [P, QUAD, QW])
        ones_row = m.sb("ones_row", [1, P])
        with Pool(nc) as g:
            xn_all = g.sb("xn_all", [P, NT, D])
            logits = g.sb("logits1", [P, NT, E])
            send_ids = g.sb("send_ids", [P, 2, NT], U32)
            norm_stage(nc, x_all, xn_all, xnT_all, ident, router[:, 1, :], logits, "n1")
            gate1_stage(nc, logits, iota_e, ltri, ones_bf, a["slots"], gates, slot_ids, send_ids, group_base)
            tables1_stage(nc, a, xn_all, send_ids, a["L1_attn_rel_emb_k"], a["L1_attn_rel_emb_v"], a["L1_attn_b_qkv"], ident,
                          bias_q, bias_k, bias_v, rel_st, tabs, pick, fold, ones_row)
        ffn1_stage(nc, a["L1_ffn_w0_kernel"], a["L1_ffn_w1_kernel"], a["L1_ffn_wo_kernel"], a["slots"], a["eo"], ident)
        attn1_stage(nc, x_all, xnT_all, a, gates, slot_ids, ident, one, bias_q, bias_k, bias_v, rel_st, tabs, pick, fold, ones_row)
        store_stage(nc, x_all, a["out"])


NAMES = ["L0_attn_x", "L0_attn_W_q", "L0_attn_W_k", "L0_attn_W_v", "L0_attn_W_o", "L0_ffn_router_w", "L0_ffn_router_b",
         "L0_ffn_W1", "L0_ffn_b1", "L0_ffn_W2", "L0_ffn_b2", "L1_attn_W_qkv", "L1_attn_b_qkv", "L1_attn_W_out",
         "L1_attn_b_out", "L1_attn_rel_emb_k", "L1_attn_rel_emb_v", "L1_ffn_router_w", "L1_ffn_w0_kernel",
         "L1_ffn_w1_kernel", "L1_ffn_wo_kernel"]


def kernel(**inputs):
    import numpy as np
    import concourse.bacc as bacc
    from concourse.bass_utils import run_bass_kernel_spmd

    nc = bacc.Bacc("TRN2", target_bir_lowering=False, num_devices=1)
    arrays, aps = {}, {}
    for name in NAMES:
        a = np.ascontiguousarray(inputs[name])
        arrays["in_" + name] = a
        aps[name] = nc.dram_tensor("in_" + name, a.shape, mybir.dt.from_np(a.dtype), kind="ExternalInput").ap()
    aps["slots"] = nc.dram_tensor("slots", (SLOTS, D), F32, kind="Internal").ap()
    aps["eo"] = nc.dram_tensor("eo", (SLOTS, D), F32, kind="Internal").ap()
    aps["skew"] = [nc.dram_tensor(f"skew{i}", (P, H1, PITCH), F32, kind="Internal").ap() for i in range(2)]
    aps["parts"] = nc.dram_tensor("parts", (P, PARTS, 3, T), BF16, kind="Internal").ap()
    aps["rv_table"] = nc.dram_tensor("rv_table", (2, TAB, HD), F32, kind="Internal").ap()
    aps["out"] = nc.dram_tensor("out", (B, T, D), F32, kind="ExternalOutput").ap()
    program(nc, aps)
    r = run_bass_kernel_spmd(nc, [arrays], core_ids=[0])
    return r.results[0]["out"]
```

```python
import concourse.bass as bass
from concourse import mybir
from contextlib import ExitStack

F32 = mybir.dt.float32
BF16 = mybir.dt.bfloat16
U32 = mybir.dt.uint32
I32 = mybir.dt.int32
ALU = mybir.AluOpType
ACT = mybir.ActivationFunctionType
AX = mybir.AxisListType

P = 128
B, T, D = 16, 256, 128
NT = B * T // P
TPG = 4
NG = NT // TPG
GT = TPG * P
EPS = 1e-5
H0, DK = 16, 64
PAIRS = H0 // 2
E = 8
FF0 = 512
FC0 = FF0 // P
EPC = P // (FF0 // E)


class Pool:

    def __init__(self, nc):
        self.nc, self.ctx = nc, ExitStack()

    def __enter__(self):
        self.ctx.__enter__()
        return self

    def __exit__(self, *a):
        return self.ctx.__exit__(*a)

    def sb(self, name, shape, dt=F32):
        return self.ctx.enter_context(self.nc.sbuf_tensor(name, shape, dt))

    def ps(self, name, shape=(P, 512), dt=F32):
        return self.ctx.enter_context(self.nc.psum_tensor(name, list(shape), dt))

    def sem(self, name):
        return self.ctx.enter_context(self.nc.semaphore(name))


class Steps:

    def __init__(self, sem, base=0):
        self.sem, self.base, self.n = sem, base, 0

    def value(self):
        self.n += 1
        return self.base + self.n


def up(n):
    return max(n, 0) if isinstance(n, int) else n


def rolled(eng, n, body):
    body(0)
    with eng.Fori(1, n) as i:
        body(i)


def constants(nc, ident, mask, iota_e, ltri, ones_bf, group_base, one):
    with Pool(nc) as m:
        cs = m.sem("const_step")
        io = m.sb("iota_i", [P, E], I32)
        io_g = m.sb("iota_g", [P, NT], I32)
        with nc.Block() as block:
            @block.gpsimd
            def _(pool):
                nc.gpsimd.memset(ident[:, :], 0.0).then_inc(cs, 1)
                nc.gpsimd.memset(mask[:, :], 1.0).then_inc(cs, 1)
                nc.gpsimd.memset(ltri[:, :], 1.0).then_inc(cs, 1)
                nc.gpsimd.memset(ones_bf[:, :], 1.0).then_inc(cs, 1)
                nc.gpsimd.memset(one[:, :], 1.0).then_inc(cs, 1)
                nc.gpsimd.iota(io[:, :], pattern=[[1, E]], base=0, channel_multiplier=0).then_inc(cs, 1)
                nc.gpsimd.iota(io_g[:, :], pattern=[[CAP, NG], [0, TPG]], base=0, channel_multiplier=0).then_inc(cs, 1)
                pool.wait_ge(cs, 7)
                nc.gpsimd.tensor_copy(group_base[:, :], io_g[:, :]).then_inc(cs, 1)
                nc.gpsimd.affine_select(out=ident[:, :], in_=ident[:, :], compare_op=ALU.not_equal, fill=1.0,
                                        base=0, pattern=[[-1, P]], channel_multiplier=1).then_inc(cs, 1)
                nc.gpsimd.affine_select(out=mask[:, 0:T], in_=mask[:, 0:T], compare_op=ALU.is_ge, fill=0.0,
                                        base=0, pattern=[[1, T]], channel_multiplier=-1).then_inc(cs, 1)
                nc.gpsimd.affine_select(out=mask[:, T:T + P], in_=mask[:, T:T + P], compare_op=ALU.is_ge, fill=0.0,
                                        base=0, pattern=[[1, P]], channel_multiplier=-1).then_inc(cs, 1)
                nc.gpsimd.affine_select(out=ltri[:, :], in_=ltri[:, :], compare_op=ALU.is_gt, fill=0.0,
                                        base=0, pattern=[[1, P]], channel_multiplier=-1).then_inc(cs, 1)
                nc.gpsimd.tensor_copy(iota_e[:, :], io[:, :]).then_inc(cs, 1)
                pool.wait_ge(cs, 13)


def norm_stage(nc, x_all, xn_all, xnT_all, ident, router, logits, tag, load=None):
    with Pool(nc) as m:
        stats = m.sb(tag + "stats", [P, NT, 6])
        mean = m.sb(tag + "mean", [P, NT])
        mean2 = m.sb(tag + "mean2", [P, NT])
        rstd = m.sb(tag + "rstd", [P, NT])
        xn = [m.sb(f"{tag}xn{i}", [P, TPG, D]) for i in range(2)]
        xT = [m.sb(f"{tag}xT{i}", [P, GT]) for i in range(2)]
        ps_t = [m.ps(f"{tag}ps_t{i}") for i in range(2)]
        ps_l = [m.ps(f"{tag}ps_l{i}", (P, TPG, E)) for i in range(2)]
        loaded = m.sem(tag + "loaded")
        own = m.sem(tag + "vec_step")
        var_ready = m.sem(tag + "var_ready")
        std_ready = m.sem(tag + "std_ready")
        xn_ready = m.sem(tag + "xn_ready")
        xn_kept = m.sem(tag + "xn_kept")
        xT_done = m.sem(tag + "xT_done")
        xT_ready = m.sem(tag + "xT_ready")
        xT_kept = m.sem(tag + "xT_kept")
        lg_done = m.sem(tag + "lg_done")
        lg_kept = m.sem(tag + "lg_kept")
        with nc.Block() as block:
            @block.sync
            def _(sp):
                if load is not None:
                    for dst, src in load:
                        sp.dma_start(dst, src).then_inc(loaded, 16)

            @block.vector
            def _(v):
                st = Steps(own, NT)

                def done(ins):
                    ins.then_inc(own, 1)
                    v.wait_ge(own, st.value())

                if load is not None:
                    v.wait_ge(loaded, 16 * len(load))
                with v.Fori(0, NT // 8) as r:
                    for i in range(8):
                        t = r * 8 + i
                        nc.vector.bn_stats(stats[:, bass.ds(t, 1), :], x_all[:, bass.ds(t, 1), :]).then_inc(own, 1)
                v.wait_ge(own, NT)
                done(nc.vector.tensor_tensor(mean[:, :], stats[:, :, 1], stats[:, :, 4], ALU.subtract))
                done(nc.vector.tensor_tensor(rstd[:, :], mean[:, :], mean[:, :], ALU.mult))
                done(nc.vector.tensor_scalar(rstd[:, :], rstd[:, :], 0.25, EPS, ALU.mult, ALU.add))
                done(nc.vector.tensor_tensor(mean[:, :], stats[:, :, 2], stats[:, :, 5], ALU.add))
                done(nc.vector.tensor_scalar(mean[:, :], mean[:, :], 1.0 / D, None, ALU.mult))
                nc.vector.tensor_tensor(rstd[:, :], rstd[:, :], mean[:, :], ALU.add).then_inc(var_ready, 1)
                done(nc.vector.tensor_tensor(mean2[:, :], stats[:, :, 1], stats[:, :, 4], ALU.add))
                done(nc.vector.tensor_scalar(mean2[:, :], mean2[:, :], 0.5, None, ALU.mult))
                v.wait_ge(std_ready, 1)
                done(nc.vector.reciprocal(rstd[:, :], rstd[:, :]))
                def group(half):
                    g = half * 2
                    for i in range(2):
                        v.wait_ge(xT_done, g)
                        if xn_all is not None:
                            v.wait_ge(xn_kept, g)
                        for j in range(TPG):
                            t = (g + i) * TPG + j
                            ins = nc.vector.tensor_scalar(xn[i][:, j, :], x_all[:, bass.ds(t, 1), :],
                                                          mean2[:, bass.ds(t, 1)], rstd[:, bass.ds(t, 1)],
                                                          ALU.subtract, ALU.mult)
                        ins.then_inc(xn_ready, 1)
                    for i in range(2):
                        v.wait_ge(lg_done, g + i + 1)
                        nc.vector.tensor_copy(logits[:, bass.ds((g + i) * TPG, TPG), :], ps_l[i][:, :, :]).then_inc(lg_kept, 1)

                rolled(v, NG // 2, group)
                v.wait_ge(lg_kept, NG)

            @block.scalar
            def _(a):
                a.wait_ge(var_ready, 1)
                nc.scalar.activation(rstd[:, :], rstd[:, :], ACT.Sqrt).then_inc(std_ready, 1)
                def group(half):
                    g = half * 2
                    for i in range(2):
                        a.wait_ge(xT_done, g + i + 1)
                        a.wait_ge(xT_kept, g)
                        nc.scalar.activation(xT[i][:, :], ps_t[i][:, :], ACT.Copy).then_inc(xT_ready, 1)

                rolled(a, NG // 2, group)
                a.wait_ge(xT_ready, NG)

            @block.tensor
            def _(pe):
                if load is not None:
                    pe.wait_ge(loaded, 16 * len(load))
                def group(half):
                    g = half * 2
                    for i in range(2):
                        pe.wait_ge(xn_ready, g + i + 1)
                        for j in range(TPG):
                            ins = nc.tensor.transpose(ps_t[i][:, j * P:(j + 1) * P], xn[i][:, j, :], ident[:, :])
                        ins.then_inc(xT_done, 1)
                    for i in range(2):
                        pe.wait_ge(xT_ready, g + i + 1)
                        pe.wait_ge(lg_kept, g)
                        for j in range(TPG):
                            ins = nc.tensor.matmul(ps_l[i][:, j, :], xT[i][:, j * P:(j + 1) * P], router[:, :],
                                                   start=True, stop=True)
                        ins.then_inc(lg_done, 1)

                rolled(pe, NG // 2, group)

            @block.gpsimd
            def _(pool):
                def group(half):
                    g = half * 2
                    for i in range(2):
                        if xn_all is not None:
                            pool.wait_ge(xn_ready, g + i + 1)
                            nc.gpsimd.tensor_copy(xn_all[:, bass.ds((g + i) * TPG, TPG), :], xn[i][:, :, :]).then_inc(xn_kept, 1)
                    for i in range(2):
                        pool.wait_ge(xT_ready, g + i + 1)
                        nc.gpsimd.tensor_copy(xnT_all[:, bass.ds((g + i) * GT, GT)], xT[i][:, :]).then_inc(xT_kept, 1)

                rolled(pool, NG // 2, group)
                pool.wait_ge(xT_kept, NG)
                if xn_all is not None:
                    pool.wait_ge(xn_kept, NG)


def bc(ap, axis, n):
    shape = list(ap.shape)
    shape.insert(axis, n)
    return ap.unsqueeze(axis).to_broadcast(shape)


def top2_steps(nc, v, done, soft, iota_e, m, tag, exp_start, exp_done):
    shape = [P, NT, E]
    mx = m.sb(tag + "mx", [P, NT])
    done(nc.vector.reduce_max(mx[:, :], soft[:, :, :], AX.X))
    nc.vector.tensor_tensor(soft[:, :, :], soft[:, :, :], bc(mx[:, :], 2, E), ALU.subtract).then_inc(exp_start, 1)
    v.wait_ge(exp_done, 1)
    done(nc.vector.reduce_sum(mx[:, :], soft[:, :, :], AX.X))
    done(nc.vector.reciprocal(mx[:, :], mx[:, :]))
    done(nc.vector.tensor_tensor(soft[:, :, :], soft[:, :, :], bc(mx[:, :], 2, E), ALU.mult))
    picks = []
    rest = soft
    for k in range(2):
        gate = m.sb(f"{tag}gate{k}", [P, NT])
        idx = m.sb(f"{tag}idx{k}", [P, NT])
        hot = m.sb(f"{tag}hot{k}", shape)
        cand = m.sb(f"{tag}cand{k}", shape)
        done(nc.vector.reduce_max(gate[:, :], rest[:, :, :], AX.X))
        done(nc.vector.tensor_tensor(hot[:, :, :], rest[:, :, :], bc(gate[:, :], 2, E), ALU.is_equal))
        done(nc.vector.tensor_scalar(cand[:, :, :], hot[:, :, :], -16.0, None, ALU.mult))
        done(nc.vector.tensor_tensor(cand[:, :, :], cand[:, :, :], bc(iota_e[:, :], 1, NT), ALU.add))
        done(nc.vector.tensor_reduce(idx[:, :], cand[:, :, :], AX.X, ALU.min))
        done(nc.vector.tensor_tensor(hot[:, :, :], cand[:, :, :], bc(idx[:, :], 2, E), ALU.is_equal))
        done(nc.vector.tensor_scalar(idx[:, :], idx[:, :], 16.0, None, ALU.add))
        picks.append((hot, idx, gate))
        if k == 0:
            rest = m.sb(tag + "rest", shape)
            done(nc.vector.tensor_tensor(cand[:, :, :], soft[:, :, :], hot[:, :, :], ALU.mult))
            done(nc.vector.tensor_tensor(rest[:, :, :], soft[:, :, :], cand[:, :, :], ALU.subtract))
    return picks


def ffn0_stage(nc, x_all, xnT_all, logits, router_b, W1, b1, W2, b2, ident, iota_e):
    with Pool(nc) as m:
        w1 = m.sb("f0w1", [P, FC0, P])
        w2 = m.sb("f0w2", [P, FC0, D])
        b1c = m.sb("f0b1", [P, FC0])
        b2s = m.sb("f0b2", [E, D])
        rb = m.sb("f0rb", [P, E])
        wt = m.sb("f0wt", [P, NT, E])
        wx = m.sb("f0wx", [P, TPG, E, FF0 // E])
        wT = m.sb("f0wT", [E, GT])
        h = m.sb("f0h", [P, FC0, GT])
        hw = m.sb("f0hw", [P, FC0, GT])
        den = m.sb("f0den", [P, NT])
        ps_h = [m.ps(f"f0ps_h{i}") for i in range(FC0)]
        ps_w = [m.ps(f"f0ps_w{i}") for i in range(2)]
        ps_t = m.ps("f0ps_t")
        ps_y = m.ps("f0ps_y", (P, TPG, D))
        loaded = m.sem("f0loaded")
        own = m.sem("f0vec_step")
        exp_start = m.sem("f0exp_start")
        exp_done = m.sem("f0exp_done")
        h_done = m.sem("f0h_done")
        h_ready = m.sem("f0h_ready")
        wt_ready = m.sem("f0wt_ready")
        wx_ready = m.sem("f0wx_ready")
        wT_done = m.sem("f0wT_done")
        wT_ready = m.sem("f0wT_ready")
        w_done = m.sem("f0w_done")
        hw_ready = m.sem("f0hw_ready")
        y_done = m.sem("f0y_done")
        y_added = m.sem("f0y_added")
        NL = 6
        with nc.Block() as block:
            @block.sync
            def _(sp):
                sp.dma_start(rb[:, :], router_b.partition_broadcast(P)).then_inc(loaded, 16)
                for e in range(E):
                    c, o = divmod(e * (FF0 // E), P)
                    if e == 0:
                        sp.dma_start(w1[:, :, :].rearrange("p c (e f) -> p (c e) f", e=EPC),
                                     W1.rearrange("e d f -> d e f")).then_inc(loaded, 16)
                sp.dma_start(w2[:, :, :], W2.rearrange("e f d -> (e f) d").rearrange("(c p) d -> p c d", p=P)).then_inc(loaded, 16)
                sp.dma_start(b1c[:, :], b1.rearrange("(c e) f -> (e f) c", e=EPC), allow_slow_non_contiguous=True).then_inc(loaded, 16)
                sp.dma_start(b2s[:, :], b2).then_inc(loaded, 16)

            @block.vector
            def _(v):
                st = Steps(own)

                def done(ins):
                    ins.then_inc(own, 1)
                    v.wait_ge(own, st.value())

                v.wait_ge(loaded, 16 * 5)
                done(nc.vector.tensor_tensor(wt[:, :, :], logits[:, :, :], bc(rb[:, :], 1, NT), ALU.add))
                (hot1, _, g1), (hot2, _, g2) = top2_steps(nc, v, done, wt, iota_e, m, "f0", exp_start, exp_done)
                done(nc.vector.tensor_tensor(den[:, :], g1[:, :], g2[:, :], ALU.add))
                done(nc.vector.reciprocal(den[:, :], den[:, :]))
                done(nc.vector.tensor_tensor(g1[:, :], g1[:, :], den[:, :], ALU.mult))
                done(nc.vector.tensor_tensor(g2[:, :], g2[:, :], den[:, :], ALU.mult))
                done(nc.vector.tensor_tensor(hot1[:, :, :], hot1[:, :, :], bc(g1[:, :], 2, E), ALU.mult))
                done(nc.vector.tensor_tensor(hot2[:, :, :], hot2[:, :, :], bc(g2[:, :], 2, E), ALU.mult))
                nc.vector.tensor_tensor(wt[:, :, :], hot1[:, :, :], hot2[:, :, :], ALU.add).then_inc(wt_ready, 1)

                def group(g):
                    for c in range(FC0):
                        v.wait_ge(h_ready, g * FC0 + c + 1)
                        v.wait_ge(w_done, g * FC0 + c + 1)
                        nc.vector.tensor_tensor(hw[:, c, :], h[:, c, :], ps_w[c % 2][:, :], ALU.mult).then_inc(hw_ready, 1)
                    v.wait_ge(y_done, g + 1)
                    xs = x_all[:, bass.ds(g * TPG, TPG), :]
                    nc.vector.tensor_tensor(xs, xs, ps_y[:, :, :], ALU.add).then_inc(y_added, 1)

                rolled(v, NG, group)
                v.wait_ge(y_added, NG)

            @block.scalar
            def _(a):
                a.wait_ge(exp_start, 1)
                nc.scalar.activation(wt[:, :, :], wt[:, :, :], ACT.Exp).then_inc(exp_done, 1)
                a.wait_ge(loaded, 16 * 5)
                a.wait_ge(wt_ready, 1)
                def group(g):
                    a.wait_ge(w_done, g * FC0)
                    nc.scalar.activation(wx[:, :, :, :], bc(wt[:, bass.ds(g * TPG, TPG), :], 3, FF0 // E), ACT.Copy).then_inc(wx_ready, 1)
                    a.wait_ge(wT_done, g + 1)
                    nc.scalar.activation(wT[:, :], ps_t[0:E, :], ACT.Copy).then_inc(wT_ready, 1)
                    for c in range(FC0):
                        a.wait_ge(h_done, g * FC0 + c + 1)
                        a.wait_ge(hw_ready, g * FC0)
                        nc.scalar.activation(h[:, c, :], ps_h[c][:, :], ACT.Gelu, bias=b1c[:, c:c + 1]).then_inc(h_ready, 1)

                rolled(a, NG, group)

            @block.tensor
            def _(pe):
                pe.wait_ge(loaded, 16 * 5)
                def hidden(g):
                    for c in range(FC0):
                        pe.wait_ge(h_ready, g * FC0)
                        nc.tensor.matmul(ps_h[c][:, :], w1[:, c, :], xnT_all[:, bass.ds(g * GT, GT)],
                                         start=True, stop=True).then_inc(h_done, 1)

                def group(g, last=False):
                    pe.wait_ge(wx_ready, g + 1)
                    for j in range(TPG):
                        ins = nc.tensor.transpose(ps_t[0:E, j * P:(j + 1) * P], wx[:, j, :, 0], ident[:, :])
                    ins.then_inc(wT_done, 1)
                    for c in range(FC0):
                        if c >= 2:
                            pe.wait_ge(hw_ready, up(g * FC0 + c - 1))
                        for j in range(TPG):
                            gates = wx[:, j, c * EPC:(c + 1) * EPC, :].rearrange("p e f -> p (e f)")
                            ins = nc.tensor.transpose(ps_w[c % 2][:, j * P:(j + 1) * P], gates, ident[:, :])
                        ins.then_inc(w_done, 1)
                    if not last:
                        hidden(g + 1)
                    pe.wait_ge(wT_ready, g + 1)
                    pe.wait_ge(hw_ready, (g + 1) * FC0)
                    pe.wait_ge(y_added, g)
                    for j in range(TPG):
                        for c in range(FC0):
                            nc.tensor.matmul(ps_y[:, j, :], hw[:, c, j * P:(j + 1) * P], w2[:, c, :],
                                             start=(c == 0), stop=False)
                        ins = nc.tensor.matmul(ps_y[:, j, :], wT[:, j * P:(j + 1) * P], b2s[:, :], start=False, stop=True)
                    ins.then_inc(y_done, 1)

                hidden(0)
                rolled(pe, NG - 1, group)
                group(NG - 1, last=True)


def attn0_stage(nc, x_all, xnT_all, Wq, Wk, Wv, Wo, mask, one, zeros, clear):
    HB = T + P
    with Pool(nc) as m:
        w_in = m.sb("a0w_in", [P, 3, H0 * DK])
        w_out = m.sb("a0w_out", [P, PAIRS, D])
        w_qk = m.sb("a0w_qk", [P, 2, P])
        w_v = m.sb("a0w_v", [P, P])
        xb = m.sb("a0xb", [P, T])
        qk = m.sb("a0qk", [P, 2, T])
        vv = m.sb("a0v", [P, 2, P])
        AT = [m.sb(f"a0AT{i}", [P, HB]) for i in range(2)]
        MT = [m.sb(f"a0MT{i}", [P, HB]) for i in range(2)]
        oT = m.sb("a0oT", [P, PAIRS, T])
        ps_qk = m.ps("a0ps_qk", (P, 2, T))
        ps_v = m.ps("a0ps_v", (P, 2, P))
        ps_A = [m.ps(f"a0ps_A{i}") for i in range(2)]
        ps_M = [m.ps(f"a0ps_M{i}") for i in range(2)]
        ps_o = m.ps("a0ps_o")
        ps_y = m.ps("a0ps_y", (P, 2, D))
        loaded = m.sem("a0loaded")
        zero_ready, zeroed = m.sem("a0zero_ready"), m.sem("a0zeroed")
        xb_ready = m.sem("a0xb_ready")
        wqk_ready = m.sem("a0wqk_ready")
        wv_ready = m.sem("a0wv_ready")
        qk_done, qk_ready = m.sem("a0qk_done"), m.sem("a0qk_ready")
        v_done, v_ready = m.sem("a0v_done"), m.sem("a0v_ready")
        A_done, A_ready = m.sem("a0A_done"), m.sem("a0A_ready")
        M_done, M_ready = m.sem("a0M_done"), m.sem("a0M_ready")
        o_done, o_ready = m.sem("a0o_done"), m.sem("a0o_ready")
        y_done, y_added = m.sem("a0y_done"), m.sem("a0y_added")
        with nc.Block() as block:
            @block.sync
            def _(sp):
                for i, w in enumerate((Wq, Wk, Wv)):
                    sp.dma_start(w_in[:, i, :], w).then_inc(loaded, 16)
                sp.dma_start(w_out[:, :, :], Wo.rearrange("(c p) d -> p c d", p=P)).then_inc(loaded, 16)
                sp.wait_ge(zero_ready, 1)
                clear(sp, zeroed)
                sp.wait_ge(zeroed, 16 * CLEARS)

            @block.gpsimd
            def _(pool):
                def copy(dst, src):
                    return nc.gpsimd.tensor_tensor(dst, src, one[:, :].to_broadcast([P, P]) if len(dst.shape) == 2
                                                   else bc(one[:, :].to_broadcast([P, P]), 1, 2), ALU.mult)

                pool.wait_ge(loaded, 16 * 4)
                def batch(b):
                    pool.wait_ge(v_done, b * PAIRS)
                    nc.gpsimd.tensor_copy(xb[:, :], xnT_all[:, bass.ds(b * T, T)]).then_inc(xb_ready, 1)

                    def pair(p):
                        pool.wait_ge(qk_done, b * PAIRS + p)
                        copy(w_qk[:, :, :], w_in[:, 0:2, bass.ds(p * P, P)]).then_inc(wqk_ready, 1)
                        pool.wait_ge(v_done, b * PAIRS + p)
                        copy(w_v[:, :], w_in[:, 2, bass.ds(p * P, P)]).then_inc(wv_ready, 1)

                    rolled(pool, PAIRS, pair)

                rolled(pool, B, batch)

            @block.tensor
            def _(pe):
                def project_qk(b, p):
                    pe.wait_ge(wqk_ready, b * PAIRS + p + 1)
                    for i in range(2):
                        ins = nc.tensor.matmul(ps_qk[:, i, :], w_qk[:, i, :], xnT_all[:, bass.ds(b * T, T)],
                                               start=True, stop=True)
                    ins.then_inc(qk_done, 1)

                def scores(b, p):
                    pe.wait_ge(qk_ready, b * PAIRS + p + 1)
                    for h in range(2):
                        r = slice(h * DK, (h + 1) * DK)
                        nc.tensor.matmul(ps_A[h][:, 0:T], qk[r, 1, 0:P], qk[r, 0, :], start=True, stop=True)
                        nc.tensor.matmul(ps_A[h][:, T:HB], qk[r, 1, P:T], qk[r, 0, P:T],
                                         start=True, stop=True).then_inc(A_done, 1)

                def values(b, p):
                    pe.wait_ge(wv_ready, b * PAIRS + p + 1)
                    pe.wait_ge(xb_ready, b + 1)
                    for j in range(2):
                        ins = nc.tensor.matmul(ps_v[:, j, :], xb[:, j * P:(j + 1) * P], w_v[:, :], start=True, stop=True)
                    ins.then_inc(v_done, 1)

                def squares(b, p):
                    for h in range(2):
                        pe.wait_ge(A_ready, (b * PAIRS + p) * 2 + h + 1)
                        nc.tensor.matmul(ps_M[h][:, 0:T], AT[h][:, 0:P], AT[h][:, 0:T], start=True, stop=True)
                        nc.tensor.matmul(ps_M[h][:, T:HB], AT[h][:, P:T], AT[h][:, P:T], start=True, stop=False)
                        nc.tensor.matmul(ps_M[h][:, T:HB], AT[h][:, T:HB], AT[h][:, T:HB],
                                         start=False, stop=True).then_inc(M_done, 1)

                def outputs(b, p):
                    pe.wait_ge(o_ready, b * PAIRS + p + 1)
                    pe.wait_ge(v_ready, b * PAIRS + p + 1)
                    rows = [slice(h * DK, (h + 1) * DK) for h in range(2)]
                    for h, r in enumerate(rows):
                        pe.wait_ge(M_ready, (b * PAIRS + p) * 2 + h + 1)
                        nc.tensor.matmul(ps_o[r, 0:T], vv[:, 0, r], MT[h][:, 0:T], start=True, stop=False)
                    for h, r in enumerate(rows):
                        ins = nc.tensor.matmul(ps_o[r, P:T], vv[:, 1, r], MT[h][:, T:HB], start=False, stop=True)
                    ins.then_inc(o_done, 1)

                pe.wait_ge(loaded, 16 * 4)
                def batch(b):
                    project_qk(b, 0)
                    scores(b, 0)
                    project_qk(b, 1)
                    values(b, 0)
                    squares(b, 0)
                    with pe.Fori(1, PAIRS - 1) as p:
                        scores(b, p)
                        project_qk(b, p + 1)
                        outputs(b, p - 1)
                        values(b, p)
                        squares(b, p)
                    last = PAIRS - 1
                    scores(b, last)
                    outputs(b, last - 1)
                    values(b, last)
                    squares(b, last)
                    outputs(b, last)
                    pe.wait_ge(y_added, b)
                    for j in range(2):
                        for p in range(PAIRS):
                            if j == 0 and p in (0, last):
                                pe.wait_ge(o_ready, b * PAIRS + (last if p == 0 else PAIRS) + 1)
                            ins = nc.tensor.matmul(ps_y[:, j, :], oT[:, p, j * P:(j + 1) * P], w_out[:, p, :],
                                                   start=(p == 0), stop=(p == last))
                    ins.then_inc(y_done, 1)

                rolled(pe, B, batch)

            @block.scalar
            def _(a):
                nc.scalar.sem_inc(o_ready, 1)

                def keep_qk(b, p):
                    a.wait_ge(qk_done, b * PAIRS + p + 1)
                    nc.scalar.activation(qk[:, :, :], ps_qk[:, :, :], ACT.Copy).then_inc(qk_ready, 1)

                def keep_v(b, p):
                    a.wait_ge(v_done, b * PAIRS + p + 1)
                    nc.scalar.activation(vv[:, :, :], ps_v[:, :, :], ACT.Copy).then_inc(v_ready, 1)

                def keep_o(b, p):
                    a.wait_ge(o_done, b * PAIRS + p + 1)
                    a.wait_ge(y_done, b)
                    nc.scalar.activation(oT[:, bass.ds(p, 1), :], ps_o[:, 0:T], ACT.Copy).then_inc(o_ready, 1)

                def batch(b):
                    keep_qk(b, 0)
                    keep_qk(b, 1)
                    keep_v(b, 0)
                    with a.Fori(1, PAIRS - 1) as p:
                        keep_qk(b, p + 1)
                        keep_o(b, p - 1)
                        keep_v(b, p)
                    keep_o(b, PAIRS - 2)
                    keep_v(b, PAIRS - 1)
                    keep_o(b, PAIRS - 1)

                rolled(a, B, batch)

            @block.vector
            def _(v):
                nc.vector.memset(zeros[:, :, :], 0.0).then_inc(zero_ready, 1)

                def batch(b):
                    with v.Fori(0, PAIRS) as p:
                        for h in range(2):
                            v.wait_ge(A_done, (b * PAIRS + p) * 2 + h + 1)
                            nc.vector.tensor_tensor(AT[h][:, :], ps_A[h][:, 0:HB], mask[:, :], ALU.mult).then_inc(A_ready, 1)
                        for h in range(2):
                            v.wait_ge(M_done, (b * PAIRS + p) * 2 + h + 1)
                            nc.vector.tensor_tensor(MT[h][:, :], ps_M[h][:, 0:HB], mask[:, :], ALU.mult).then_inc(M_ready, 1)
                    v.wait_ge(y_done, b + 1)
                    xs = x_all[:, bass.ds(b * 2, 2), :]
                    nc.vector.tensor_tensor(xs, xs, ps_y[:, :, :], ALU.add).then_inc(y_added, 1)

                rolled(v, B, batch)
                v.wait_ge(y_added, B)


CAP = (int(2.0 * GT / E) + 3) // 4 * 4
HID = int(8.0 * D) * 2 // 3
HID = HID + (8 - HID) % 8
HC = -(-HID // P)
SLOTS = E * NG * CAP
ET = NG * CAP
DROPPED = float(2 * SLOTS)


def hrows(c):
    return min(P, HID - c * P)


ZW = 16
ZH = SLOTS // P * ZW // (P - 1)
CLEARS = D // ZW + 2 * 16 // ZH


def clear_dram(sp, zeros, slots_dram, skew, zeroed):
    for z in range(D // ZW):
        sp.dma_start(slots_dram.rearrange("(p s) d -> p s d", p=P)[:, :, z * ZW:(z + 1) * ZW],
                     zeros[:, :, :]).then_inc(zeroed, 16)
    some = zeros[:, :, :].rearrange("p a b -> p (a b)")[:, 0:ZH * (P - 1)].rearrange("p (h c) -> p h c", h=ZH)
    for h in range(0, H1, ZH):
        sp.dma_start(skew[0][:, h:h + ZH, BAND:PITCH], some).then_inc(zeroed, 16)
        sp.dma_start(skew[1][:, h:h + ZH, 0:P - 1], some).then_inc(zeroed, 16)


def gate1_stage(nc, logits, iota_e, ltri, ones_bf, gates, slot_ids, send_ids, group_base):
    with Pool(nc) as m:
        soft = m.sb("g1soft", [P, NT, E])
        hotb = [m.sb(f"g1hotb{k}", [P, NT, E], BF16) for k in range(2)]
        keptb = m.sb("g1keptb", [P, NT, E], BF16)
        kept = m.sb("g1kept", [P, NT, E])
        place = m.sb("g1place", [P, NT, E])
        pos = m.sb("g1pos", [P, NT])
        flat = m.sb("g1flat", [P, NT])
        slot = m.sb("g1slot", [P, NT])
        gone = m.sb("g1gone", [P, NT])
        ps_p = [m.ps(f"g1ps_p{k}", (P, TPG, NG, E)) for k in range(2)]
        own = m.sem("g1vec_step")
        exp_start, exp_done = m.sem("g1exp_start"), m.sem("g1exp_done")
        hot_ready, kept_ready = m.sem("g1hot_ready"), m.sem("g1kept_ready")
        place_done = m.sem("g1place_done")
        ids_ready = m.sem("g1ids_ready")
        with nc.Block() as block:
            @block.vector
            def _(v):
                st = Steps(own)

                def done(ins):
                    ins.then_inc(own, 1)
                    v.wait_ge(own, st.value())

                done(nc.vector.tensor_copy(soft[:, :, :], logits[:, :, :]))
                picks = top2_steps(nc, v, done, soft, iota_e, m, "g1", exp_start, exp_done)
                for k in range(2):
                    nc.vector.tensor_copy(hotb[k][:, :, :], picks[k][0][:, :, :]).then_inc(hot_ready, 1)
                for k in range(2):
                    hot, idx, gate = picks[k]
                    v.wait_ge(place_done, k + 1)
                    done(nc.vector.tensor_copy(place[:, :, :].rearrange("p (g q) e -> p q g e", q=TPG), ps_p[k][:, :, :, :]))
                    done(nc.vector.tensor_scalar(kept[:, :, :], place[:, :, :], float(CAP), None, ALU.is_lt))
                    done(nc.vector.tensor_tensor(kept[:, :, :], kept[:, :, :], hot[:, :, :], ALU.mult))
                    if k == 0:
                        nc.vector.tensor_copy(keptb[:, :, :], kept[:, :, :]).then_inc(kept_ready, 1)
                    done(nc.vector.tensor_tensor(place[:, :, :], place[:, :, :], kept[:, :, :], ALU.mult))
                    done(nc.vector.reduce_sum(pos[:, :], place[:, :, :], AX.X))
                    done(nc.vector.reduce_sum(flat[:, :], kept[:, :, :], AX.X))
                    done(nc.vector.tensor_scalar(slot[:, :], idx[:, :], float(ET), None, ALU.mult))
                    done(nc.vector.tensor_tensor(slot[:, :], slot[:, :], pos[:, :], ALU.add))
                    done(nc.vector.tensor_tensor(slot[:, :], slot[:, :], group_base[:, :], ALU.add))
                    done(nc.vector.tensor_tensor(gates[:, k, :], gate[:, :], flat[:, :], ALU.mult))
                    done(nc.vector.tensor_tensor(pos[:, :], slot[:, :], flat[:, :], ALU.mult))
                    done(nc.vector.tensor_copy(slot_ids[:, k, :], pos[:, :]))
                    done(nc.vector.tensor_scalar(gone[:, :], flat[:, :], -DROPPED, DROPPED, ALU.mult, ALU.add))
                    done(nc.vector.tensor_tensor(slot[:, :], slot[:, :], gone[:, :], ALU.add))
                    nc.vector.tensor_copy(send_ids[:, k, :], slot[:, :]).then_inc(ids_ready, 1)
                v.wait_ge(ids_ready, 2)

            @block.scalar
            def _(a):
                a.wait_ge(exp_start, 1)
                nc.scalar.activation(soft[:, :, :], soft[:, :, :], ACT.Exp).then_inc(exp_done, 1)

            @block.tensor
            def _(pe):
                def tiles(t, q):
                    return t[:, :, :].rearrange("p (g q) e -> p q g e", q=TPG)[:, q, :, :]

                for k in range(2):
                    pe.wait_ge(hot_ready, k + 1)
                    if k == 1:
                        pe.wait_ge(kept_ready, 1)
                    for q in range(TPG):
                        terms = [(ltri, hotb[k], q)] + [(ones_bf, hotb[k], r) for r in range(q)]
                        if k == 1:
                            terms += [(ones_bf, keptb, r) for r in range(TPG)]
                        for n, (w, src, r) in enumerate(terms):
                            ins = nc.tensor.matmul(ps_p[k][:, q, :, :], w[:, :], tiles(src, r),
                                                   start=(n == 0), stop=(n == len(terms) - 1))
                    ins.then_inc(place_done, 1)


def ffn1_stage(nc, w0_d, w1_d, wo_d, slots_dram, eo_dram, xn_all, send_ids, ident):
    GH = NG // 2
    N = GH * CAP
    PAIRS1 = 2 * E // 2
    with Pool(nc) as m:
        w0 = [m.sb(f"f1w0{i}", [P, HID]) for i in range(2)]
        w1 = [m.sb(f"f1w1{i}", [P, HID]) for i in range(2)]
        wo = [m.sb(f"f1wo{i}", [P, HC, D]) for i in range(2)]
        xe = [m.sb(f"f1xe{i}", [P, GH, D]) for i in range(2)]
        xT = [m.sb(f"f1xT{i}", [P, N]) for i in range(2)]
        ge = m.sb("f1ge", [P, 2, N])
        hid = m.sb("f1hid", [P, HC, N])
        eo = [m.sb(f"f1eo{i}", [P, GH, D]) for i in range(2)]
        ps_t = [m.ps(f"f1ps_t{i}") for i in range(2)]
        ps_a = [m.ps(f"f1ps_a{i}") for i in range(2)]
        ps_b = [m.ps(f"f1ps_b{i}") for i in range(2)]
        ps_o = [m.ps(f"f1ps_o{i}", (P, GH, D)) for i in range(2)]
        loaded = [m.sem(f"f1loaded{i}") for i in range(2)]
        xT_done, xT_ready = m.sem("f1xT_done"), m.sem("f1xT_ready")
        a_done, a_ready = m.sem("f1a_done"), m.sem("f1a_ready")
        b_done, hid_ready = m.sem("f1b_done"), m.sem("f1hid_ready")
        o_done, o_ready = m.sem("f1o_done"), m.sem("f1o_ready")
        stored = [m.sem(f"f1stored{i}") for i in range(2)]
        sent = m.sem("f1sent")
        NL = 5
        xs_v = slots_dram.rearrange("(e g p) d -> e p g d", e=E, p=P)
        eo_v = eo_dram.rearrange("(e g p) d -> e p g d", e=E, p=P)
        full = (HC - 1) * P
        with nc.Block() as block:
            @block.sync
            def _(sp):
                def experts(half, r):
                    for i in range(2):
                        e = r * 2 + i
                        g = slice(half * GH, (half + 1) * GH)
                        sp.wait_ge(o_done, up(half * E + e - 1))
                        sp.dma_start(w0[i][:, :], w0_d[bass.ds(e, 1)]).then_inc(loaded[i], 16)
                        sp.dma_start(w1[i][:, :], w1_d[bass.ds(e, 1)]).then_inc(loaded[i], 16)
                        sp.dma_start(wo[i][:, 0:HC - 1, :], wo_d[bass.ds(e, 1), 0:full].rearrange("a (c p) d -> p (a c) d", p=P)).then_inc(loaded[i], 16)
                        sp.dma_start(wo[i][0:HID - full, HC - 1, :], wo_d[bass.ds(e, 1), full:HID]).then_inc(loaded[i], 16)
                        sp.dma_start(xe[i][:, :, :], xs_v[bass.ds(e, 1), :, g, :]).then_inc(loaded[i], 16)

                rolled(sp, E // 2, lambda r: experts(0, r))
                sp.wait_ge(sent, 16 * NT)
                rolled(sp, E // 2, lambda r: experts(1, r))

            @block.gpsimd
            def _(pool):
                def experts(half, r):
                    for i in range(2):
                        e = r * 2 + i
                        pool.wait_ge(o_ready, half * E + e + 1)
                        pool.dma_start(eo_v[bass.ds(e, 1), :, half * GH:(half + 1) * GH, :], eo[i][:, :, :]).then_inc(stored[i], 16)

                scatter(nc, slots_dram, xn_all, send_ids, range(NT // 2, NT), sent)
                pool.wait_ge(sent, 16 * NT)
                for half in range(2):
                    rolled(pool, E // 2, lambda r: experts(half, r))
                for i in range(2):
                    pool.wait_ge(stored[i], 16 * PAIRS1)

            @block.tensor
            def _(pe):
                def transposes(R, i):
                    pe.wait_ge(loaded[i], (R + 1) * (16 * NL))
                    pe.wait_ge(xT_ready, up(R * 2 + i - 1))
                    for g in range(GH):
                        ins = nc.tensor.transpose(ps_t[i][:, g * P:(g + 1) * P], xe[i][:, g, :], ident[:, :])
                    ins.then_inc(xT_done, 1)

                def step(R, i, last=False):
                    q = R * 2 + i
                    pe.wait_ge(xT_ready, q + 1)
                    for u in range(HC):
                        n = hrows(u)
                        pe.wait_ge(a_ready, up(q * HC + u - 1))
                        pe.wait_ge(hid_ready, up(q * HC + u - 1))
                        nc.tensor.matmul(ps_a[u % 2][0:n, :], w0[i][:, u * P:u * P + n], xT[i][:, :], start=True, stop=True).then_inc(a_done, 1)
                        nc.tensor.matmul(ps_b[u % 2][0:n, :], w1[i][:, u * P:u * P + n], xT[i][:, :], start=True, stop=True).then_inc(b_done, 1)
                    if not last:
                        transposes(R + i, 1 - i)
                    pe.wait_ge(hid_ready, (q + 1) * HC)
                    pe.wait_ge(o_ready, up(q - 1))
                    for s in range(GH):
                        for c in range(HC):
                            n = hrows(c)
                            ins = nc.tensor.matmul(ps_o[i][:, s, :], hid[0:n, c, s * P:(s + 1) * P], wo[i][0:n, c, :],
                                                   start=(c == 0), stop=(c == HC - 1))
                    ins.then_inc(o_done, 1)

                def pair(R):
                    for i in range(2):
                        step(R, i)

                transposes(0, 0)
                rolled(pe, PAIRS1 - 1, pair)
                step(PAIRS1 - 1, 0)
                step(PAIRS1 - 1, 1, last=True)

            @block.scalar
            def _(a):
                def keep_T(R, i):
                    a.wait_ge(xT_done, R * 2 + i + 1)
                    nc.scalar.activation(xT[i][:, :], ps_t[i][:, :], ACT.Copy).then_inc(xT_ready, 1)

                def step(R, i, last=False):
                    q = R * 2 + i
                    for u in range(HC):
                        n = hrows(u)
                        a.wait_ge(a_done, q * HC + u + 1)
                        a.wait_ge(hid_ready, up(q * HC + u - 1))
                        nc.scalar.activation(ge[0:n, u % 2, :], ps_a[u % 2][0:n, :], ACT.Gelu_apprx_tanh).then_inc(a_ready, 1)
                    if not last:
                        keep_T(R + i, 1 - i)
                    a.wait_ge(o_done, q + 1)
                    a.wait_ge(stored[i], R * 16)
                    nc.scalar.activation(eo[i][:, :, :], ps_o[i][:, :, :], ACT.Copy).then_inc(o_ready, 1)

                def pair(R):
                    for i in range(2):
                        step(R, i)

                keep_T(0, 0)
                rolled(a, PAIRS1 - 1, pair)
                step(PAIRS1 - 1, 0)
                step(PAIRS1 - 1, 1, last=True)

            @block.vector
            def _(v):
                def pair(R):
                    for i in range(2):
                        q = R * 2 + i
                        for u in range(HC):
                            n = hrows(u)
                            v.wait_ge(a_ready, q * HC + u + 1)
                            v.wait_ge(b_done, q * HC + u + 1)
                            nc.vector.tensor_tensor(hid[0:n, u, :], ge[0:n, u % 2, :], ps_b[u % 2][0:n, :], ALU.mult).then_inc(hid_ready, 1)

                rolled(v, PAIRS1, pair)


def scatter(nc, slots_dram, xn_all, send_ids, tiles, sent):
    for t in tiles:
        for k in range(2):
            nc.gpsimd.indirect_dma_start(
                out=slots_dram, out_offset=bass.IndirectOffsetOnAxis(ap=send_ids[:, k, t:t + 1], axis=0),
                in_=xn_all[:, t, :], in_offset=None, bounds_check=SLOTS - 1, oob_is_err=False).then_inc(sent, 16)




H1 = 16
HD = D // H1
REL = 64
NREL = 2 * REL + 1
BAND = P + REL
PITCH = BAND + P - 1
GI = 16
PARTS = 3
KS = PARTS * PARTS * HD
QUAD = 4
QW = QUAD * HD
TAB = 2 * T - 1


STACK = 16 * PARTS * (2 + PARTS)


class Attn1Front:

    def __init__(self, m):
        self.w_in = m.sb("a1w_in", [P, 3, D])
        self.w_out = m.sb("a1w_out", [P, D])
        self.b_out = m.sb("a1b_out", [1, D])
        self.qkf = m.sb("a1qkf", [P, 3, T])
        self.low = m.sb("a1low", [P, 3, T])
        self.prt = m.sb("a1prt", [P, PARTS, 3, T], BF16)
        self.stk = [m.sb(f"a1stk{i}", [KS, 3, H1, T], BF16) for i in range(2)]
        names = ("loaded xb_ready qk_done qk_ready split parts_out stacked0 stacked1 v_done v_ready R_done R_ready skew_out0 skew_out1 "
                 "skew_in00 skew_in01 skew_in10 skew_in11 S_done S_ready P_ready T_done Ta_ready Tv_ready X_done X_ready c_done cT_ready rrep_ready "
                 "rdT_done rdT_ready y_done y_added pool_step vec_step cleared ids_ready rows_in first_added combined")
        self.sm = {n: m.sem("a1" + n) for n in names.split()}
        self.stacked = [self.sm["stacked0"], self.sm["stacked1"]]


def multiply_qk(nc, front, ps_p, xnT_all, n):
    for w in range(2):
        ins = nc.tensor.matmul(ps_p[:, w, :], front.w_in[:, w, :], xnT_all[:, bass.ds(n * T, T)], start=True, stop=True)
    ins.then_inc(front.sm["qk_done"], 1)


def keep_qk(nc, act, front, ps_p, bias_q, bias_k, n):
    act.wait_ge(front.sm["qk_done"], n + 1)
    act.wait_ge(front.sm["split"], n)
    qkf = front.qkf
    nc.scalar.activation(qkf[:, 0, :], ps_p[:, 0, :], ACT.Identity, bias=bias_q[:, 0:1], scale=float(HD) ** -0.5)
    nc.scalar.activation(qkf[:, 1, :], ps_p[:, 1, :], ACT.Identity, bias=bias_k[:, 0:1])
    nc.scalar.activation(qkf[:, 2, :], ps_p[:, 1, :], ACT.Identity, bias=bias_k[:, 1:2]).then_inc(front.sm["qk_ready"], 1)


def split_qk(ops, eng, front, one, n, free, count):
    sm, prt, low = front.sm, front.prt, front.low
    eng.wait_ge(sm["qk_ready"], n + 1)
    eng.wait_ge(free, count)
    src = front.qkf
    for k in range(PARTS):
        ins = ops.tensor_tensor(prt[:, k, :, :], src[:, :, :], bc(one[:, :].to_broadcast([P, T]), 1, 3), ALU.mult)
        if k == PARTS - 1:
            ins.then_inc(sm["split"], 1)
        else:
            ins.then_inc(sm["pool_step"], 1)
            eng.wait_ge(sm["pool_step"], n * 4 + 2 * k + 1)
            ops.tensor_tensor(low[:, :, :], src[:, :, :], prt[:, k, :, :], ALU.subtract).then_inc(sm["pool_step"], 1)
            eng.wait_ge(sm["pool_step"], n * 4 + 2 * k + 2)
            src = low


def send_parts(sp, front, parts, n):
    sp.wait_ge(front.sm["split"], n + 1)
    sp.dma_start(parts, front.prt[:, :, :, :]).then_inc(front.sm["parts_out"], 16)


def stack(sp, front, parts, n, par):
    sp.wait_ge(front.sm["parts_out"], (n + 1) * 16)
    stk = front.stk
    k_rows = parts.rearrange("(h d) k w t -> (d k) w h t", d=HD)
    q_rows = parts.rearrange("(h d) k w t -> d k w h t", d=HD)
    for c in range(PARTS):
        rows = slice(c * PARTS * HD, (c + 1) * PARTS * HD)
        for w in (1, 2):
            sp.dma_start(stk[par][rows, w, :, :], k_rows[:, w, :, :]).then_inc(front.stacked[par], 16)
        for k in range(PARTS):
            sp.dma_start(stk[par][c * PARTS * HD + k:(c + 1) * PARTS * HD:PARTS, 0, :, :],
                         q_rows[:, (k + c) % PARTS, 0, :, :]).then_inc(front.stacked[par], 16)


class TableInputs:

    LOADS = 1 + 3 + 2 * (1 + H1) + 2

    def __init__(self, m):
        self.rk = m.sb("t1rk", [HD, NREL])
        self.rv = m.sb("t1rv", [1, TAB, HD])
        self.edge_v = m.sb("t1edge_v", [P, 2, HD])
        self.edge_k = m.sb("t1edge_k", [P, 2])
        self.bq = m.sb("t1bq", [P, 2])
        self.bv = m.sb("t1bv", [P, D])
        self.loaded = m.sem("t1loaded")


def load_table_inputs(sp, tin, rel_k, rel_v, b_qkv):
    rk, rv, edge_v, edge_k, bq, bv = tin.rk, tin.rv, tin.edge_v, tin.edge_k, tin.bq, tin.bv

    def load(dst, src):
        sp.dma_start(dst, src, allow_slow_non_contiguous=True).then_inc(tin.loaded, 16)

    load(rk[:, :], rel_k.rearrange("m d -> d m"))
    lo = T - 1 - REL
    load(rv[:, 0:lo, :], rel_v[0:1, :].unsqueeze(1).to_broadcast([1, lo, HD]))
    load(rv[:, lo:lo + NREL, :], rel_v.unsqueeze(0))
    load(rv[:, lo + NREL:TAB, :], rel_v[NREL - 1:NREL, :].unsqueeze(1).to_broadcast([1, TAB - lo - NREL, HD]))
    for n, row in enumerate((NREL - 1, 0)):
        load(edge_v[:, n, :], rel_v[row, :].partition_broadcast(P))
        for h in range(H1):
            load(edge_k[h * HD:(h + 1) * HD, n:n + 1], rel_k[row, :].unsqueeze(1))
    load(bq[:, :], b_qkv[0:2 * D].rearrange("(w p) -> p w", p=P))
    load(bv[:, :], b_qkv[2 * D:3 * D].partition_broadcast(P))


def tables1_stage(nc, a, tin, front, xnT_all, xn_all, send_ids, ident, one, bias_q, bias_k, bias_v, rel_st, tabs, pick, fold, ones_row):
    with Pool(nc) as m:
        rk, rv, edge_v, edge_k, bq, bv = tin.rk, tin.rv, tin.edge_v, tin.edge_k, tin.bq, tin.bv
        rpad = m.sb("t1rpad", [HD, 2, BAND])
        rlow = m.sb("t1rlow", [HD, 2, BAND])
        parts = [m.sb(f"t1parts{i}", [HD, 2, BAND], BF16) for i in range(PARTS)]
        rvd = m.sb("t1rvd", [1, 2, TAB, HD])
        own = m.sem("t1step")
        own_p = m.sem("t1pool_step")
        made = m.sem("t1made")
        biased = m.sem("t1biased")
        moved = m.sem("t1moved")
        listed = m.sem("t1listed")
        ps_p = m.ps("t1ps_p", (P, 2, T))
        sent = m.sem("t1sent")
        rv_dram = a["rv_table"]
        with nc.Block() as block:
            @block.sync
            def _(sp):
                to = front.sm["loaded"]
                sp.dma_start(front.w_in[:, :, :], a["L1_attn_W_qkv"].rearrange("d (w n) -> d w n", w=3)).then_inc(to, 16)
                sp.dma_start(front.w_out[:, :], a["L1_attn_W_out"]).then_inc(to, 16)
                sp.dma_start(front.b_out[:, :], a["L1_attn_b_out"].unsqueeze(0)).then_inc(to, 16)
                sp.dma_start(xnT_all[:, B * T:(B + 2) * T], xnT_all[:, 0:2 * T]).then_inc(to, 16)
                sp.wait_ge(made, 1)
                for c in range(PARTS):
                    for k in range(PARTS):
                        sp.dma_start(rel_st[c * PARTS * HD + k:(c + 1) * PARTS * HD:PARTS, :, :], parts[k][:, :, :]).then_inc(moved, 16)
                send_parts(sp, front, a["parts"], 0)
                sp.wait_ge(made, 2)
                sp.dma_start(rv_dram.unsqueeze(0), rvd[:, :, :, :]).then_inc(listed, 16)
                stack(sp, front, a["parts"], 0, 0)
                sp.wait_ge(moved, 16 * (PARTS * PARTS + len(TABLES)))

            @block.tensor
            def _(pe):
                pe.wait_ge(front.sm["loaded"], 16 * 4)
                for n in range(2):
                    pe.wait_ge(front.sm["qk_ready"], n)
                    multiply_qk(nc, front, ps_p, xnT_all, n)

            @block.scalar
            def _(act):
                act.wait_ge(biased, 3)
                keep_qk(nc, act, front, ps_p, bias_q, bias_k, 0)
                keep_qk(nc, act, front, ps_p, bias_q, bias_k, 1)
                act.wait_ge(listed, 16)
                for n, (it, jt, ig) in enumerate(TABLES):
                    first = jt * P - (it * P + ig * GI + GI - 1) + T - 1
                    flat = rv_dram[it].rearrange("t d -> (t d)")
                    src = bass.AP(flat.tensor, flat.offset + first * HD, [[HD, P], [1, P]])
                    act.dma_start(tabs[:, n, :], src).then_inc(moved, 16)

            @block.vector
            def _(v):
                st = Steps(own)

                def done(ins):
                    ins.then_inc(own, 1)
                    v.wait_ge(own, st.value())

                v.wait_ge(tin.loaded, 16 * tin.LOADS)
                nc.vector.tensor_scalar(bias_q[:, :], bq[:, 0:1], float(HD) ** -0.5, None, ALU.mult).then_inc(biased, 1)
                for n in range(2):
                    nc.vector.tensor_tensor(bias_k[:, n:n + 1], bq[:, 1:2], edge_k[:, n:n + 1], ALU.add).then_inc(biased, 1)
                e = NREL - 1
                done(nc.vector.tensor_scalar(rpad[:, 0, REL - 1:BAND], rk[:, :], rk[:, e:e + 1], None, ALU.subtract))
                done(nc.vector.tensor_scalar(rpad[:, 1, 0:NREL], rk[:, :], rk[:, 0:1], None, ALU.subtract))
                done(nc.vector.tensor_copy(rpad[:, 0, 0:REL - 1], rpad[:, 0, REL - 1:REL].to_broadcast([HD, REL - 1])))
                done(nc.vector.tensor_copy(rpad[:, 1, NREL:BAND], rpad[:, 1, NREL - 1:NREL].to_broadcast([HD, REL - 1])))
                done(nc.vector.tensor_copy(parts[0][:, :, :], rpad[:, :, :]))
                done(nc.vector.tensor_tensor(rlow[:, :, :], rpad[:, :, :], parts[0][:, :, :], ALU.subtract))
                done(nc.vector.tensor_copy(parts[1][:, :, :], rlow[:, :, :]))
                done(nc.vector.tensor_tensor(rlow[:, :, :], rlow[:, :, :], parts[1][:, :, :], ALU.subtract))
                nc.vector.tensor_copy(parts[2][:, :, :], rlow[:, :, :]).then_inc(made, 1)
                split_qk(nc.vector, v, front, one, 0, made, 0)
                for n in range(2):
                    row = TAB - 1 if n == 0 else 0
                    ins = nc.vector.tensor_tensor(rvd[:, n, :, :], rv[:, :, :], rv[:, row:row + 1, :].to_broadcast([1, TAB, HD]), ALU.subtract)
                    done(ins)
                    done(nc.vector.tensor_tensor(bias_v[:, n, :, :], bv[:, :].rearrange("p (h d) -> p h d", h=H1),
                                                 bc(edge_v[:, n, :], 1, H1), ALU.add))
                done(nc.vector.memset(fold[:, :, :], 0.0))
                done(nc.vector.memset(ones_row[:, :], 1.0))
                for q in range(QUAD):
                    ins = nc.vector.tensor_reduce(fold[:, q, q * HD:(q + 1) * HD],
                                                  ident[:, :].rearrange("p (r d) -> p d r", d=HD), AX.X, ALU.add)
                ins.then_inc(made, 1)
                v.wait_ge(made, 2)
                split_qk(nc.vector, v, front, one, 1, front.sm["parts_out"], 16)

            @block.gpsimd
            def _(pool):
                nc.gpsimd.memset(pick[:, :], 1.0).then_inc(own_p, 1)
                pool.wait_ge(own_p, 1)
                nc.gpsimd.affine_select(out=pick[:, :], in_=pick[:, :], compare_op=ALU.is_ge, fill=0.0,
                                        base=-(GI - 1) * HD, pattern=[[HD, GI]], channel_multiplier=1).then_inc(own_p, 1)
                pool.wait_ge(own_p, 2)
                nc.gpsimd.affine_select(out=pick[:, :], in_=pick[:, :], compare_op=ALU.is_ge, fill=0.0,
                                        base=GI * HD - 1, pattern=[[-HD, GI]], channel_multiplier=-1).then_inc(own_p, 1)
                pool.wait_ge(own_p, 3)
                scatter(nc, a["slots"], xn_all, send_ids, range(NT // 2), sent)
                pool.wait_ge(sent, 16 * NT)


TABLES = [(it, jt, ig) for it in range(2) for ig in range(P // GI)
          for jt in range(2) if jt == it or (ig >= REL // GI if it == 0 else ig < REL // GI)]


def attn1_stage(nc, front, x_all, xnT_all, a, gates, slot_ids, ident, one, bias_q, bias_k, bias_v, rel_st, tabs, pick, fold, ones_row):
    skew, parts = a["skew"], a["parts"]
    HP = H1 // 2
    S2 = 2 * B
    with Pool(nc) as m:
        w_in, w_out, b_out, prt, stk = front.w_in, front.w_out, front.b_out, front.prt, front.stk
        xb = m.sb("a1xb", [P, T])
        vx = m.sb("a1vx", [P, 2, 2, H1, QW])
        Rt = m.sb("a1Rt", [P, H1, BAND])
        Sb = [m.sb(f"a1Sb{i}", [P, H1, T]) for i in range(2)]
        Pm = m.sb("a1Pm", [P, H1, T])
        nmx = [m.sb(f"a1nmx{i}", [P, H1]) for i in range(2)]
        PT = m.sb("a1PT", [P, 2, H1, P])
        X = m.sb("a1X", [P, H1, P])
        ids = m.sb("a1ids", [P, 2, 1], U32)
        rows = m.sb("a1rows", [P, 2, D])
        pool_taker = m.sb("a1pool_taker", [P, 1])
        taker = m.sb("a1taker", [1, HP])
        den = [m.sb(f"a1den{i}", [P, H1]) for i in range(2)]
        rden = m.sb("a1rden", [P, H1])
        rrep = m.sb("a1rrep", [P, H1, HD])
        rdT = m.sb("a1rdT", [P, P])
        cT = m.sb("a1cT", [P, P])
        ps_p = m.ps("a1ps_p", (P, 2, T))
        ps_R0 = m.ps("a1ps_R", (P, 2, BAND))
        ps_S0 = [m.ps(f"a1ps_S{i}", (P, 2, T)) for i in range(2)]
        ps_T = [m.ps(f"a1ps_T{i}", (P, 2, 2, P)) for i in range(2)]
        ps_R = [ps_R0[:, :, :], ps_T[0][:, :, :, :].rearrange("p a b i -> p (a b i)")[:, 0:2 * BAND].rearrange("p (n c) -> p n c", n=2)]
        ps_TT = [ps_T[0][:, :, :, :], ps_T[1][:, :, :, :]] + [b[:, :, :].rearrange("p a (b i) -> p a b i", b=2) for b in ps_S0]
        ps_S = [ps_S0[0][:, :, :], ps_S0[1][:, :, :], ps_T[1][:, :, :, :].rearrange("p a b i -> p a (b i)")]
        ps_X = [m.ps("a1ps_X", (P, 2, H1, GI))[:, :, :, :], ps_p[:, :, :].rearrange("p n (h i) -> p n h i", h=H1)]
        ps_c = m.ps("a1ps_c", (P, 512))
        ctx_ps, rdT_ps, y_ps = ps_c[:, 0:P], ps_c[:, P:2 * P], ps_c[:, 2 * P:3 * P]
        sm = front.sm
        stacked = [sm["stacked0"], sm["stacked1"]]
        skew_out = [sm["skew_out0"], sm["skew_out1"]]
        skew_in = [[sm[f"skew_in{it}{half}"] for half in range(2)] for it in range(2)]
        HH = H1 // 2

        def steps(eng, step):
            for i in range(4):
                step(0, i)
            with eng.Fori(1, B // 2) as r:
                for i in range(4):
                    step(r, i)

        def tile_of(i):
            i %= 4
            return i % 2, i // 2

        with nc.Block() as block:
            @block.tensor
            def _(pe):
                def project_qk(n):
                    pe.wait_ge(sm["v_ready"], up(n - 1))
                    pe.wait_ge(sm["X_ready"], up((n - 2) * 8 + 4))
                    pe.wait_ge(sm["qk_ready"], n)
                    multiply_qk(nc, front, ps_p, xnT_all, n)

                def project_v(n):
                    pe.wait_ge(sm["xb_ready"], n + 1)
                    pe.wait_ge(sm["qk_ready"], n + 2)
                    pe.wait_ge(sm["X_ready"], n * 8)
                    for j in range(2):
                        ins = nc.tensor.matmul(ps_p[:, 0, j * D:(j + 1) * D], xb[:, j * P:(j + 1) * P], w_in[:, 2, :],
                                               start=True, stop=True)
                    ins.then_inc(sm["v_done"], 1)

                def rel_scores(s, it, par, hp):
                    pe.wait_ge(sm["R_ready"], up(s * HP + hp - 1))
                    if hp == 1:
                        pe.wait_ge(sm["Ta_ready"], up((s - 1) * 4))
                    for n in range(2):
                        ins = nc.tensor.matmul(ps_R[hp % 2][:, n, :], stk[par][:, 0, 2 * hp + n, it * P:(it + 1) * P], rel_st[:, it, :],
                                               start=True, stop=True)
                    ins.then_inc(sm["R_done"], 1)

                def key_scores(s, it, par, hp):
                    pe.wait_ge(sm["S_ready"], up(s * H1 + 2 * (hp - 2) if hp > 2 else s * H1))
                    if hp == 0:
                        pe.wait_ge(sm["Ta_ready"], s * 4)
                    if hp == 1:
                        pe.wait_ge(sm["Tv_ready"], s * 4)
                    for n in range(2):
                        h = 2 * hp + n
                        ins = nc.tensor.matmul(ps_S[hp % 3][:, n, :], stk[par][:, 0, h, it * P:(it + 1) * P],
                                               stk[par][:, 1 + it, h, :], start=True, stop=True)
                    ins.then_inc(sm["S_done"], 1)

                def rel_values(s, b, it, k):
                    pe.wait_ge(sm["X_ready"], up(s * 4 + k - 1))
                    if k == 1:
                        if it == 0:
                            pe.wait_ge(sm["v_ready"], b + 1)
                        else:
                            pe.wait_ge(sm["qk_ready"], b + 3)
                    if k == 0:
                        pe.wait_ge(sm["Ta_ready"], (s + 1) * 4)
                        pe.wait_ge(sm["Tv_ready"], (s + 1) * 4)
                    for n in range(2):
                        ig = 2 * k + n
                        use = [(t, jt) for t, (i2, jt, g2) in enumerate(TABLES) if (i2, g2) == (it, ig)]
                        for q, (t, jt) in enumerate(use):
                            ins = nc.tensor.matmul(ps_X[k % 2][:, n, :, :], tabs[:, t, :], PT[:, jt, :, ig * GI:(ig + 1) * GI],
                                                   start=(q == 0), stop=(q == len(use) - 1))
                    ins.then_inc(sm["X_done"], 1)

                def context(s, b, it, quads):
                    if 0 in quads:
                        pe.wait_ge(sm["rdT_ready"], s + 1)
                        pe.wait_ge(sm["v_ready"], b + 1)
                        pe.wait_ge(sm["X_ready"], (s + 1) * 4)
                    for q in quads:
                        for part in range(3):
                            for g in range(H1 // QUAD):
                                h = g * QUAD + q
                                w, rhs = (fold[:, q, :], X[:, h, :]) if part == 2 else (vx[:, it, part, h, :], PT[:, part, h, :])
                                ins = nc.tensor.matmul(ctx_ps[g * QW:(g + 1) * QW, :], w, rhs,
                                                       start=(q == 0 and part == 0), stop=(q == QUAD - 1 and part == 2))
                    if QUAD - 1 in quads:
                        ins.then_inc(sm["c_done"], 1)

                def reciprocals(s):
                    pe.wait_ge(sm["rrep_ready"], s + 1)
                    pe.wait_ge(sm["y_added"], s)
                    nc.tensor.transpose(rdT_ps, rrep[:, :, :].rearrange("p h d -> p (h d)"), ident[:, :]).then_inc(sm["rdT_done"], 1)

                def project_out(s):
                    pe.wait_ge(sm["cT_ready"], s + 1)
                    nc.tensor.matmul(y_ps, cT[:, :], w_out[:, :], start=True, stop=False)
                    nc.tensor.matmul(y_ps, ones_row[:, :], b_out[:, :], start=False, stop=True).then_inc(sm["y_done"], 1)

                def transposes(s, k):
                    if k == 0:
                        pe.wait_ge(sm["R_ready"], (s + 2) * HP)
                    if 0 < k < 4:
                        pe.wait_ge(sm["S_ready"], s * H1 + 2 * (5 if k == 1 else k + 4) + 2)
                    pe.wait_ge(sm["P_ready"], s * H1 + 2 * k + 2)
                    if k >= 4:
                        pe.wait_ge(sm["Ta_ready" if k % 2 == 0 else "Tv_ready"], s * 4 + k // 2 - 1)
                    for n in range(2):
                        for jt in range(2):
                            ins = nc.tensor.transpose(ps_TT[k % 4][:, n, jt, :], Pm[:, 2 * k + n, jt * P:(jt + 1) * P], ident[:, :])
                    ins.then_inc(sm["T_done"], 1)

                def step(r, i):
                    s = r * 4 + i
                    it, par = tile_of(i)
                    nit, npar = tile_of(i + 1)
                    pit, ppar = tile_of(i + 3)
                    after_first = not isinstance(r, int) or i > 0
                    prev_b = r * 2 + par - (1 if it == 0 else 0)
                    if it == 1:
                        pe.wait_ge(stacked[npar], (r + 1 + (1 if i == 3 else 0)) * STACK)
                    for hp in range(HP):
                        key_scores(s, it, par, hp)
                        rel_scores(s + 1, nit, npar, hp)
                        if after_first and hp == 1:
                            reciprocals(s - 1)
                        if after_first and hp < 4:
                            rel_values(s - 1, prev_b, pit, hp)
                        if it == 1 and hp == 4:
                            project_qk(r * 2 + par + 2)
                        if after_first and hp >= 4:
                            context(s - 1, prev_b, pit, (hp - 4,))
                    for k in range(HP):
                        transposes(s, k)
                        if after_first and k == HP // 2 - 1:
                            project_out(s - 1)
                    if it == 0:
                        project_v(r * 2 + par)

                pe.wait_ge(sm["loaded"], 16 * 4)
                pe.wait_ge(stacked[0], STACK)
                for hp in range(HP):
                    rel_scores(0, 0, 0, hp)
                steps(pe, step)
                last = 2 * B - 1
                for k in range(4):
                    rel_values(last, B - 1, 1, k)
                reciprocals(last)
                context(last, B - 1, 1, range(QUAD))
                project_out(last)

            @block.scalar
            def _(act):
                def keep_R(s, hp):
                    act.wait_ge(sm["R_done"], s * HP + hp + 1)
                    if hp % (HP // 2) == 0:
                        act.wait_ge(skew_out[hp // (HP // 2)], s * 16)
                    nc.scalar.activation(Rt[:, 2 * hp:2 * hp + 2, :], ps_R[hp % 2], ACT.Copy).then_inc(sm["R_ready"], 1)

                def exponentials(s, it, hp):
                    for h in (2 * hp, 2 * hp + 1):
                        act.wait_ge(sm["S_ready"], s * H1 + h + 1)
                        nc.scalar.activation(Pm[:, h, :], Pm[:, h, :], ACT.Exp, bias=nmx[it][:, h:h + 1], scale=-1.0,
                                             accum_out=den[it][:, h:h + 1]).then_inc(sm["P_ready"], 1)

                def keep_rdT(s):
                    act.wait_ge(sm["rdT_done"], s + 1)
                    act.wait_ge(sm["cT_ready"], s)
                    nc.scalar.activation(rdT[:, :], rdT_ps, ACT.Copy).then_inc(sm["rdT_ready"], 1)

                def keep_T(s, k):
                    act.wait_ge(sm["T_done"], s * HP + k + 1)
                    act.wait_ge(sm["c_done"], s)
                    nc.scalar.activation(PT[:, :, 2 * k:2 * k + 2, :].rearrange("p j h i -> p h j i"), ps_TT[k % 4],
                                         ACT.Copy).then_inc(sm["Ta_ready"], 1)

                def step(r, i):
                    s = r * 4 + i
                    it, par = tile_of(i)
                    for hp in range(HP):
                        keep_R(s + 1, hp)
                        exponentials(s, it, hp)
                        if hp == 1 and (not isinstance(r, int) or i > 0):
                            keep_rdT(s - 1)
                        if it == 1 and hp == 4:
                            keep_qk(nc, act, front, ps_p, bias_q, bias_k, r * 2 + par + 2)
                    for k in range(0, HP, 2):
                        keep_T(s, k)

                for hp in range(HP):
                    keep_R(0, hp)
                steps(act, step)
                keep_rdT(2 * B - 1)

            @block.vector
            def _(v):
                def keep_v(n):
                    v.wait_ge(sm["v_done"], n + 1)
                    for tile in range(2):
                        to = vx[:, tile, :, :, :].rearrange("p j (g q) c -> p j g q c", q=QUAD)
                        src = ps_p[:, 0, :].rearrange("p (j g q d) -> p j g q d", j=2, q=QUAD, d=HD)
                        bias = bias_v[:, tile, :, :].rearrange("p (g q) d -> p g q d", q=QUAD)
                        for q in range(QUAD):
                            ins = nc.vector.tensor_tensor(to[:, :, :, q, q * HD:(q + 1) * HD], src[:, :, :, q, :],
                                                          bc(bias[:, :, q, :], 1, 2), ALU.add)
                    ins.then_inc(sm["v_ready"], 1)

                def add_scores(r, i, hp):
                    s = r * 4 + i
                    it, par = tile_of(i)
                    if hp % (HP // 2) == 0:
                        v.wait_ge(skew_in[it][hp // (HP // 2)], (r * 2 + par + 1) * 16)
                    v.wait_ge(sm["S_done"], s * HP + hp + 1)
                    v.wait_ge(sm["T_done"], up((s - 1) * HP + hp + 1))
                    nc.vector.memset(taker[:, hp:hp + 1], 0.0)
                    for h in (2 * hp, 2 * hp + 1):
                        nc.vector.tensor_tensor_reduce(out=Pm[:, h, :], in0=ps_S[hp % 3][:, h % 2, :], in1=Sb[it][:, h, :],
                                                       scale=-1.0, scalar=3.0e38, op0=ALU.add, op1=ALU.min,
                                                       accum_out=nmx[it][:, h:h + 1]).then_inc(sm["S_ready"], 1)

                def pick_diagonal(s, k):
                    v.wait_ge(sm["X_done"], s * 4 + k + 1)
                    v.wait_ge(sm["c_done"], s)
                    out = X[:, :, k * 2 * GI:(k + 1) * 2 * GI].rearrange("p h (n i) -> p n h i", n=2)
                    nc.vector.tensor_tensor(out, ps_X[k % 2], bc(bc(pick[:, :], 1, H1), 1, 2), ALU.mult).then_inc(sm["X_ready"], 1)

                def divide(s):
                    v.wait_ge(sm["c_done"], s + 1)
                    v.wait_ge(sm["rdT_ready"], s + 1)
                    v.wait_ge(sm["y_done"], s)
                    nc.vector.tensor_tensor(cT[:, :], ctx_ps, rdT[:, :], ALU.mult).then_inc(sm["cT_ready"], 1)

                def add_y(s):
                    v.wait_ge(sm["y_done"], s + 1)
                    xs = x_all[:, bass.ds(s, 1), :]
                    nc.vector.tensor_tensor(xs, xs, y_ps.unsqueeze(1), ALU.add).then_inc(sm["y_added"], 1)

                def combine(s):
                    v.wait_ge(sm["rows_in"], (s + 1) * 32)
                    v.wait_ge(sm["y_added"], s + 1)
                    xs = x_all[:, bass.ds(s, 1), :]
                    for k in range(2):
                        if k == 1:
                            v.wait_ge(sm["first_added"], s + 1)
                        nc.vector.scalar_tensor_tensor(out=xs, in0=rows[:, k:k + 1, :], scalar=gates[:, k, bass.ds(s, 1)], in1=xs,
                                                       op0=ALU.mult, op1=ALU.add).then_inc(sm["first_added" if k == 0 else "combined"], 1)

                def invert(s, it):
                    v.wait_ge(sm["P_ready"], (s + 1) * H1)
                    nc.vector.reciprocal(rden[:, :], den[it][:, :]).then_inc(sm["vec_step"], 1)
                    v.wait_ge(sm["vec_step"], s + 1)
                    v.wait_ge(sm["rdT_done"], s)
                    nc.vector.tensor_copy(rrep[:, :, :], bc(rden[:, :], 2, HD)).then_inc(sm["rrep_ready"], 1)

                def keep_T(s, k):
                    v.wait_ge(sm["T_done"], s * HP + k + 1)
                    nc.vector.tensor_copy(PT[:, :, 2 * k:2 * k + 2, :].rearrange("p j h i -> p h j i"),
                                          ps_TT[k % 4]).then_inc(sm["Tv_ready"], 1)

                def step(r, i):
                    s = r * 4 + i
                    it, par = tile_of(i)
                    after_first = not isinstance(r, int) or i > 0
                    for hp in range(HP):
                        add_scores(r, i, hp)
                        if after_first and hp < 4:
                            pick_diagonal(s - 1, hp)
                    if after_first:
                        divide(s - 1)
                    for k in range(1, HP, 2):
                        keep_T(s, k)
                        if after_first and k == HP // 2 + 1:
                            add_y(s - 1)
                            combine(s - 1)
                    if it == 0:
                        keep_v(r * 2 + par)
                    invert(s, it)

                nc.vector.memset(vx[:, :, :, :, :], 0.0)
                nc.vector.memset(Sb[0][:, :, BAND:T], 0.0)
                nc.vector.memset(Sb[1][:, :, 0:T - BAND], 0.0).then_inc(sm["cleared"], 1)
                v.wait_ge(sm["cleared"], 1)
                steps(v, step)
                last = 2 * B - 1
                for k in range(4):
                    pick_diagonal(last, k)
                divide(last)
                add_y(last)
                combine(last)
                v.wait_ge(sm["combined"], 2 * B)

            @block.gpsimd
            def _(pool):
                def copy_x(n):
                    pool.wait_ge(sm["v_done"], n)
                    nc.gpsimd.tensor_copy(xb[:, :], xnT_all[:, bass.ds(n * T, T)]).then_inc(sm["xb_ready"], 1)

                def gather(s):
                    pool.wait_ge(sm["combined"], s)
                    nc.gpsimd.tensor_copy(ids[:, :, :], slot_ids[:, :, bass.ds(s, 1)]).then_inc(sm["ids_ready"], 1)
                    pool.wait_ge(sm["ids_ready"], s + 1)
                    nc.gpsimd.tensor_tensor(pool_taker[:, :], one[:, :], one[:, :], ALU.mult)
                    for k in range(2):
                        nc.gpsimd.indirect_dma_start(
                            out=rows[:, k, :], out_offset=None, in_=a["eo"],
                            in_offset=bass.IndirectOffsetOnAxis(ap=ids[:, k, :], axis=0)).then_inc(sm["rows_in"], 16)

                def step(r, i):
                    it, par = tile_of(i)
                    if it == 0:
                        copy_x(r * 2 + par + 1)
                    else:
                        split_qk(nc.gpsimd, pool, front, one, r * 2 + par + 2, stacked[1 - par], (r + 1 + par) * STACK)
                    gather(r * 4 + i)

                pool.wait_ge(sm["loaded"], 16 * 4)
                pool.wait_ge(sm["cleared"], 1)
                copy_x(0)
                steps(pool, step)

            @block.sync
            def _(sp):
                def skew_tile(s, it, between):
                    for half in range(2):
                        hs = slice(half * HH, (half + 1) * HH)
                        sp.wait_ge(sm["R_ready"], s * HP + (half + 1) * (HP // 2))
                        c0 = 0 if it == 0 else P - 1
                        sp.dma_start(skew[it][:, hs, c0:c0 + BAND], Rt[:, hs, :]).then_inc(skew_out[half], 16)
                        between(half)
                        sp.wait_ge(skew_out[half], (s + 1) * 16)
                        c0 = 0 if it == 0 else T - BAND
                        flat = skew[it].rearrange("i h c -> (i h c)")
                        sp.dma_start(Sb[it][:, hs, c0:c0 + BAND],
                                     bass.AP(flat.tensor, flat.offset + half * HH * PITCH + P - 1,
                                             [[H1 * PITCH - 1, P], [PITCH, HH], [1, BAND]])).then_inc(skew_in[it][half], 16)

                def step(r, i):
                    s = r * 4 + i
                    it, par = tile_of(i)
                    nit, npar = tile_of(i + 1)
                    if it == 0:
                        skew_tile(s + 1, nit, lambda half: stack(sp, front, parts, r * 2 + par + 1, 1 - par) if half == 0 else None)
                    else:
                        skew_tile(s + 1, nit, lambda half: None)
                        send_parts(sp, front, parts, r * 2 + par + 2)

                sp.wait_ge(stacked[0], STACK)
                send_parts(sp, front, parts, 1)
                sp.wait_ge(sm["cleared"], 1)
                skew_tile(0, 0, lambda half: None)
                steps(sp, step)
                sp.wait_ge(stacked[0], (B // 2 + 1) * STACK)
                sp.wait_ge(sm["parts_out"], (B + 2) * 16)
                for half in range(2):
                    sp.wait_ge(skew_in[0][half], (B + 1) * 16)


def store_stage(nc, x_all, out):
    with Pool(nc) as m:
        stored = m.sem("stored")
        with nc.Block() as block:
            @block.sync
            def _(sp):
                sp.dma_start(out.rearrange("b (t p) d -> p (b t) d", p=P), x_all[:, :, :]).then_inc(stored, 16)
                sp.wait_ge(stored, 16)


def program(nc, a):
    with Pool(nc) as m:
        ident = m.sb("ident", [P, P])
        iota_e = m.sb("iota_e", [P, E])
        ltri = m.sb("ltri", [P, P], BF16)
        ones_bf = m.sb("ones_bf", [P, P], BF16)
        group_base = m.sb("group_base", [P, NT])
        one = m.sb("one", [P, 1])
        router = m.sb("router", [P, 2, E])
        x_all = m.sb("x_all", [P, NT, D])
        xnT_all = m.sb("xnT_all", [P, (B + 2) * T])
        gates = m.sb("gates", [P, 2, NT])
        slot_ids = m.sb("slot_ids", [P, 2, NT], U32)
        bias_q = m.sb("bias_q", [P, 1])
        bias_k = m.sb("bias_k", [P, 2])
        bias_v = m.sb("bias_v", [P, 2, H1, HD])
        rel_st = m.sb("rel_st", [KS, 2, BAND], BF16)
        tabs = m.sb("tabs", [P, len(TABLES), P])
        pick = m.sb("pick", [P, GI])
        fold = m.sb("fold", [P, QUAD, QW])
        ones_row = m.sb("ones_row", [1, P])
        front = Attn1Front(m)
        with Pool(nc) as t:
            zeros = t.sb("zeros", [P, SLOTS // P, ZW])
            tin = TableInputs(t)

            def prepare(sp, zeroed):
                clear_dram(sp, zeros, a["slots"], a["skew"], zeroed)
                load_table_inputs(sp, tin, a["L1_attn_rel_emb_k"], a["L1_attn_rel_emb_v"], a["L1_attn_b_qkv"])

            with Pool(nc) as g:
                mask = g.sb("mask", [P, T + P])
                logits = g.sb("logits0", [P, NT, E])
                constants(nc, ident, mask, iota_e, ltri, ones_bf, group_base, one)
                x_dram = a["L0_attn_x"].rearrange("b (t p) d -> p (b t) d", p=P)
                load = [(x_all[:, :, :], x_dram), (router[:, 0, :], a["L0_ffn_router_w"]), (router[:, 1, :], a["L1_ffn_router_w"])]
                norm_stage(nc, x_all, None, xnT_all, ident, router[:, 0, :], logits, "n0", load)
                ffn0_stage(nc, x_all, xnT_all, logits, a["L0_ffn_router_b"], a["L0_ffn_W1"], a["L0_ffn_b1"], a["L0_ffn_W2"],
                           a["L0_ffn_b2"], ident, iota_e)
                attn0_stage(nc, x_all, xnT_all, a["L0_attn_W_q"], a["L0_attn_W_k"], a["L0_attn_W_v"], a["L0_attn_W_o"], mask, one,
                            zeros, prepare)
            with Pool(nc) as g:
                xn_all = g.sb("xn_all", [P, NT, D])
                logits = g.sb("logits1", [P, NT, E])
                send_ids = g.sb("send_ids", [P, 2, NT], U32)
                norm_stage(nc, x_all, xn_all, xnT_all, ident, router[:, 1, :], logits, "n1")
                gate1_stage(nc, logits, iota_e, ltri, ones_bf, gates, slot_ids, send_ids, group_base)
                tables1_stage(nc, a, tin, front, xnT_all, xn_all, send_ids, ident, one,
                              bias_q, bias_k, bias_v, rel_st, tabs, pick, fold, ones_row)
                ffn1_stage(nc, a["L1_ffn_w0_kernel"], a["L1_ffn_w1_kernel"], a["L1_ffn_wo_kernel"], a["slots"], a["eo"],
                           xn_all, send_ids, ident)
        attn1_stage(nc, front, x_all, xnT_all, a, gates, slot_ids, ident, one, bias_q, bias_k, bias_v, rel_st, tabs, pick, fold, ones_row)
        store_stage(nc, x_all, a["out"])


NAMES = ["L0_attn_x", "L0_attn_W_q", "L0_attn_W_k", "L0_attn_W_v", "L0_attn_W_o", "L0_ffn_router_w", "L0_ffn_router_b",
         "L0_ffn_W1", "L0_ffn_b1", "L0_ffn_W2", "L0_ffn_b2", "L1_attn_W_qkv", "L1_attn_b_qkv", "L1_attn_W_out",
         "L1_attn_b_out", "L1_attn_rel_emb_k", "L1_attn_rel_emb_v", "L1_ffn_router_w", "L1_ffn_w0_kernel",
         "L1_ffn_w1_kernel", "L1_ffn_wo_kernel"]


def kernel(**inputs):
    import numpy as np
    import concourse.bacc as bacc
    from concourse.bass_utils import run_bass_kernel_spmd

    nc = bacc.Bacc("TRN2", target_bir_lowering=False, num_devices=1)
    arrays, aps = {}, {}
    for name in NAMES:
        a = np.ascontiguousarray(inputs[name])
        arrays["in_" + name] = a
        aps[name] = nc.dram_tensor("in_" + name, a.shape, mybir.dt.from_np(a.dtype), kind="ExternalInput").ap()
    aps["slots"] = nc.dram_tensor("slots", (SLOTS, D), F32, kind="Internal").ap()
    aps["eo"] = nc.dram_tensor("eo", (SLOTS, D), F32, kind="Internal").ap()
    aps["skew"] = [nc.dram_tensor(f"skew{i}", (P, H1, PITCH), F32, kind="Internal").ap() for i in range(2)]
    aps["parts"] = nc.dram_tensor("parts", (P, PARTS, 3, T), BF16, kind="Internal").ap()
    aps["rv_table"] = nc.dram_tensor("rv_table", (2, TAB, HD), F32, kind="Internal").ap()
    aps["out"] = nc.dram_tensor("out", (B, T, D), F32, kind="ExternalOutput").ap()
    program(nc, aps)
    r = run_bass_kernel_spmd(nc, [arrays], core_ids=[0])
    return r.results[0]["out"]
```
